# Optimizing a Trainium2 kernel written in Bass

```python
import numpy as np
import jax
import jax.numpy as jnp

def _softmax(x, axis=-1):
    return jax.nn.softmax(x, axis=axis)

def _gelu(x):
    return jax.nn.gelu(x, approximate=True)

def _silu(x):
    return jax.nn.silu(x)

def _sigmoid(x):
    return jax.nn.sigmoid(x)

def _layernorm(x, axis=-1, eps=1e-05):
    m = jnp.mean(x, axis=axis, keepdims=True)
    v = jnp.var(x, axis=axis, keepdims=True)
    return (x - m) / jnp.sqrt(v + eps)

def _scatter_add(tgt, idx, src, axis=0):
    return tgt.at[idx].add(src)

def _segment_sum(src, seg, n):
    return jax.ops.segment_sum(src, seg, n)
kernel_name = 'mk_flamingo_gated_d2_seqx_r4_e11094'

def setup_inputs(seed: int=0):
    np.random.seed(seed)
    _w = jnp.asarray

    def _rec_inputs():
        import jax
        import jax.numpy as jnp
        _rk = jax.random.key(seed)
        x = -0.0003929 + 0.9999 * jax.random.normal(jax.random.fold_in(_rk, 1), (16, 256, 256), jnp.float32)
        _lenS = 256 - jax.random.randint(jax.random.fold_in(_rk, 7), (16,), 0, max(1, 256 // 4) + 1, jnp.int32)
        _lenS2 = 256 - jax.random.randint(jax.random.fold_in(_rk, 8), (16,), 0, max(1, 256 // 4) + 1, jnp.int32)
        _ctx_2048P = jax.random.normal(jax.random.fold_in(_rk, 11), (16, 16, 512), jnp.float32)
        _ctx_2048c = jax.random.dirichlet(jax.random.fold_in(_rk, 511), 0.3 * jnp.ones((16,), jnp.float32), (16, 256))
        _ctx_2048t = jnp.einsum('bsk,bkd->bsd', _ctx_2048c, _ctx_2048P)
        _ctx_2048t = _ctx_2048t * jax.lax.rsqrt(jnp.mean(jnp.square(_ctx_2048t)) + 1e-12) * 0.953939
        ctx_2048 = 4.13588e-05 + 0.999923 * (_ctx_2048t + 0.3 * jax.random.normal(jax.random.fold_in(_rk, 611), (16, 256, 512), jnp.float32))
        _validS = jnp.arange(256)[None, :] < _lenS[:, None]
        _validS2 = jnp.arange(256)[None, :] < _lenS2[:, None]
        _causal = jnp.tril(jnp.ones((256, 256), dtype=bool))
        mask_BxS2_if0 = jnp.where(jnp.ones((16, 256), dtype=bool), 4, 0).astype(jnp.int32)
        mask_BxS2_fk1 = jnp.where(jnp.broadcast_to(_validS2[:, :], (16, 256)), 1.0, 0.0).astype(jnp.float32)
        _g = jax.random.normal(jax.random.fold_in(_rk, 9001), (2, 2), jnp.float32)
        _g = jnp.sign(_g) * jnp.maximum(jnp.abs(_g), 1.0) + (_g == 0) * 1.0
        g_xattn = _g[0]
        g_ffn = _g[1]
        return (x, ctx_2048, mask_BxS2_if0, mask_BxS2_fk1, g_xattn, g_ffn)
    x, ctx_2048, mask_BxS2_if0, mask_BxS2_fk1, g_xattn, g_ffn = _rec_inputs()

    def _L0_xattn_setup():
        import jax, jax.numpy as jnp
        import numpy as np
        B, L, P = (4, 1024, 256)
        D_MODEL = 256
        D_GLOBAL = 512
        HEADDIM = 32
        EPSILON = 0.001
        RMS_EPS = 1e-05

        def rmsnorm(x, g, eps=RMS_EPS):
            var = jnp.mean(jnp.square(x), axis=-1, keepdims=True)
            return x * jax.lax.rsqrt(var + eps) * g

        def _hnet_depool(h, h_patch_full, patch_lens):
            h_patch = h_patch_full[..., :D_MODEL]
            bsz, plen = (h_patch.shape[0], h_patch.shape[1])
            seqlen = h.shape[1]
            logp = jnp.full((bsz, plen), -EPSILON, dtype=jnp.float32)
            bidx = jnp.cumsum(patch_lens, axis=1) - 1
            boundary_mask = jnp.zeros((bsz, seqlen), dtype=jnp.int32)
            boundary_mask = boundary_mask.at[jnp.arange(bsz)[:, None], bidx].set(1)
            dt = (-jnp.log(-jnp.expm1(logp))).astype(h_patch.dtype)
            x = h_patch / dt[..., None]
            n_heads = D_MODEL // HEADDIM
            A = -jnp.ones((n_heads,), dtype=jnp.float32)
            bcoef = jnp.exp(logp).astype(h_patch.dtype)
            x4 = x.reshape(bsz, plen, n_heads, HEADDIM)
            a = jnp.exp(dt[:, :, None] * A[None, None, :])
            u = (dt * bcoef)[:, :, None, None] * x4
            a_b = jnp.broadcast_to(a[..., None], u.shape)

            def comb(lft, rgt):
                aL, uL = lft
                aR, uR = rgt
                return (aL * aR, uL * aR + uR)
            _, s = jax.lax.associative_scan(comb, (a_b, u), axis=1)
            depool = s.reshape(bsz, plen, D_MODEL)
            plug = jnp.clip(jnp.cumsum(boundary_mask, axis=1) - 1, 0, plen - 1)
            depool_out = depool[jnp.arange(bsz)[:, None], plug]
            return depool_out + h
        key = jax.random.key(seed)
        k1, k2, k3, k4 = jax.random.split(key, 4)
        embeds = jax.random.normal(k1, (B, L, D_MODEL), dtype=jnp.float32)
        patch_embeds = jax.random.normal(k2, (B, P, D_GLOBAL), dtype=jnp.float32)
        patch_lens = jnp.full((B, P), L // P, dtype=jnp.int64)
        W_in = jax.random.normal(k3, (D_MODEL, D_MODEL), dtype=jnp.float32) * 0.02
        b_in = jnp.zeros((D_MODEL,), dtype=jnp.float32)
        g_res = jnp.ones((D_MODEL,), dtype=jnp.float32)
        g_init = jnp.ones((D_GLOBAL,), dtype=jnp.float32)
        return {'embeds': embeds, 'patch_embeds': patch_embeds, 'patch_lens': patch_lens, 'W_in': W_in, 'b_in': b_in, 'g_res': g_res, 'g_init': g_init}
    _L0_xattn_all = _L0_xattn_setup()
    _L0_xattn_in = {k: v for k, v in _L0_xattn_all.items() if k in ('W_in', 'b_in', 'g_res', 'g_init')}
    del _L0_xattn_all

    def _L0_ffn_setup():
        import jax, jax.numpy as jnp
        import numpy as np
        B, S, DIM = (4, 1024, 256)
        BASE_COUPLING = 0.1
        NUM_CYCLES = 3

        def _gelu(x):
            return jax.nn.gelu(x, approximate=False)

        def _coupling_net(h, w1, b1, w2, b2, w3, b3, w4, b4):
            h = _gelu(h @ w1 + b1)
            h = _gelu(h @ w2 + b2)
            h = _gelu(h @ w3 + b3)
            return jax.nn.sigmoid(h @ w4 + b4)

        def _global_net(h, w1, b1, w2, b2, w3, b3):
            h = _gelu(h @ w1 + b1)
            h = _gelu(h @ w2 + b2)
            return jax.nn.sigmoid(h @ w3 + b3)

        def _twist(x):
            o_r, o_i, p_r, p_i = jnp.split(x, 4, axis=-1)
            return jnp.concatenate([p_r, -p_i, -o_r, o_i], axis=-1)
        key = jax.random.key(seed)
        ks = jax.random.split(key, 9)
        d = DIM

        def w(k, fan_in, fan_out):
            return jax.random.normal(k, (fan_in, fan_out), dtype=jnp.float32) / np.sqrt(fan_in).astype(np.float32)
        inp = {'x': jax.random.normal(ks[0], (B, S, d), dtype=jnp.float32)}
        cn_dims = [(d, d), (d, d // 2), (d // 2, d // 4), (d // 4, 1)]
        for i, (a, b) in enumerate(cn_dims):
            inp[f'cn_w{i + 1}'] = w(ks[1 + i], a, b)
            inp[f'cn_b{i + 1}'] = jnp.zeros((b,), dtype=jnp.float32)
        gc_dims = [(d, d // 2), (d // 2, d // 4), (d // 4, 1)]
        for i, (a, b) in enumerate(gc_dims):
            inp[f'gc_w{i + 1}'] = w(ks[5 + i], a, b)
            inp[f'gc_b{i + 1}'] = jnp.zeros((b,), dtype=jnp.float32)
        inp['adaptive_range'] = jnp.full((1,), 0.2, dtype=jnp.float32)
        return inp
    _L0_ffn_all = _L0_ffn_setup()
    _L0_ffn_in = {k: v for k, v in _L0_ffn_all.items() if k in ('cn_w1', 'cn_b1', 'cn_w2', 'cn_b2', 'cn_w3', 'cn_b3', 'cn_w4', 'cn_b4', 'gc_w1', 'gc_b1', 'gc_w2', 'gc_b2', 'gc_w3', 'gc_b3', 'adaptive_range')}
    del _L0_ffn_all

    def _L1_xattn_setup():
        import jax, jax.numpy as jnp
        import numpy as np
        B, S, T = (32, 128, 128)
        SRC_SIZE, TGT_SIZE, OUT_SIZE, NUM_HEAD = (512, 256, 256, 8)
        HEAD_DIM = OUT_SIZE // NUM_HEAD
        key = jax.random.key(seed)
        ks = jax.random.split(key, 12)
        src = jax.random.normal(ks[0], (B, S, SRC_SIZE), dtype=jnp.float32)
        tgt = jax.random.normal(ks[1], (B, T, TGT_SIZE), dtype=jnp.float32)
        src_mask = (jax.random.uniform(ks[2], (B, S)) > 0.3).astype(jnp.float32)
        src_mask = src_mask.at[:, 0].set(1.0)
        tgt_mask = (jax.random.uniform(ks[3], (B, T)) > 0.3).astype(jnp.float32)
        tgt_mask = tgt_mask.at[:, 0].set(1.0)

        def lin(k, out_f, in_f):
            return jax.random.normal(k, (out_f, in_f), dtype=jnp.float32) / np.sqrt(in_f)
        W_src = lin(ks[4], 2 * OUT_SIZE, SRC_SIZE)
        b_src = jnp.zeros((2 * OUT_SIZE,), jnp.float32)
        W_tgt = lin(ks[5], OUT_SIZE, TGT_SIZE)
        b_tgt = jnp.zeros((OUT_SIZE,), jnp.float32)
        W_out = lin(ks[6], OUT_SIZE, OUT_SIZE + TGT_SIZE)
        b_out = jnp.zeros((OUT_SIZE,), jnp.float32)
        return {'src': src, 'tgt': tgt, 'src_mask': src_mask, 'tgt_mask': tgt_mask, 'W_src': W_src, 'b_src': b_src, 'W_tgt': W_tgt, 'b_tgt': b_tgt, 'W_out': W_out, 'b_out': b_out}
    _L1_xattn_all = _L1_xattn_setup()
    _L1_xattn_in = {k: v for k, v in _L1_xattn_all.items() if k in ('W_src', 'b_src', 'W_tgt', 'b_tgt', 'W_out', 'b_out')}
    del _L1_xattn_all

    def _L1_ffn_setup():
        import jax, jax.numpy as jnp
        import numpy as np
        D_MODEL, D_FF, RANK = (256, 1024, 64)
        B, S = (4, 1024)
        key = jax.random.key(seed)
        ks = jax.random.split(key, 7)
        return {'x': jax.random.normal(ks[0], (B, S, D_MODEL), dtype=jnp.float32), 'U1': jax.random.normal(ks[1], (D_MODEL, RANK), dtype=jnp.float32) * 0.02, 'V1': jax.random.normal(ks[2], (RANK, D_FF), dtype=jnp.float32) * 0.02, 'b1': jnp.zeros((D_FF,), dtype=jnp.float32), 'U2': jax.random.normal(ks[3], (D_FF, RANK), dtype=jnp.float32) * 0.02, 'V2': jax.random.normal(ks[4], (RANK, D_MODEL), dtype=jnp.float32) * 0.02, 'b2': jnp.zeros((D_MODEL,), dtype=jnp.float32)}
    _L1_ffn_all = _L1_ffn_setup()
    _L1_ffn_in = {k: v for k, v in _L1_ffn_all.items() if k in ('U1', 'V1', 'b1', 'U2', 'V2', 'b2')}
    del _L1_ffn_all
    return {'x': x, 'ctx_2048': ctx_2048, 'mask_BxS2_if0': mask_BxS2_if0, 'mask_BxS2_fk1': mask_BxS2_fk1, 'g_xattn': g_xattn, 'g_ffn': g_ffn, 'L0_xattn_W_in': _L0_xattn_in['W_in'], 'L0_xattn_b_in': _L0_xattn_in['b_in'], 'L0_xattn_g_res': _L0_xattn_in['g_res'], 'L0_xattn_g_init': _L0_xattn_in['g_init'], 'L0_ffn_cn_w1': _L0_ffn_in['cn_w1'], 'L0_ffn_cn_b1': _L0_ffn_in['cn_b1'], 'L0_ffn_cn_w2': _L0_ffn_in['cn_w2'], 'L0_ffn_cn_b2': _L0_ffn_in['cn_b2'], 'L0_ffn_cn_w3': _L0_ffn_in['cn_w3'], 'L0_ffn_cn_b3': _L0_ffn_in['cn_b3'], 'L0_ffn_cn_w4': _L0_ffn_in['cn_w4'], 'L0_ffn_cn_b4': _L0_ffn_in['cn_b4'], 'L0_ffn_gc_w1': _L0_ffn_in['gc_w1'], 'L0_ffn_gc_b1': _L0_ffn_in['gc_b1'], 'L0_ffn_gc_w2': _L0_ffn_in['gc_w2'], 'L0_ffn_gc_b2': _L0_ffn_in['gc_b2'], 'L0_ffn_gc_w3': _L0_ffn_in['gc_w3'], 'L0_ffn_gc_b3': _L0_ffn_in['gc_b3'], 'L0_ffn_adaptive_range': _L0_ffn_in['adaptive_range'], 'L1_xattn_W_src': _L1_xattn_in['W_src'], 'L1_xattn_b_src': _L1_xattn_in['b_src'], 'L1_xattn_W_tgt': _L1_xattn_in['W_tgt'], 'L1_xattn_b_tgt': _L1_xattn_in['b_tgt'], 'L1_xattn_W_out': _L1_xattn_in['W_out'], 'L1_xattn_b_out': _L1_xattn_in['b_out'], 'L1_ffn_U1': _L1_ffn_in['U1'], 'L1_ffn_V1': _L1_ffn_in['V1'], 'L1_ffn_b1': _L1_ffn_in['b1'], 'L1_ffn_U2': _L1_ffn_in['U2'], 'L1_ffn_V2': _L1_ffn_in['V2'], 'L1_ffn_b2': _L1_ffn_in['b2']}

def reference(x, ctx_2048, mask_BxS2_if0, mask_BxS2_fk1, g_xattn, g_ffn, L0_xattn_W_in, L0_xattn_b_in, L0_xattn_g_res, L0_xattn_g_init, L0_ffn_cn_w1, L0_ffn_cn_b1, L0_ffn_cn_w2, L0_ffn_cn_b2, L0_ffn_cn_w3, L0_ffn_cn_b3, L0_ffn_cn_w4, L0_ffn_cn_b4, L0_ffn_gc_w1, L0_ffn_gc_b1, L0_ffn_gc_w2, L0_ffn_gc_b2, L0_ffn_gc_w3, L0_ffn_gc_b3, L0_ffn_adaptive_range, L1_xattn_W_src, L1_xattn_b_src, L1_xattn_W_tgt, L1_xattn_b_tgt, L1_xattn_W_out, L1_xattn_b_out, L1_ffn_U1, L1_ffn_V1, L1_ffn_b1, L1_ffn_U2, L1_ffn_V2, L1_ffn_b2):
    import jax
    import jax.numpy as jnp

    def _L0_xattn_ref(embeds, patch_embeds, patch_lens, W_in, b_in, g_res, g_init):
        import jax, jax.numpy as jnp
        import numpy as np
        B, L, P = (4, 1024, 256)
        D_MODEL = 256
        D_GLOBAL = 512
        HEADDIM = 32
        EPSILON = 0.001
        RMS_EPS = 1e-05

        def rmsnorm(x, g, eps=RMS_EPS):
            var = jnp.mean(jnp.square(x), axis=-1, keepdims=True)
            return x * jax.lax.rsqrt(var + eps) * g

        def _hnet_depool(h, h_patch_full, patch_lens):
            h_patch = h_patch_full[..., :D_MODEL]
            bsz, plen = (h_patch.shape[0], h_patch.shape[1])
            seqlen = h.shape[1]
            logp = jnp.full((bsz, plen), -EPSILON, dtype=jnp.float32)
            bidx = jnp.cumsum(patch_lens, axis=1) - 1
            boundary_mask = jnp.zeros((bsz, seqlen), dtype=jnp.int32)
            boundary_mask = boundary_mask.at[jnp.arange(bsz)[:, None], bidx].set(1)
            dt = (-jnp.log(-jnp.expm1(logp))).astype(h_patch.dtype)
            x = h_patch / dt[..., None]
            n_heads = D_MODEL // HEADDIM
            A = -jnp.ones((n_heads,), dtype=jnp.float32)
            bcoef = jnp.exp(logp).astype(h_patch.dtype)
            x4 = x.reshape(bsz, plen, n_heads, HEADDIM)
            a = jnp.exp(dt[:, :, None] * A[None, None, :])
            u = (dt * bcoef)[:, :, None, None] * x4
            a_b = jnp.broadcast_to(a[..., None], u.shape)

            def comb(lft, rgt):
                aL, uL = lft
                aR, uR = rgt
                return (aL * aR, uL * aR + uR)
            _, s = jax.lax.associative_scan(comb, (a_b, u), axis=1)
            depool = s.reshape(bsz, plen, D_MODEL)
            plug = jnp.clip(jnp.cumsum(boundary_mask, axis=1) - 1, 0, plen - 1)
            depool_out = depool[jnp.arange(bsz)[:, None], plug]
            return depool_out + h
        h = rmsnorm(embeds, g_res)
        h = jnp.einsum('bld,ed->ble', h, W_in) + b_in
        h_patch = rmsnorm(patch_embeds, g_init)
        return _hnet_depool(h, h_patch, patch_lens)

    def _L0_ffn_ref(x, cn_w1, cn_b1, cn_w2, cn_b2, cn_w3, cn_b3, cn_w4, cn_b4, gc_w1, gc_b1, gc_w2, gc_b2, gc_w3, gc_b3, adaptive_range):
        import jax, jax.numpy as jnp
        import numpy as np
        B, S, DIM = (4, 1024, 256)
        BASE_COUPLING = 0.1
        NUM_CYCLES = 3

        def _gelu(x):
            return jax.nn.gelu(x, approximate=False)

        def _coupling_net(h, w1, b1, w2, b2, w3, b3, w4, b4):
            h = _gelu(h @ w1 + b1)
            h = _gelu(h @ w2 + b2)
            h = _gelu(h @ w3 + b3)
            return jax.nn.sigmoid(h @ w4 + b4)

        def _global_net(h, w1, b1, w2, b2, w3, b3):
            h = _gelu(h @ w1 + b1)
            h = _gelu(h @ w2 + b2)
            return jax.nn.sigmoid(h @ w3 + b3)

        def _twist(x):
            o_r, o_i, p_r, p_i = jnp.split(x, 4, axis=-1)
            return jnp.concatenate([p_r, -p_i, -o_r, o_i], axis=-1)
        global_context = x.mean(axis=1, keepdims=True)
        gf = _global_net(global_context, gc_w1, gc_b1, gc_w2, gc_b2, gc_w3, gc_b3)
        out = x
        for _ in range(NUM_CYCLES):
            tf = _coupling_net(out, cn_w1, cn_b1, cn_w2, cn_b2, cn_w3, cn_b3, cn_w4, cn_b4)
            combined = 0.7 * gf + 0.3 * tf
            coupling = BASE_COUPLING + adaptive_range * (combined - 0.5) * 2.0
            out = out + coupling * _twist(out)
        return out

    def _L1_xattn_ref(src, tgt, src_mask, tgt_mask, W_src, b_src, W_tgt, b_tgt, W_out, b_out):
        import jax, jax.numpy as jnp
        import numpy as np
        B, S, T = (32, 128, 128)
        SRC_SIZE, TGT_SIZE, OUT_SIZE, NUM_HEAD = (512, 256, 256, 8)
        HEAD_DIM = OUT_SIZE // NUM_HEAD
        b, s, _ = src.shape
        t = tgt.shape[1]
        src_trans = jnp.einsum('bsf,of->bso', src, W_src) + b_src
        tgt_trans = jnp.einsum('btf,of->bto', tgt, W_tgt) + b_tgt
        src_trans = src_trans * src_mask[:, :, None]
        tgt_trans = tgt_trans * tgt_mask[:, :, None]
        src_key, src_val = jnp.split(src_trans, 2, axis=2)
        k = src_key.reshape(b, s, NUM_HEAD, HEAD_DIM)
        v = src_val.reshape(b, s, NUM_HEAD, HEAD_DIM)
        q = tgt_trans.reshape(b, t, NUM_HEAD, HEAD_DIM)
        scores = jnp.einsum('bthd,bshd->bhts', q, k) / np.sqrt(HEAD_DIM)
        scores = jnp.where(src_mask[:, None, None, :] == 0, -jnp.inf, scores)
        attn = jax.nn.softmax(scores, axis=-1)
        tgt_update = jnp.einsum('bhts,bshd->bthd', attn, v).reshape(b, t, OUT_SIZE)
        cat_tgt = jnp.concatenate([tgt, tgt_update], axis=2)
        return jnp.einsum('btf,of->bto', cat_tgt, W_out) + b_out

    def _L1_ffn_ref(x, U1, V1, b1, U2, V2, b2):
        import jax, jax.numpy as jnp
        import numpy as np
        D_MODEL, D_FF, RANK = (256, 1024, 64)
        B, S = (4, 1024)
        P = jnp.einsum('bsd,dr->bsr', x, U1)
        H = jax.nn.gelu(jnp.einsum('bsr,rf->bsf', P, V1) + b1)
        Q = jnp.einsum('bsf,fr->bsr', H, U2)
        return jnp.einsum('bsr,rd->bsd', Q, V2) + b2
    x = x + jnp.tanh(g_xattn[0]) * _L0_xattn_ref(_layernorm(x, axis=-1), ctx_2048, mask_BxS2_if0, L0_xattn_W_in, L0_xattn_b_in, L0_xattn_g_res, L0_xattn_g_init)
    x = x + jnp.tanh(g_ffn[0]) * _L0_ffn_ref(_layernorm(x, axis=-1), L0_ffn_cn_w1, L0_ffn_cn_b1, L0_ffn_cn_w2, L0_ffn_cn_b2, L0_ffn_cn_w3, L0_ffn_cn_b3, L0_ffn_cn_w4, L0_ffn_cn_b4, L0_ffn_gc_w1, L0_ffn_gc_b1, L0_ffn_gc_w2, L0_ffn_gc_b2, L0_ffn_gc_w3, L0_ffn_gc_b3, L0_ffn_adaptive_range)
    x = x + jnp.tanh(g_xattn[1]) * _L1_xattn_ref(ctx_2048, _layernorm(x, axis=-1), mask_BxS2_fk1, mask_BxS2_fk1, L1_xattn_W_src, L1_xattn_b_src, L1_xattn_W_tgt, L1_xattn_b_tgt, L1_xattn_W_out, L1_xattn_b_out)
    x = x + jnp.tanh(g_ffn[1]) * _L1_ffn_ref(_layernorm(x, axis=-1), L1_ffn_U1, L1_ffn_V1, L1_ffn_b1, L1_ffn_U2, L1_ffn_V2, L1_ffn_b2)
    return x

_drawn_inputs = setup_inputs


def setup_inputs(seed=0):
    import zlib

    import numpy as np

    out = dict(_drawn_inputs(seed))
    spreads = {'g_ffn': (-1.0, 0.6),
     'L0_xattn_b_in': (0.0, 0.1),
     'L0_xattn_g_res': (1.0, 0.2),
     'L0_xattn_g_init': (1.0, 0.2),
     'L0_ffn_cn_b1': (0.0, 0.8),
     'L0_ffn_cn_b2': (0.0, 2.0),
     'L0_ffn_cn_b3': (0.0, 2.0),
     'L0_ffn_gc_b1': (0.0, 0.8),
     'L0_ffn_gc_b2': (0.0, 0.8),
     'L1_xattn_b_src': (0.0, 0.1),
     'L1_xattn_b_tgt': (0.0, 0.57),
     'L1_xattn_b_out': (0.0, 0.1),
     'L1_ffn_b1': (0.0, 0.8),
     'L1_ffn_b2': (0.0, 0.8)}
    factors = {'L0_ffn_cn_w1': 3.624,
     'L0_ffn_cn_w2': 3.798,
     'L0_ffn_cn_w3': 2.928,
     'L0_ffn_cn_w4': 3.331,
     'L0_ffn_gc_w1': 4.113,
     'L0_ffn_gc_w2': 3.386,
     'L0_ffn_gc_w3': 3.27,
     'L1_ffn_U1': 8.0,
     'L1_ffn_V1': 8.0,
     'L1_ffn_U2': 8.0,
     'L1_ffn_V2': 8.0}
    for name, (base, spread) in spreads.items():
        noise = np.random.default_rng([zlib.crc32(name.encode()), seed]).standard_normal(out[name].shape)
        drawn = base * np.exp(spread * noise) if base else spread * noise
        out[name] = jnp.asarray(drawn.astype(out[name].dtype))
    for name, factor in factors.items():
        out[name] = (out[name] * factor).astype(out[name].dtype)
    return out
```

```python
import math
from contextlib import ExitStack

import numpy as np
import concourse.bass as bass
from concourse import mybir

F32 = mybir.dt.float32
I32 = mybir.dt.int32
BF16 = mybir.dt.bfloat16
ALU = mybir.AluOpType
ACT = mybir.ActivationFunctionType

P = 128
B, S, D, DC = 16, 256, 256, 512
TILES = B * S // P
TS = S // P
DK = D // P
FK = DC // P
GROUP = 512
GT = GROUP // P
NG = B * S // GROUP
HEADS, HD = 8, 32
QH = 4
F = 1024
RANK = 64
CYCLES = 3
LN_EPS = 1e-5
RMS_EPS = 1e-5
LOGP = -0.001
DT = -math.log(-math.expm1(LOGP))
SCALE = 1.0 / math.sqrt(HD)
MASKED = -1e30


def need(eng, sem, count):
    if isinstance(count, int) and count <= 0:
        return
    eng.wait_ge(sem, count)


def need_alone(eng, sem, count, passed):
    if isinstance(count, int):
        return need(eng, sem, count)
    eng.wait_ge(sem, count)
    eng.sem_inc(passed, 1)


def over_pairs(eng, n, body):
    body(0, 0)
    body(1, 1)
    with eng.Fori(1, n // 2 - 1) as i:
        body(2 * i, 0)
        body(2 * i + 1, 1)
    body(n - 2, 0)
    body(n - 1, 1)


def beyond(b, n):
    return isinstance(b, int) and b >= n


def is_last(b, n):
    return isinstance(b, int) and b == n - 1


def is_first(b):
    return isinstance(b, int) and b == 0


def build(nc, x, ctx_in, lens, mask, g_xattn, g_ffn, w_in, b_in, g_res, g_init,
          cn_w1, cn_b1, cn_w2, cn_b2, cn_w3, cn_b3, cn_w4, cn_b4,
          gc_w1, gc_b1, gc_w2, gc_b2, gc_w3, gc_b3, adaptive_range,
          w_src, b_src, w_tgt, b_tgt, w_out, b_out, u1, v1, b1, u2, v2, b2, out):
    x_dram = x.rearrange("b (k p) d -> b p k d", p=P)
    ctx_dram = ctx_in.rearrange("b (k p) d -> b p k d", p=P)
    out_dram = out.rearrange("(n c) (k p) d -> n p c k d", c=GROUP // S, p=P)

    with ExitStack() as whole:
        def sb(name, shape, dt=F32, stack=whole):
            return stack.enter_context(nc.sbuf_tensor(name, shape, dt))

        def sem(name):
            return whole.enter_context(nc.semaphore(name))

        bank = [whole.enter_context(nc.psum_tensor(f"bank{i}", [P, 512], F32)) for i in range(8)]

        x_sb = sb("x_sb", [P, TILES, D])
        mu = sb("mu", [P, TILES])
        rstd = sb("rstd", [P, TILES])
        ident = sb("ident", [P, P])
        ones_bf = sb("ones_bf", [P, P], BF16)
        ones_row = sb("ones_row", [B, S])
        iota_row = sb("iota_row", [P, S])
        q_col = sb("q_col", [P, TS])
        neg_half = sb("neg_half", [P, 2 * TS])
        sgn = sb("sgn", [P, 1])
        gates = sb("gates", [P, 4])
        gates_raw = sb("gates_raw", [P, 4])
        mask_b = sb("mask_b", [P, B, S])
        mask_col = sb("mask_col", [P, B, TS])
        plug_b = sb("plug_b", [P, B, S])
        winT = sb("winT", [P, DK, D])
        gres_col = sb("gres_col", [P, DK])
        ginit_b = sb("ginit_b", [P, D])
        bin_b = sb("bin_b", [P, D])
        bout_b = sb("bout_b", [P, D])
        b2_b = sb("b2_b", [P, D])
        bv_b = sb("bv_b", [P, D])
        cw1 = sb("cw1", [P, DK, D])
        cw2 = sb("cw2", [P, DK, D // 2])
        cw3 = sb("cw3", [P, D // 4])
        cw4_col = sb("cw4_col", [D // 4, 1])
        cw4 = sb("cw4", [D // 4, P])
        cb1 = sb("cb1", [P, DK])
        cb2 = sb("cb2", [P, 1])
        cb3 = sb("cb3", [D // 4, 1])
        cb4 = sb("cb4", [P, 1])
        gw1 = sb("gw1", [P, DK, D // 2])
        gw2 = sb("gw2", [P, D // 4])
        gw3_col = sb("gw3_col", [D // 4, 1])
        gw3 = sb("gw3", [D // 4, P])
        gb1 = sb("gb1", [P, 1])
        gb2 = sb("gb2", [D // 4, 1])
        gb3 = sb("gb3", [P, 1])
        arange = sb("arange", [P, 1])
        k_tt = sb("k_tt", [P, 1])
        k_gt = sb("k_gt", [P, 1])
        k_one = sb("k_one", [P, 1])
        wsrcT = sb("wsrcT", [P, FK, 2 * D])
        wtgtT = sb("wtgtT", [P, DK, D])
        woutT = sb("woutT", [P, 2 * DK, D])
        bk_col = sb("bk_col", [P, DK])
        bq_col = sb("bq_col", [P, DK])
        u1_sb = sb("u1_sb", [P, DK, 2 * RANK])
        v1_sb = sb("v1_sb", [P, F // P // 2, P])
        b1_col = sb("b1_col", [P, F // P])
        u2_sb = sb("u2_sb", [P, F // P, RANK])
        v2_sb = sb("v2_sb", [P, D])

        n_st = sb("n_st", [P, TS, 6])
        n_mv = [sb(f"n_mv{s}", [P, TS, 2]) for s in range(2)]
        n_tmp = [sb(f"n_tmp{s}", [P, TS]) for s in range(2)]

        with ExitStack() as st:
            lens_i = sb("lens_i", [B, S], I32, st)
            lens_f = sb("lens_f", [B, S], F32, st)
            bound = sb("bound", [B, S], F32, st)
            wrap = sb("wrap", [B, S], F32, st)
            boundT = sb("boundT", [P, TS, B], F32, st)
            hit = [[sb(f"hit{s}{j}", [P, S], BF16, st) for j in range(TS)] for s in range(2)]
            bmask = [sb(f"bmask{s}", [P, S], F32, st) for s in range(2)]
            plug1 = [sb(f"plug1{s}", [P, S], F32, st) for s in range(2)]
            ones_full = sb("ones_full", [P, S], F32, st)
            win_raw = sb("win_raw", [P, DK, D], F32, st)
            wsrc_raw = sb("wsrc_raw", [P, FK, DC], F32, st)
            wtgt_raw = sb("wtgt_raw", [P, DK, D], F32, st)
            wout_raw = sb("wout_raw", [P, DK, 2 * D], F32, st)
            a_ctx = [sb(f"a_ctx{s}", [P, TS, DC], F32, st) for s in range(2)]
            a_junk = [[sb(f"a_junk{s}{k}", [P, DC], F32, st) for k in range(TS)] for s in range(2)]
            a_ssq = [sb(f"a_ssq{s}", [P, TS], F32, st) for s in range(2)]
            a_st = [sb(f"a_st{s}", [P, TS, 6], F32, st) for s in range(2)]
            a_mv = [sb(f"a_mv{s}", [P, TS, 2], F32, st) for s in range(2)]
            a_tmp = [sb(f"a_tmp{s}", [P, 2 * TS], F32, st) for s in range(2)]
            a_scl = [sb(f"a_scl{s}", [P, 2 * TS], F32, st) for s in range(2)]
            a_xs = [sb(f"a_xs{s}", [P, TS, D], F32, st) for s in range(2)]
            a_xsT = [sb(f"a_xsT{s}", [P, DK, S], F32, st) for s in range(2)]
            a_u = [sb(f"a_u{s}", [P, TS, D], F32, st) for s in range(2)]
            a_z = [sb(f"a_z{s}", [P, TS, S], F32, st) for s in range(2)]
            a_e = [sb(f"a_e{s}", [P, TS, S], F32, st) for s in range(2)]
            a_mT = [sb(f"a_mT{s}", [P, TS, S], F32, st) for s in range(2)]
        with ExitStack() as st:
            b_xn = [sb(f"b_xn{g}", [P, GT, D], F32, st) for g in range(4)]
            b_o = [sb(f"b_o{g}", [P, DK, GROUP], F32, st) for g in range(4)]
            b_h1 = [sb(f"b_h1{g}", [P, DK, GROUP], F32, st) for g in range(4)]
            b_h2 = [sb(f"b_h2{g}", [P, GROUP], F32, st) for g in range(4)]
            b_h3 = [sb(f"b_h3{g}", [D // 4, GROUP], F32, st) for g in range(4)]
            b_tt = [sb(f"b_tt{g}", [P, GROUP], F32, st) for g in range(4)]
            b_t0 = sb("b_t0", [P, GROUP], F32, st)
            b_t1 = sb("b_t1", [P, GROUP], F32, st)
            b_sum = sb("b_sum", [P, DK, 8], F32, st)
            b_g1 = sb("b_g1", [P, 8], F32, st)
            b_g2 = sb("b_g2", [D // 4, 8], F32, st)
            b_gt = sb("b_gt", [P, 8], F32, st)
            b_kb = sb("b_kb", [P, 8], F32, st)
            b_st = sb("b_st", [P, GT, 6], F32, st)
            b_mv = [sb(f"b_mv{s}", [P, GT, 2], F32, st) for s in range(2)]
            b_tmp = [sb(f"b_tmp{s}", [P, GT], F32, st) for s in range(2)]
        with ExitStack() as st:
            c_ctx = [sb(f"c_ctx{s}", [P, TS, DC], F32, st) for s in range(2)]
            c_ctxT = [sb(f"c_ctxT{s}", [P, FK, S], F32, st) for s in range(2)]
            c_xn = [sb(f"c_xn{s}", [P, TS, D], F32, st) for s in range(2)]
            c_xnT = [sb(f"c_xnT{s}", [P, DK, S], F32, st) for s in range(2)]
            c_kT = [sb(f"c_kT{s}", [P, DK, S], F32, st) for s in range(2)]
            c_qT = [sb(f"c_qT{s}", [P, DK, S], F32, st) for s in range(2)]
            c_v = [sb(f"c_v{s}", [P, TS, D], F32, st) for s in range(2)]
            c_vb = sb("c_vb", [P, TS, D], F32, st)
            c_upT = [sb(f"c_upT{s}", [P, DK, S], F32, st) for s in range(2)]
            c_neg = [sb(f"c_neg{s}", [P, S], F32, st) for s in range(2)]
            c_s = [sb(f"c_s{h}", [P, TS, QH, S], F32, st) for h in range(2)]
            c_p = [sb(f"c_p{h}", [P, TS, QH, S], F32, st) for h in range(2)]
            c_pT = [sb(f"c_pT{h}", [P, QH, TS * S], F32, st) for h in range(2)]
            c_mx = [sb(f"c_mx{h}", [P, TS, QH], F32, st) for h in range(2)]
            c_nmx = [sb(f"c_nmx{h}", [P, TS, QH], F32, st) for h in range(2)]
            c_sum = [sb(f"c_sum{h}", [P, TS, QH], F32, st) for h in range(2)]
            c_inv = [sb(f"c_inv{h}", [P, TS, QH], F32, st) for h in range(2)]
        with ExitStack() as st:
            d_xn = [sb(f"d_xn{s}", [P, GT, D], F32, st) for s in range(2)]
            d_xnT = [sb(f"d_xnT{s}", [P, DK, GROUP], F32, st) for s in range(2)]
            d_pT = [sb(f"d_pT{s}", [P, GROUP], F32, st) for s in range(2)]
            d_h = [sb(f"d_h{s}", [P, 2, GROUP], F32, st) for s in range(2)]
            d_qT = [sb(f"d_qT{s}", [P, GROUP], F32, st) for s in range(2)]

        s_lens, s_wa, s_wb, s_wc, s_wd = (sem(n) for n in ("lens_in", "weights_a_in", "weights_b_in",
                                                           "weights_c_in", "weights_d_in"))
        s_zero, s_const, s_vconst = sem("ident_zeroed"), sem("pool_consts"), sem("dve_consts")
        s_bchain, s_boundT_ps, s_boundT = sem("bound_chain"), sem("boundT_in_psum"), sem("boundT_copied")
        s_hit, s_cnt, s_plug = sem("hits_ready"), sem("hit_counts_in_psum"), sem("plug_chain")
        s_winT_ps, s_winT = sem("w_inT_in_psum"), sem("w_inT_ready")
        s_wT_ps, s_wT = sem("weightT_in_psum"), sem("weightT_copied")
        s_gate, s_scaled = sem("gates_ready"), sem("weights_scaled")

        s_passed = sem("waits_passed")

        a_x_in = [sem(f"a_x_in{s}") for s in range(2)]
        a_ctx_in = [sem(f"a_ctx_in{s}") for s in range(2)]
        a_bn, a_stat, a_ssqd, a_pre, a_scale = (sem("a_" + n) for n in (
            "bn_stats", "moments_ready", "square_sums_ready", "scale_chain", "scales_ready"))
        a_xs_ok, a_xsT_ps, a_xsT_ok, a_u_ok = (sem("a_" + n) for n in (
            "xs_ready", "xsT_in_psum", "xsT_copied", "u_ready"))
        a_z_ok, a_e_ok, a_mT_ok, a_out_ps, a_xb, a_x1 = (sem("a_" + n) for n in (
            "lag_ready", "decay_ready", "mix_ready", "out_in_psum", "bias_added", "x_updated"))
        a_nbn, a_nstat, a_npre, a_next = (sem("a_" + n) for n in (
            "next_bn", "next_moments", "next_chain", "next_stats_ready"))

        b_xn_ok, b_xT_ps, b_o_ok = sem("b_xn_ready"), sem("b_xnT_in_psum"), sem("b_state_ready")
        b_ps = [sem(f"b_layer{i}_in_psum") for i in range(1, 5)]
        b_ok = [sem(f"b_layer{i}_ready") for i in range(1, 5)]
        b_gps, b_gok, b_kbok = sem("b_global_in_psum"), sem("b_global_ready"), sem("b_offset_ready")
        b_mid, b_upd = sem("b_update_chain"), sem("b_cycle_done")
        b_back, b_x2 = sem("b_result_in_psum"), sem("b_x_updated")
        b_nbn, b_nstat, b_npre, b_next = (sem("b_" + n) for n in (
            "next_bn", "next_moments", "next_chain", "next_stats_ready"))

        c_ctx_in = [sem(f"c_ctx_in{s}") for s in range(2)]
        c_xn_ok, c_ctxT_ps, c_ctxT_ok, c_xnT_ps, c_xnT_ok = (sem("c_" + n) for n in (
            "xn_ready", "ctxT_in_psum", "ctxT_copied", "xnT_in_psum", "xnT_copied"))
        c_k_ps, c_k_ok, c_q_ps, c_q_ok, c_v_ps, c_vraw, c_v_ok = (sem("c_" + n) for n in (
            "kT_in_psum", "kT_ready", "qT_in_psum", "qT_ready", "v_in_psum", "v_biased", "v_ready"))
        c_neg_ok, c_s_ps, c_mx_ok, c_s_ok, c_p_ok, c_inv_ok, c_pn_ok = (sem("c_" + n) for n in (
            "mask_bias_ready", "scores_in_psum", "max_ready", "scores_ready", "probs_ready",
            "inverse_sums_ready", "probs_normalised"))
        c_pT_ps, c_pT_act, c_pT_dve, c_up_ps, c_up_ok, c_out_ps, c_xb, c_x3 = (sem("c_" + n) for n in (
            "probsT_in_psum", "even_probsT_copied", "odd_probsT_copied", "update_in_psum",
            "update_copied", "out_in_psum", "bias_added", "x_updated"))
        c_nbn, c_nstat, c_npre, c_next = (sem("c_" + n) for n in (
            "next_bn", "next_moments", "next_chain", "next_stats_ready"))

        d_xn_ok, d_xT_ps, d_xT_ok, d_p_ps, d_p_ok, d_h_ps, d_h_ok = (sem("d_" + n) for n in (
            "xn_ready", "xnT_in_psum", "xnT_copied", "lowrank_in_psum", "lowrank_copied",
            "hidden_in_psum", "hidden_ready"))
        d_q_ps, d_q_ok, d_y_ps, d_y_ok, d_xb, d_stored = (sem("d_" + n) for n in (
            "second_lowrank_in_psum", "second_lowrank_copied", "out_in_psum", "x_updated",
            "bias_added", "stored"))

        def column(v):
            return v.rearrange("(c p) -> p c", p=P)

        def row_on_all(v):
            return v.partition_broadcast(P)

        loads_a = [
            (win_raw[:], w_in.rearrange("(c p) e -> p c e", p=P)),
            (gres_col[:], column(g_res)), (ginit_b[:], row_on_all(g_init[0:D])),
            (bin_b[:], row_on_all(b_in)), (gates_raw[:, 0:4:2], row_on_all(g_xattn)),
            (gates_raw[:, 1:4:2], row_on_all(g_ffn)), (bout_b[:], row_on_all(b_out)),
            (b2_b[:], row_on_all(b2)), (bv_b[:], row_on_all(b_src[D:2 * D])),
        ]
        loads_c = [
            (wsrc_raw[:], w_src.rearrange("(c p) f -> p c f", p=P)),
            (wtgt_raw[:], w_tgt.rearrange("(c p) f -> p c f", p=P)),
            (wout_raw[:], w_out.rearrange("(c p) f -> p c f", p=P)),
            (bk_col[:], column(b_src[0:D])), (bq_col[:], column(b_tgt)),
            (mask_b[:], mask.partition_broadcast(P)),
            (mask_col[:], mask.rearrange("b (k p) -> p b k", p=P)),
        ]
        loads_b = [
            (cw1[:], cn_w1.rearrange("(c p) e -> p c e", p=P)),
            (cw2[:], cn_w2.rearrange("(c p) e -> p c e", p=P)), (cw3[:], cn_w3),
            (cw4_col[:], cn_w4), (cb1[:], column(cn_b1)), (cb2[:], column(cn_b2)),
            (cb3[:], cn_b3.rearrange("(p c) -> p c", c=1)), (cb4[:], row_on_all(cn_b4)),
            (gw1[:], gc_w1.rearrange("(c p) e -> p c e", p=P)), (gw2[:], gc_w2),
            (gw3_col[:], gc_w3), (gb1[:], column(gc_b1)),
            (gb2[:], gc_b2.rearrange("(p c) -> p c", c=1)), (gb3[:], row_on_all(gc_b3)),
            (arange[:], row_on_all(adaptive_range)),
        ]
        v1_halves = v1.rearrange("r (j e f) -> e r j f", e=2, f=P)
        loads_d = [
            (u1_sb[:, :, 0:RANK], u1.rearrange("(c p) r -> p c r", p=P)),
            (u1_sb[:, :, RANK:2 * RANK], u1.rearrange("(c p) r -> p c r", p=P)),
            (v1_sb[0:RANK], v1_halves[0]), (v1_sb[RANK:2 * RANK], v1_halves[1]),
            (b1_col[:], column(b1)), (u2_sb[:], u2.rearrange("(c p) r -> p c r", p=P)),
            (v2_sb[0:RANK, :], v2), (v2_sb[RANK:2 * RANK, :], v2),
        ]
        weight_turns = ([(wsrc_raw, o, f, wsrcT) for f in range(FK) for o in range(FK)]
                        + [(wtgt_raw, o, f, wtgtT) for f in range(DK) for o in range(DK)]
                        + [(wout_raw, o, f, woutT) for f in range(2 * DK) for o in range(DK)])
        WT_BANKS = len(weight_turns) // 4

        def scores_free(eng, b, hg):
            n = QH // 2 * (2 * b + hg)
            need(eng, c_pT_act, n)
            need(eng, c_pT_dve, n)

        block = whole.enter_context(nc.Block())

        @block.sync
        def _(sp):
            sp.dma_start(lens_i[:], lens).then_inc(s_lens, 16)

            def stream_a(b, s):
                need(sp, a_u_ok, b - 1)
                need(sp, a_ssqd, b - 1)
                sp.dma_start(x_sb[:, bass.ds(TS * b, TS), :], x_dram[b]).then_inc(a_x_in[s], 16)
                sp.dma_start(a_ctx[s][:], ctx_dram[b]).then_inc(a_ctx_in[s], 16)

            over_pairs(sp, B, stream_a)

            need(sp, b_next, 2 * NG)

            def stream_c(b, s):
                need(sp, c_ctxT_ps, 2 * (b - 1))
                sp.dma_start(c_ctx[s][:], ctx_dram[b]).then_inc(c_ctx_in[s], 16)

            over_pairs(sp, B, stream_c)

            def store(n, s):
                need(sp, d_y_ok, 2 * (n + 1))
                sp.dma_start(out_dram[n], x_sb[:, bass.ds(GT * n, GT), :]
                             .rearrange("p (c k) d -> p c k d", k=TS)).then_inc(d_stored, 16)

            over_pairs(sp, NG, store)
            sp.wait_ge(d_stored, 16 * NG)

        @block.gpsimd
        def _(pool):
            nc.gpsimd.memset(ident[:], 0.0).then_inc(s_zero, 1)
            pool.wait_ge(s_zero, 1)
            nc.gpsimd.affine_select(out=ident[:], in_=ident[:], compare_op=ALU.not_equal, fill=1.0,
                                    base=0, pattern=[[-1, P]], channel_multiplier=1).then_inc(s_const, 1)
            nc.gpsimd.iota(iota_row[:], pattern=[[1, S]], base=0, channel_multiplier=0,
                           allow_small_or_imprecise_dtypes=True).then_inc(s_const, 1)
            nc.gpsimd.iota(q_col[:], pattern=[[P, TS]], base=0, channel_multiplier=1,
                           allow_small_or_imprecise_dtypes=True).then_inc(s_const, 1)
            nc.gpsimd.memset(neg_half[:], -0.5).then_inc(s_const, 1)
            pool.wait_ge(s_const, 4)

            def next_stats(b, s, tiles, mv, tmp, nstat, npre, nnext, count):
                need_alone(pool, nstat, count, s_passed)
                nc.gpsimd.tensor_scalar(tmp[:], mv[:, :, 1], LN_EPS, None, ALU.add).then_inc(npre, 1)
                nc.gpsimd.tensor_copy(mu[:, bass.ds(tiles * b, tiles)], mv[:, :, 0]).then_inc(nnext, 1)
                need(pool, npre, count)
                nc.gpsimd.tensor_tensor(rstd[:, bass.ds(tiles * b, tiles)], tmp[:],
                                        neg_half[:, 0:tiles], ALU.pow).then_inc(nnext, 1)

            def scales_a(b, s):
                need(pool, a_stat, b + 1)
                need(pool, a_xs_ok, b - 1)
                need_alone(pool, a_u_ok, b - 1, s_passed)
                nc.gpsimd.tensor_scalar(a_tmp[s][:, 0:TS], a_mv[s][:, :, 1], 1.0 + RMS_EPS,
                                        RMS_EPS * LN_EPS, ALU.mult, ALU.add).then_inc(a_pre, 1)
                need_alone(pool, a_ssqd, b + 1, s_passed)
                nc.gpsimd.tensor_scalar(a_tmp[s][:, TS:2 * TS], a_ssq[s][:], 1.0 / DC, RMS_EPS,
                                        ALU.mult, ALU.add).then_inc(a_pre, 1)
                need(pool, a_pre, 2 * b + 2)
                nc.gpsimd.tensor_tensor(a_scl[s][:], a_tmp[s][:], neg_half[:], ALU.pow).then_inc(a_scale, 1)

            def bias_a(b):
                need(pool, a_xs_ok, b + 1)
                xb = x_sb[:, bass.ds(TS * b, TS), :]
                nc.gpsimd.tensor_tensor(xb, xb, bin_b[:].unsqueeze(1).to_broadcast([P, TS, D]),
                                        ALU.add).then_inc(a_xb, 1)

            pool.wait_ge(s_scaled, 3)
            scales_a(0, 0)
            scales_a(1, 1)
            bias_a(0)

            def body_a(b, s):
                if not beyond(b + 2, B):
                    scales_a(b + 2, s)
                if not is_first(b):
                    next_stats(b - 1, 1 - s, TS, n_mv[1 - s], n_tmp[1 - s], a_nstat, a_npre, a_next, b)
                if not is_last(b, B):
                    bias_a(b + 1)

            over_pairs(pool, B, body_a)
            next_stats(B - 1, 1, TS, n_mv[1], n_tmp[1], a_nstat, a_npre, a_next, B)

            for half in range(2):
                for g in range(4):
                    n = 4 * half + g
                    next_stats(n, g % 2, GT, b_mv[g % 2], b_tmp[g % 2], b_nstat, b_npre, b_next, n + 1)

            def bias_c(b):
                need(pool, c_xn_ok, b + 1)
                xb = x_sb[:, bass.ds(TS * b, TS), :]
                nc.gpsimd.tensor_tensor(xb, xb, bout_b[:].unsqueeze(1).to_broadcast([P, TS, D]),
                                        ALU.add).then_inc(c_xb, 1)

            def body_c(b, s):
                if not is_last(b, B):
                    bias_c(b + 1)
                if not is_first(b):
                    next_stats(b - 1, 1 - s, TS, n_mv[1 - s], n_tmp[1 - s], c_nstat, c_npre, c_next, b)

            bias_c(0)
            over_pairs(pool, B, body_c)
            next_stats(B - 1, 1, TS, n_mv[1], n_tmp[1], c_nstat, c_npre, c_next, B)

            def bias_d(n, s):
                need(pool, d_xn_ok, n + 1)
                xb = x_sb[:, bass.ds(GT * n, GT), :]
                nc.gpsimd.tensor_tensor(xb, xb, b2_b[:].unsqueeze(1).to_broadcast([P, GT, D]),
                                        ALU.add).then_inc(d_xb, 1)

            over_pairs(pool, NG, bias_d)

        @block.scalar
        def _(act):
            for dst, src in loads_a:
                act.dma_start(dst, src, allow_slow_non_contiguous=True).then_inc(s_wa, 16)
            for dst, src in loads_c:
                act.dma_start(dst, src, allow_slow_non_contiguous=True).then_inc(s_wc, 16)
            for dst, src in loads_b:
                act.dma_start(dst, src, allow_slow_non_contiguous=True).then_inc(s_wb, 16)
            for dst, src in loads_d:
                act.dma_start(dst, src, allow_slow_non_contiguous=True).then_inc(s_wd, 16)
            act.wait_ge(s_wa, 16 * len(loads_a))
            nc.scalar.activation(gates[:], gates_raw[:], ACT.Tanh).then_inc(s_gate, 1)

            act.wait_ge(s_winT_ps, 1)
            for c in range(DK):
                op = nc.scalar.activation(winT[:, c, :], bank[6][:, c * D:(c + 1) * D], ACT.Copy,
                                          scale=gres_col[:, c:c + 1])
            op.then_inc(s_winT, 1)
            for t in range(WT_BANKS):
                raw, _, f, turned = weight_turns[4 * t]
                act.wait_ge(s_wT_ps, t + 1)
                rows = 512 // turned.shape[2]
                nc.scalar.copy(turned[:, f:f + rows, :],
                               bank[4 + t % 2][:].rearrange("p (f o) -> p f o", f=rows)).then_inc(s_wT, 1)

            def decays_a(b, s):
                need(act, a_ctx_in[s], 8 * (b - s) + 16)
                need(act, a_scale, b - 1)
                for k in range(TS):
                    op = nc.scalar.activation(a_junk[s][k][:], a_ctx[s][:, k, :], ACT.Square,
                                              accum_out=a_ssq[s][:, k:k + 1])
                op.then_inc(a_ssqd, 1)
                need(act, a_z_ok, b + 1)
                need(act, a_mT_ok, b - 1)
                nc.scalar.activation(a_e[s][:], a_z[s][:], ACT.Exp, scale=-DT).then_inc(a_e_ok, 1)

            def turned_a(b, s):
                need(act, a_xsT_ps, b + 1)
                need(act, a_out_ps, b - 1)
                nc.scalar.copy(a_xsT[s][:].rearrange("p c t -> p (c t)"), bank[s][:]).then_inc(a_xsT_ok, 1)

            def body_a(b, s):
                if not beyond(b + 2, B):
                    decays_a(b + 2, s)
                if not is_last(b, B):
                    turned_a(b + 1, 1 - s)

            decays_a(0, 0)
            decays_a(1, 1)
            turned_a(0, 0)
            over_pairs(act, B, body_a)

            act.wait_ge(a_nstat, B)
            act.wait_ge(s_wb, 16 * len(loads_b))

            def gelus(layer, g, count):
                src = [bank[2 * g], bank[2 * g + 1]]
                act.wait_ge(b_ps[layer - 1], count)
                if layer == 1:
                    for m in range(DK):
                        op = nc.scalar.activation(b_h1[g][:, m, :], src[m][:], ACT.Gelu, bias=cb1[:, m:m + 1])
                elif layer == 2:
                    op = nc.scalar.activation(b_h2[g][:], src[0][:], ACT.Gelu, bias=cb2[:])
                elif layer == 3:
                    op = nc.scalar.activation(b_h3[g][:], src[1][0:D // 4, :], ACT.Gelu, bias=cb3[:])
                else:
                    op = nc.scalar.activation(b_tt[g][:], src[0][:], ACT.Tanh, bias=cb4[:], scale=0.5)
                op.then_inc(b_ok[layer - 1], 1)

            act.wait_ge(s_vconst, 8)
            for half in range(2):
                for g in range(4):
                    act.wait_ge(b_xT_ps, 4 * half + g + 1)
                    for c in range(DK):
                        for q in range(2):
                            op = nc.scalar.activation(
                                b_o[g][:, c, q * S:(q + 1) * S], bank[2 * g + c][:, q * S:(q + 1) * S],
                                ACT.Copy, accum_out=b_sum[:, c, 2 * g + q:2 * g + q + 1])
                    op.then_inc(b_o_ok, 1)
                cyc = CYCLES * half
                for layer in range(1, 5):
                    for g in range(4):
                        gelus(layer, g, 4 * cyc + g + 1)
                        if layer == 1 and g == 3:
                            act.wait_ge(b_gps, 3 * half + 1)
                            nc.scalar.activation(b_g1[:], bank[1][:, 0:8], ACT.Gelu, bias=gb1[:],
                                                 scale=1.0 / S).then_inc(b_gok, 1)
                        if layer == 2 and g == 1:
                            act.wait_ge(b_gps, 3 * half + 2)
                            nc.scalar.activation(b_g2[:], bank[3][0:D // 4, 0:8], ACT.Gelu,
                                                 bias=gb2[:]).then_inc(b_gok, 1)
                        if layer == 2 and g == 3:
                            act.wait_ge(b_gps, 3 * half + 3)
                            nc.scalar.activation(b_gt[:], bank[5][:, 0:8], ACT.Tanh, bias=gb3[:],
                                                 scale=0.5).then_inc(b_gok, 1)
                with act.Fori(1, CYCLES) as c:
                    for layer in range(1, 5):
                        for g in range(4):
                            gelus(layer, g, 4 * (c + cyc) + g + 1)

            act.wait_ge(b_nstat, NG)
            act.wait_ge(s_wc, 16 * len(loads_c))

            def ctxT_c(b, s):
                for h in range(2):
                    need(act, c_ctxT_ps, 2 * b + h + 1)
                    need(act, c_v_ps, b - 1)
                    nc.scalar.copy(c_ctxT[s][:, 2 * h:2 * h + 2, :].rearrange("p c t -> p (c t)"),
                                   bank[4 + h][:]).then_inc(c_ctxT_ok, 1)

            def xnT_c(b, s):
                need(act, c_xnT_ps, b + 1)
                need(act, c_out_ps, b - 1)
                nc.scalar.copy(c_xnT[s][:].rearrange("p c t -> p (c t)"), bank[5][:]).then_inc(c_xnT_ok, 1)

            def exps_c(b, hg, tc):
                n = 2 * b + hg
                need(act, c_s_ok, TS * n + tc + 1)
                need(act, c_pT_ps, QH * (n - 1))
                for j in range(QH):
                    op = nc.scalar.activation(c_p[hg][:, tc, j, :], c_s[hg][:, tc, j, :], ACT.Exp,
                                              bias=c_nmx[hg][:, tc, j:j + 1], scale=SCALE,
                                              accum_out=c_sum[hg][:, tc, j:j + 1])
                op.then_inc(c_p_ok, 1)

            def probsT_c(b, hg):
                n = 2 * b + hg
                for j in range(0, QH, 2):
                    need(act, c_pT_ps, QH * n + j + 1)
                    need(act, c_up_ps, n - 1)
                    nc.scalar.copy(c_pT[hg][:, j, :], bank[j][:]).then_inc(c_pT_act, 1)

            def update_c(b, s, hg):
                need(act, c_up_ps, 2 * b + hg + 1)
                need(act, c_out_ps, b - 1)
                nc.scalar.copy(c_upT[s][:, hg, :], bank[6][:, hg * S:(hg + 1) * S]).then_inc(c_up_ok, 1)

            def body_c(b, s):
                last, first = is_last(b, B), is_first(b)
                exps_c(b, 0, 0)
                exps_c(b, 0, 1)
                if not first:
                    probsT_c(b - 1, 1)
                    update_c(b - 1, 1 - s, 1)
                if not beyond(b + 2, B):
                    ctxT_c(b + 2, s)
                exps_c(b, 1, 0)
                if not last:
                    xnT_c(b + 1, 1 - s)
                exps_c(b, 1, 1)
                probsT_c(b, 0)
                update_c(b, s, 0)

            ctxT_c(0, 0)
            xnT_c(0, 0)
            ctxT_c(1, 1)
            over_pairs(act, B, body_c)
            probsT_c(B - 1, 1)
            update_c(B - 1, 1, 1)

            act.wait_ge(c_nstat, B)
            act.wait_ge(s_wd, 16 * len(loads_d))

            def xnT_d(n, s):
                need(act, d_xT_ps, n + 1)
                need(act, d_p_ps, n - 1)
                for c in range(DK):
                    op = nc.scalar.copy(d_xnT[s][:, c, :], bank[4 + c][:])
                op.then_inc(d_xT_ok, 1)

            def hidden_d(n, j):
                m = 4 * n + j
                need(act, d_h_ps, m + 1)
                need(act, d_q_ps, m - 1)
                for e in range(2):
                    op = nc.scalar.activation(d_h[j % 2][:, e, :], bank[2 * (j % 2) + e][:],
                                              ACT.Gelu_apprx_tanh, bias=b1_col[:, 2 * j + e:2 * j + e + 1])
                op.then_inc(d_h_ok, 1)

            def body_d(n, s):
                hidden_d(n, 0)
                hidden_d(n, 1)
                if not is_last(n, NG):
                    xnT_d(n + 1, 1 - s)
                hidden_d(n, 2)
                hidden_d(n, 3)

            xnT_d(0, 0)
            over_pairs(act, NG, body_d)

        @block.tensor
        def _(pe):
            mm = nc.tensor.matmul
            pe.wait_ge(s_const, 4)
            pe.wait_ge(s_bchain, 4)
            for k in range(TS):
                op = nc.tensor.transpose(bank[0][:, k * B:(k + 1) * B], bound[:, k * P:(k + 1) * P],
                                         ident[0:B, 0:B])
            op.then_inc(s_boundT_ps, 1)

            pe.wait_ge(s_wa, 16 * len(loads_a))
            for c in range(DK):
                for o in range(DK):
                    op = nc.tensor.transpose(bank[6][:, c * D + o * P:c * D + (o + 1) * P],
                                             win_raw[:, o, c * P:(c + 1) * P], ident[:])
            op.then_inc(s_winT_ps, 1)

            def count(b, s):
                need(pe, s_hit, b + 1)
                need(pe, s_plug, 2 * (b - 1) - 1)
                for k in range(TS):
                    op = mm(bank[2 + s][:, 0:S], ones_bf[:], hit[s][k][:], start=k == 0, stop=k == TS - 1)
                op.then_inc(s_cnt, 1)

            over_pairs(pe, B, count)

            pe.wait_ge(s_wc, 16 * len(loads_c))
            for t in range(WT_BANKS):
                need(pe, s_wT, t - 1)
                for q in range(4):
                    raw, o, f, _ = weight_turns[4 * t + q]
                    op = nc.tensor.transpose(bank[4 + t % 2][:, q * P:(q + 1) * P],
                                             raw[:, o, f * P:(f + 1) * P], ident[:])
                op.then_inc(s_wT_ps, 1)

            pe.wait_ge(s_boundT, 1)
            pe.wait_ge(s_winT, 1)

            def turn_a(b, s):
                need(pe, a_xs_ok, b + 1)
                need(pe, a_xsT_ok, b - 1)
                for c in range(DK):
                    for k in range(TS):
                        op = nc.tensor.transpose(bank[s][:, c * S + k * P:c * S + (k + 1) * P],
                                                 a_xs[s][:, k, c * P:(c + 1) * P], ident[:])
                op.then_inc(a_xsT_ps, 1)

            def mix_a(b, s):
                need(pe, a_xsT_ok, b + 1)
                need(pe, a_u_ok, b + 1)
                need(pe, a_mT_ok, b + 1)
                need(pe, a_x1, b - 1)
                for k in range(TS):
                    dst = bank[2 + s][:, k * D:(k + 1) * D]
                    for c in range(DK):
                        mm(dst, a_xsT[s][:, c, k * P:(k + 1) * P], winT[:, c, :], start=c == 0, stop=False)
                    for q in range(TS):
                        op = mm(dst, a_mT[s][:, q, k * P:(k + 1) * P], a_u[s][:, q, :],
                                start=False, stop=q == TS - 1)
                op.then_inc(a_out_ps, 1)

            def body_a(b, s):
                if not is_last(b, B):
                    turn_a(b + 1, 1 - s)
                mix_a(b, s)

            turn_a(0, 0)
            over_pairs(pe, B, body_a)

            pe.wait_ge(a_x1, B)
            pe.wait_ge(s_wb, 16 * len(loads_b))
            pe.wait_ge(s_vconst, 8)

            def layer_b(layer, g, count):
                lo, hi = bank[2 * g], bank[2 * g + 1]
                if layer == 1:
                    for m in range(DK):
                        for c in range(DK):
                            op = mm((lo, hi)[m][:], cw1[:, c, m * P:(m + 1) * P], b_o[g][:, c, :],
                                    start=c == 0, stop=c == DK - 1)
                elif layer == 2:
                    pe.wait_ge(b_ok[0], count)
                    for c in range(DK):
                        op = mm(lo[:], cw2[:, c, :], b_h1[g][:, c, :], start=c == 0, stop=c == DK - 1)
                elif layer == 3:
                    pe.wait_ge(b_ok[1], count)
                    op = mm(hi[0:D // 4, :], cw3[:], b_h2[g][:], start=True, stop=True)
                else:
                    pe.wait_ge(b_ok[2], count)
                    op = mm(lo[:], cw4[:], b_h3[g][:], start=True, stop=True)
                op.then_inc(b_ps[layer - 1], 1)

            def global_b(step):
                if step == 0:
                    for c in range(DK):
                        op = mm(bank[1][:, 0:8], gw1[:, c, :], b_sum[:, c, :], start=c == 0, stop=c == DK - 1)
                elif step == 1:
                    op = mm(bank[3][0:D // 4, 0:8], gw2[:], b_g1[:], start=True, stop=True)
                else:
                    op = mm(bank[5][:, 0:8], gw3[:], b_g2[:], start=True, stop=True)
                op.then_inc(b_gps, 1)

            for half in range(2):
                for g in range(4):
                    pe.wait_ge(b_xn_ok, 4 * half + g + 1)
                    need(pe, b_x2, 4 * (half - 1) + g + 1)
                    for c in range(DK):
                        for k in range(GT):
                            op = nc.tensor.transpose(bank[2 * g + c][:, k * P:(k + 1) * P],
                                                     b_xn[g][:, k, c * P:(c + 1) * P], ident[:])
                    op.then_inc(b_xT_ps, 1)
                cyc = CYCLES * half
                for layer in range(1, 5):
                    for g in range(4):
                        if layer == 1:
                            pe.wait_ge(b_o_ok, 4 * half + g + 1)
                        layer_b(layer, g, 4 * cyc + g + 1)
                        if layer == 1 and g == 3:
                            pe.wait_ge(b_ok[0], 4 * cyc + 1)
                            global_b(0)
                        if layer == 2 and g == 1:
                            pe.wait_ge(b_gok, 3 * half + 1)
                            global_b(1)
                        if layer == 2 and g == 3:
                            pe.wait_ge(b_gok, 3 * half + 2)
                            global_b(2)
                            pe.wait_ge(b_gok, 3 * half + 3)
                with pe.Fori(1, CYCLES) as c:
                    for layer in range(1, 5):
                        for g in range(4):
                            if layer == 1:
                                pe.wait_ge(b_upd, 4 * (c + cyc - 1) + g + 1)
                            layer_b(layer, g, 4 * (c + cyc) + g + 1)
                for g in range(4):
                    pe.wait_ge(b_upd, 4 * (cyc + CYCLES - 1) + g + 1)
                    for k in range(GT):
                        for c in range(DK):
                            op = nc.tensor.transpose(
                                bank[2 * g + k // 2][:, (k % 2) * D + c * P:(k % 2) * D + (c + 1) * P],
                                b_o[g][:, c, k * P:(k + 1) * P], ident[:])
                    op.then_inc(b_back, 1)

            pe.wait_ge(b_x2, NG)

            def ctxT_c(b, s):
                need(pe, c_ctx_in[s], 8 * (b - s) + 16)
                for h in range(2):
                    need(pe, (c_v_ok, c_q_ok)[h], b - h if not isinstance(b, int) or b > 1 else b)
                    for c in range(2):
                        for k in range(TS):
                            f = 2 * h + c
                            op = nc.tensor.transpose(bank[4 + h][:, c * S + k * P:c * S + (k + 1) * P],
                                                     c_ctx[s][:, k, f * P:(f + 1) * P], ident[:])
                    op.then_inc(c_ctxT_ps, 1)

            def k_c(b, s):
                need(pe, c_ctxT_ok, 2 * b + 2)
                for m in range(DK):
                    for f in range(FK):
                        op = mm(bank[4][:, m * S:(m + 1) * S], wsrcT[:, f, m * P:(m + 1) * P],
                                c_ctxT[s][:, f, :], start=f == 0, stop=f == FK - 1)
                op.then_inc(c_k_ps, 1)

            def xnT_c(b, s, ctx_turned):
                need(pe, c_xn_ok, b + 1)
                need(pe, c_ctxT_ok, 2 * ctx_turned)
                for c in range(DK):
                    for k in range(TS):
                        op = nc.tensor.transpose(bank[5][:, c * S + k * P:c * S + (k + 1) * P],
                                                 c_xn[s][:, k, c * P:(c + 1) * P], ident[:])
                op.then_inc(c_xnT_ps, 1)

            def v_c(b, s):
                need(pe, c_k_ok, b + 1)
                for k in range(TS):
                    for f in range(FK):
                        op = mm(bank[4][:, k * D:(k + 1) * D], c_ctxT[s][:, f, k * P:(k + 1) * P],
                                wsrcT[:, f, D:2 * D], start=f == 0, stop=f == FK - 1)
                op.then_inc(c_v_ps, 1)

            def q_c(b, s):
                need(pe, c_xnT_ok, b + 1)
                for m in range(DK):
                    for c in range(DK):
                        op = mm(bank[5][:, m * S:(m + 1) * S], wtgtT[:, c, m * P:(m + 1) * P],
                                c_xnT[s][:, c, :], start=c == 0, stop=c == DK - 1)
                op.then_inc(c_q_ps, 1)

            def scores_c(b, s, hg):
                need(pe, c_q_ok, b + 1)
                need(pe, c_k_ok, b + 1)
                scores_free(pe, b, hg - 1)
                need(pe, c_s_ok, TS * (2 * b + hg))
                for tc in range(TS):
                    for j in range(QH):
                        rows = slice(j * HD, (j + 1) * HD)
                        op = mm(bank[j][:, tc * S:(tc + 1) * S], c_qT[s][rows, hg, tc * P:(tc + 1) * P],
                                c_kT[s][rows, hg, :], start=True, stop=True)
                op.then_inc(c_s_ps, 1)

            def probsT_c(b, hg):
                need(pe, c_pn_ok, 2 * b + hg + 1)
                n = 2 * b + hg + 2
                need(pe, c_s_ok, TS * (min(n, 2 * B) if isinstance(n, int) else n))
                for j in range(QH):
                    for q in range(TS):
                        for tc in range(TS):
                            op = nc.tensor.transpose(
                                bank[j][:, q * S + tc * P:q * S + (tc + 1) * P],
                                c_p[hg][:, tc, j, q * P:(q + 1) * P], ident[:])
                    op.then_inc(c_pT_ps, 1)

            def update_c(b, s, hg):
                scores_free(pe, b, hg + 1)
                need(pe, c_v_ok, b + 1)
                need(pe, c_up_ok, 2 * b + hg)
                for q in range(TS):
                    for j in range(QH):
                        h = QH * hg + j
                        op = mm(bank[6][j * HD:(j + 1) * HD, hg * S:(hg + 1) * S],
                                c_v[s][:, q, h * HD:(h + 1) * HD], c_pT[hg][:, j, q * S:(q + 1) * S],
                                start=q == 0, stop=q == TS - 1)
                op.then_inc(c_up_ps, 1)

            def out_c(b, s):
                need(pe, c_up_ok, 2 * b + 2)
                need(pe, c_x3, b)
                for k in range(TS):
                    for f in range(2 * DK):
                        src = c_xnT[s][:, f, :] if f < DK else c_upT[s][:, f - DK, :]
                        op = mm(bank[7][:, k * D:(k + 1) * D], src[:, k * P:(k + 1) * P], woutT[:, f, :],
                                start=f == 0, stop=f == 2 * DK - 1)
                op.then_inc(c_out_ps, 1)

            def body_c(b, s):
                last, first = is_last(b, B), is_first(b)
                scores_c(b, s, 0)
                if not last:
                    k_c(b + 1, 1 - s)
                if not first:
                    probsT_c(b - 1, 1)
                if not last:
                    v_c(b + 1, 1 - s)
                if not first:
                    update_c(b - 1, 1 - s, 1)
                scores_c(b, s, 1)
                if not beyond(b + 2, B):
                    ctxT_c(b + 2, s)
                if not first:
                    out_c(b - 1, 1 - s)
                if not last:
                    xnT_c(b + 1, 1 - s, B if beyond(b + 3, B) else b + 3)
                probsT_c(b, 0)
                if not last:
                    q_c(b + 1, 1 - s)
                update_c(b, s, 0)

            ctxT_c(0, 0)
            k_c(0, 0)
            xnT_c(0, 0, 1)
            v_c(0, 0)
            q_c(0, 0)
            ctxT_c(1, 1)
            over_pairs(pe, B, body_c)
            probsT_c(B - 1, 1)
            update_c(B - 1, 1, 1)
            out_c(B - 1, 1)

            pe.wait_ge(s_wd, 16 * len(loads_d))
            pe.wait_ge(c_x3, B)

            def xnT_d(n, s):
                need(pe, d_xn_ok, n + 1)
                need(pe, d_p_ok, n)
                for c in range(DK):
                    for k in range(GT):
                        op = nc.tensor.transpose(bank[4 + c][:, k * P:(k + 1) * P],
                                                 d_xn[s][:, k, c * P:(c + 1) * P], ident[:])
                op.then_inc(d_xT_ps, 1)

            def lowrank_d(n, s):
                need(pe, d_xT_ok, n + 1)
                for c in range(DK):
                    op = mm(bank[4][:], u1_sb[:, c, :], d_xnT[s][:, c, :], start=c == 0, stop=c == DK - 1)
                op.then_inc(d_p_ps, 1)

            def hidden_d(n, s, j):
                need(pe, d_p_ok, n + 1)
                need(pe, d_h_ok, 4 * n + j - 1)
                for e in range(2):
                    rows = slice(e * RANK, (e + 1) * RANK)
                    op = mm(bank[2 * (j % 2) + e][:], v1_sb[rows, j, :], d_pT[s][rows, :],
                            start=True, stop=True)
                op.then_inc(d_h_ps, 1)

            def second_d(n, s, j):
                need(pe, d_h_ok, 4 * n + j + 1)
                need(pe, d_q_ok, n)
                for e in range(2):
                    op = mm(bank[6][e * RANK:(e + 1) * RANK, :], u2_sb[:, 2 * j + e, :],
                            d_h[j % 2][:, e, :], start=j == 0, stop=j == 3)
                op.then_inc(d_q_ps, 1)

            def out_d(n, s, half):
                need(pe, d_q_ok, n + 1)
                need(pe, d_y_ok, 2 * n + half)
                for k in range(2):
                    t = 2 * half + k
                    op = mm(bank[7][:, k * D:(k + 1) * D], d_qT[s][:, t * P:(t + 1) * P], v2_sb[:],
                            start=True, stop=True)
                op.then_inc(d_y_ps, 1)

            def body_d(n, s):
                first, last = is_first(n), is_last(n, NG)
                hidden_d(n, s, 0)
                hidden_d(n, s, 1)
                if not last:
                    xnT_d(n + 1, 1 - s)
                if not first:
                    out_d(n - 1, 1 - s, 0)
                second_d(n, s, 0)
                hidden_d(n, s, 2)
                second_d(n, s, 1)
                hidden_d(n, s, 3)
                if not last:
                    lowrank_d(n + 1, 1 - s)
                if not first:
                    out_d(n - 1, 1 - s, 1)
                second_d(n, s, 2)
                second_d(n, s, 3)

            xnT_d(0, 0)
            lowrank_d(0, 0)
            over_pairs(pe, NG, body_d)
            out_d(NG - 1, 1, 0)
            out_d(NG - 1, 1, 1)

        @block.vector
        def _(dve):
            v = nc.vector

            v.memset(ones_row[:], 1.0).then_inc(s_bchain, 1)
            v.memset(ones_full[:], 1.0)
            v.memset(ones_bf[:], 1.0)
            v.memset(sgn[0:P // 2, :], 1.0)
            v.memset(sgn[P // 2:P, :], -1.0).then_inc(s_vconst, 1)
            dve.wait_ge(s_lens, 16)
            v.tensor_copy(lens_f[:], lens_i[:]).then_inc(s_bchain, 1)
            dve.wait_ge(s_bchain, 2)
            v.tensor_tensor_scan(bound[:], ones_row[:], lens_f[:], -1.0, ALU.mult, ALU.add).then_inc(s_bchain, 1)
            dve.wait_ge(s_bchain, 3)
            v.tensor_scalar(wrap[:], bound[:], 0.0, float(S), ALU.is_lt, ALU.mult).then_inc(s_vconst, 1)
            dve.wait_ge(s_vconst, 2)
            v.tensor_tensor(bound[:], bound[:], wrap[:], ALU.add).then_inc(s_bchain, 1)
            dve.wait_ge(s_boundT_ps, 1)
            v.tensor_copy(boundT[:].rearrange("p k b -> p (k b)"), bank[0][:, 0:TS * B]).then_inc(s_boundT, 1)
            dve.wait_ge(s_boundT, 1)
            dve.wait_ge(s_const, 4)

            def hits(b, s):
                need(dve, s_cnt, b - 1)
                for k in range(TS):
                    op = v.tensor_scalar(hit[s][k][:], iota_row[:], boundT[:, k, bass.ds(b, 1)], None,
                                         ALU.is_equal)
                op.then_inc(s_hit, 1)

            def plugs(b, s):
                need(dve, s_cnt, b + 1)
                v.tensor_scalar(bmask[s][:], bank[2 + s][:, 0:S], 1.0, None, ALU.min).then_inc(s_plug, 1)
                need(dve, s_plug, 2 * b + 1)
                v.tensor_tensor_scan(plug1[s][:], ones_full[:], bmask[s][:], 0.0, ALU.mult, ALU.add)\
                    .then_inc(s_plug, 1)
                need(dve, s_plug, 2 * b + 2)
                v.tensor_scalar(plug_b[:, b, :], plug1[s][:], -1.0, 0.0, ALU.add, ALU.max)

            def body_plug(b, s):
                if not is_last(b, B):
                    hits(b + 1, 1 - s)
                plugs(b, s)

            hits(0, 0)
            over_pairs(dve, B, body_plug)

            dve.wait_ge(s_wa, 16 * len(loads_a))
            dve.wait_ge(s_gate, 1)
            v.tensor_scalar(ginit_b[:], ginit_b[:], math.exp(LOGP), None, ALU.mult).then_inc(s_scaled, 1)
            v.tensor_scalar(bin_b[:], bin_b[:], gates[:, 0:1], None, ALU.mult).then_inc(s_scaled, 1)
            v.tensor_scalar(bout_b[:], bout_b[:], gates[:, 2:3], None, ALU.mult)
            v.tensor_scalar(b2_b[:], b2_b[:], gates[:, 3:4], None, ALU.mult).then_inc(s_scaled, 1)
            dve.wait_ge(s_scaled, 3)

            def next_moments(b, s, nbn, nstat, nnext, x_ok):
                need_alone(dve, x_ok, b + 1, s_passed)
                for k in range(TS):
                    op = v.bn_stats(n_st[:, k, :], x_sb[:, bass.ds(TS * b + k, 1), :].rearrange("p o d -> p (o d)"))
                op.then_inc(nbn, 1)
                need(dve, nbn, b + 1)
                need_alone(dve, nnext, 2 * (b - 1), s_passed)
                for k in range(TS):
                    op = v.bn_aggr(n_mv[s][:, k, :], n_st[:, k, :])
                op.then_inc(nstat, 1)

            def moments_a(b, s):
                need_alone(dve, a_x_in[s], 8 * (b - s) + 16, s_passed)
                for k in range(TS):
                    op = v.bn_stats(a_st[s][:, k, :], x_sb[:, bass.ds(TS * b + k, 1), :].rearrange("p o d -> p (o d)"))
                op.then_inc(a_bn, 1)
                need(dve, a_e_ok, b - 1)
                for q in range(TS):
                    op = v.tensor_scalar(a_z[s][:, q, :], plug_b[:, bass.ds(b, 1), :].rearrange("p o t -> p (o t)"),
                                         q_col[:, q:q + 1], -1.0, ALU.subtract, ALU.max)
                op.then_inc(a_z_ok, 1)
                need(dve, a_bn, b + 1)
                need_alone(dve, a_scale, b - 1, s_passed)
                for k in range(TS):
                    op = v.bn_aggr(a_mv[s][:, k, :], a_st[s][:, k, :])
                op.then_inc(a_stat, 1)

            def operands_a(b, s):
                need(dve, a_stat, b + 1)
                need(dve, a_scale, b + 1)
                need(dve, a_xsT_ps, b - 1)
                for k in range(TS):
                    op = v.tensor_scalar(a_xs[s][:, k, :], x_sb[:, bass.ds(TS * b + k, 1), :].rearrange("p o d -> p (o d)"),
                                         a_mv[s][:, k, 0:1], a_scl[s][:, k:k + 1], ALU.subtract, ALU.mult)
                op.then_inc(a_xs_ok, 1)
                need(dve, a_ctx_in[s], 8 * (b - s) + 16)
                need(dve, a_out_ps, b - 1)
                for k in range(TS):
                    op = v.scalar_tensor_tensor(a_u[s][:, k, :], a_ctx[s][:, k, 0:D],
                                                a_scl[s][:, TS + k:TS + k + 1], ginit_b[:], ALU.mult, ALU.mult)
                op.then_inc(a_u_ok, 1)
                need(dve, a_e_ok, b + 1)
                v.scalar_tensor_tensor(a_mT[s][:].rearrange("p q t -> p (q t)"),
                                       a_e[s][:].rearrange("p q t -> p (q t)"), 1.5,
                                       a_e[s][:].rearrange("p q t -> p (q t)"), ALU.is_le, ALU.mult)\
                    .then_inc(a_mT_ok, 1)

            def finish_a(b, s):
                need(dve, a_out_ps, b + 1)
                need(dve, a_xb, b + 1)
                xb = x_sb[:, bass.ds(TS * b, TS), :].rearrange("p k d -> p (k d)")
                v.scalar_tensor_tensor(xb, bank[2 + s][:], gates[:, 0:1], xb, ALU.mult, ALU.add).then_inc(a_x1, 1)
                next_moments(b, s, a_nbn, a_nstat, a_next, a_x1)

            def body_a(b, s):
                if not beyond(b + 2, B):
                    moments_a(b + 2, s)
                if not is_first(b):
                    finish_a(b - 1, 1 - s)
                if not is_last(b, B):
                    operands_a(b + 1, 1 - s)

            moments_a(0, 0)
            moments_a(1, 1)
            operands_a(0, 0)
            over_pairs(dve, B, body_a)
            finish_a(B - 1, 1)

            dve.wait_ge(a_next, 2 * B)
            dve.wait_ge(s_wb, 16 * len(loads_b))
            v.tensor_copy(cw4[:], cw4_col[:].to_broadcast([D // 4, P])).then_inc(s_vconst, 1)
            v.tensor_copy(gw3[:], gw3_col[:].to_broadcast([D // 4, P])).then_inc(s_vconst, 1)
            v.tensor_scalar(cb4[:], cb4[:], 0.5, None, ALU.mult).then_inc(s_vconst, 1)
            v.tensor_scalar(gb3[:], gb3[:], 0.5, None, ALU.mult)
            v.tensor_scalar(k_tt[:], arange[:], sgn[:], 0.3, ALU.mult, ALU.mult).then_inc(s_vconst, 1)
            v.tensor_scalar(k_gt[:], arange[:], sgn[:], 0.7, ALU.mult, ALU.mult).then_inc(s_vconst, 1)
            v.tensor_scalar(k_one[:], sgn[:], 0.1, None, ALU.mult).then_inc(s_vconst, 1)
            dve.wait_ge(s_vconst, 8)

            def cycle_b(n, g):
                dve.wait_ge(b_ok[3], n + 1)
                for q in range(2):
                    tq = b_tt[g][:, q * S:(q + 1) * S]
                    op = v.tensor_scalar(tq, tq, k_tt[:], b_kb[:, 2 * g + q:2 * g + q + 1], ALU.mult, ALU.add)
                op.then_inc(b_mid, 1)
                dve.wait_ge(b_mid, 2 * n + 1)
                need(dve, b_upd, n)
                v.tensor_tensor(b_t0[:], b_tt[g][:], b_o[g][:, 1, :], ALU.mult)
                v.tensor_tensor(b_t1[:], b_tt[g][:], b_o[g][:, 0, :], ALU.mult).then_inc(b_mid, 1)
                dve.wait_ge(b_mid, 2 * n + 2)
                v.tensor_tensor(b_o[g][:, 0, :], b_o[g][:, 0, :], b_t0[:], ALU.add)
                v.tensor_tensor(b_o[g][:, 1, :], b_o[g][:, 1, :], b_t1[:], ALU.subtract).then_inc(b_upd, 1)

            def xn_b(half):
                for g in range(4):
                    n = 4 * half + g
                    need(dve, b_xT_ps, n - 3)
                    for k in range(GT):
                        t = GT * n + k
                        op = v.tensor_scalar(b_xn[g][:, k, :], x_sb[:, t, :], mu[:, t:t + 1], rstd[:, t:t + 1],
                                             ALU.subtract, ALU.mult)
                    op.then_inc(b_xn_ok, 1)

            def moments_b(half):
                for g in range(4):
                    n = 4 * half + g
                    dve.wait_ge(b_x2, n + 1)
                    need(dve, b_nstat, n)
                    for k in range(GT):
                        op = v.bn_stats(b_st[:, k, :], x_sb[:, GT * n + k, :])
                    op.then_inc(b_nbn, 1)
                    dve.wait_ge(b_nbn, n + 1)
                    need(dve, b_next, 2 * (n - 1))
                    for k in range(GT):
                        op = v.bn_aggr(b_mv[g % 2][:, k, :], b_st[:, k, :])
                    op.then_inc(b_nstat, 1)

            xn_b(0)
            for half in range(2):
                cyc = CYCLES * half
                dve.wait_ge(b_gok, 3 * half + 3)
                v.tensor_scalar(b_kb[:], b_gt[:], k_gt[:], k_one[:], ALU.mult, ALU.add).then_inc(b_kbok, 1)
                dve.wait_ge(b_kbok, half + 1)
                for g in range(4):
                    cycle_b(4 * cyc + g, g)
                if half == 0:
                    xn_b(1)
                else:
                    moments_b(0)
                with dve.Fori(1, CYCLES) as c:
                    for g in range(4):
                        cycle_b(4 * (c + cyc) + g, g)
                for g in range(4):
                    n = 4 * half + g
                    dve.wait_ge(b_back, n + 1)
                    for h in range(2):
                        xh = x_sb[:, GT * n + 2 * h:GT * n + 2 * h + 2, :].rearrange("p k d -> p (k d)")
                        op = v.scalar_tensor_tensor(xh, bank[2 * g + h][:], gates[:, 1:2], xh, ALU.mult, ALU.add)
                    op.then_inc(b_x2, 1)
            moments_b(1)

            dve.wait_ge(b_next, 2 * NG)
            dve.wait_ge(s_wc, 16 * len(loads_c))

            def xn_c(b, s):
                need(dve, c_xnT_ps, b - 1)
                for k in range(TS):
                    op = v.tensor_scalar(c_xn[s][:, k, :], x_sb[:, bass.ds(TS * b + k, 1), :].rearrange("p o d -> p (o d)"),
                                         mu[:, bass.ds(TS * b + k, 1)], rstd[:, bass.ds(TS * b + k, 1)],
                                         ALU.subtract, ALU.mult)
                op.then_inc(c_xn_ok, 1)

            def neg_c(b, s):
                v.tensor_scalar(c_neg[s][:], mask_b[:, bass.ds(b, 1), :].rearrange("p o t -> p (o t)"), 0.0, MASKED,
                                ALU.is_equal, ALU.mult).then_inc(c_neg_ok, 1)

            def biased(dst, src_bank, col, b, ps, ok):
                need(dve, ps, b + 1)
                for m in range(DK):
                    op = v.scalar_tensor_tensor(dst[:, m, :], src_bank[:, m * S:(m + 1) * S], col[:, m:m + 1],
                                                mask_b[:, bass.ds(b, 1), :].rearrange("p o t -> p (o t)"),
                                                ALU.add, ALU.mult)
                op.then_inc(ok, 1)

            def v_c(b, s):
                need(dve, c_v_ps, b + 1)
                v.tensor_tensor(c_vb[:], bank[4][:].rearrange("p (k d) -> p k d", k=TS),
                                bv_b[:].unsqueeze(1).to_broadcast([P, TS, D]), ALU.add).then_inc(c_vraw, 1)
                need(dve, c_vraw, b + 1)
                need(dve, c_up_ps, 2 * (b - 1))
                for k in range(TS):
                    op = v.tensor_scalar(c_v[s][:, k, :], c_vb[:, k, :],
                                         mask_col[:, bass.ds(b, 1), k], None, ALU.mult)
                op.then_inc(c_v_ok, 1)

            def maxima_c(b, s, hg):
                n = 2 * b + hg
                need(dve, c_neg_ok, b + 1)
                need(dve, c_p_ok, TS * (n - 1))
                need_alone(dve, c_s_ps, n + 1, s_passed)
                for tc in range(TS):
                    for j in range(QH):
                        op = v.tensor_tensor_reduce(c_s[hg][:, tc, j, :], bank[j][:, tc * S:(tc + 1) * S],
                                                    c_neg[s][:], 1.0, -3.0e38, ALU.add, ALU.max,
                                                    c_mx[hg][:, tc, j:j + 1])
                    op.then_inc(c_mx_ok, 1)
                    need(dve, c_mx_ok, TS * n + tc + 1)
                    v.tensor_scalar(c_nmx[hg][:, tc, :], c_mx[hg][:, tc, :], -SCALE, None, ALU.mult)\
                        .then_inc(c_s_ok, 1)

            def normalise_c(b, hg):
                n = 2 * b + hg
                need(dve, c_p_ok, TS * n + TS)
                v.reciprocal(c_inv[hg][:], c_sum[hg][:]).then_inc(c_inv_ok, 1)
                need(dve, c_inv_ok, n + 1)
                for tc in range(TS):
                    for j in range(QH):
                        pr = c_p[hg][:, tc, j, :]
                        op = v.tensor_scalar(pr, pr, c_inv[hg][:, tc, j:j + 1], None, ALU.mult)
                op.then_inc(c_pn_ok, 1)

            def probsT_c(b, hg):
                n = 2 * b + hg
                for j in range(1, QH, 2):
                    need(dve, c_pT_ps, QH * n + j + 1)
                    need(dve, c_up_ps, n - 1)
                    v.tensor_copy(c_pT[hg][:, j, :], bank[j][:]).then_inc(c_pT_dve, 1)

            def finish_c(b, s):
                need(dve, c_out_ps, b + 1)
                need(dve, c_xb, b + 1)
                xb = x_sb[:, bass.ds(TS * b, TS), :].rearrange("p k d -> p (k d)")
                v.scalar_tensor_tensor(xb, bank[7][:], gates[:, 2:3], xb, ALU.mult, ALU.add).then_inc(c_x3, 1)
                next_moments(b, s, c_nbn, c_nstat, c_next, c_x3)

            def body_c(b, s):
                last, first = is_last(b, B), is_first(b)
                maxima_c(b, s, 0)
                if not last:
                    biased(c_kT[1 - s], bank[4], bk_col, b + 1, c_k_ps, c_k_ok)
                    xn_c(b + 1, 1 - s)
                    neg_c(b + 1, 1 - s)
                if not first:
                    probsT_c(b - 1, 1)
                normalise_c(b, 0)
                if not last:
                    v_c(b + 1, 1 - s)
                maxima_c(b, s, 1)
                if not first:
                    finish_c(b - 1, 1 - s)
                probsT_c(b, 0)
                if not last:
                    biased(c_qT[1 - s], bank[5], bq_col, b + 1, c_q_ps, c_q_ok)
                normalise_c(b, 1)

            xn_c(0, 0)
            neg_c(0, 0)
            biased(c_kT[0], bank[4], bk_col, 0, c_k_ps, c_k_ok)
            v_c(0, 0)
            biased(c_qT[0], bank[5], bq_col, 0, c_q_ps, c_q_ok)
            over_pairs(dve, B, body_c)
            probsT_c(B - 1, 1)
            finish_c(B - 1, 1)

            dve.wait_ge(c_next, 2 * B)

            def xn_d(n, s):
                need(dve, d_xT_ps, n - 1)
                for k in range(GT):
                    t = bass.ds(GT * n + k, 1)
                    op = v.tensor_scalar(d_xn[s][:, k, :], x_sb[:, t, :].rearrange("p o d -> p (o d)"),
                                         mu[:, t], rstd[:, t], ALU.subtract, ALU.mult)
                op.then_inc(d_xn_ok, 1)

            def lowrank_d(n, s):
                need(dve, d_p_ps, n + 1)
                need(dve, d_h_ps, 4 * (n - 1))
                v.tensor_copy(d_pT[s][:], bank[4][:]).then_inc(d_p_ok, 1)

            def second_d(n, s):
                need(dve, d_q_ps, 4 * n + 4)
                need(dve, d_y_ps, 2 * (n - 1))
                v.tensor_copy(d_qT[s][:], bank[6][:]).then_inc(d_q_ok, 1)

            def out_d(n, half):
                need(dve, d_y_ps, 2 * n + half + 1)
                need(dve, d_xb, n + 1)
                xh = x_sb[:, bass.ds(GT * n + 2 * half, 2), :].rearrange("p k d -> p (k d)")
                v.scalar_tensor_tensor(xh, bank[7][:], gates[:, 3:4], xh, ALU.mult, ALU.add).then_inc(d_y_ok, 1)

            def body_d(n, s):
                first, last = is_first(n), is_last(n, NG)
                if not last:
                    xn_d(n + 1, 1 - s)
                if not first:
                    out_d(n - 1, 0)
                if not last:
                    lowrank_d(n + 1, 1 - s)
                if not first:
                    out_d(n - 1, 1)
                second_d(n, s)

            xn_d(0, 0)
            lowrank_d(0, 0)
            over_pairs(dve, NG, body_d)
            out_d(NG - 1, 0)
            out_d(NG - 1, 1)


INPUTS = ["x", "ctx_2048", "mask_BxS2_if0", "mask_BxS2_fk1", "g_xattn", "g_ffn",
          "L0_xattn_W_in", "L0_xattn_b_in", "L0_xattn_g_res", "L0_xattn_g_init",
          "L0_ffn_cn_w1", "L0_ffn_cn_b1", "L0_ffn_cn_w2", "L0_ffn_cn_b2", "L0_ffn_cn_w3", "L0_ffn_cn_b3",
          "L0_ffn_cn_w4", "L0_ffn_cn_b4", "L0_ffn_gc_w1", "L0_ffn_gc_b1", "L0_ffn_gc_w2", "L0_ffn_gc_b2",
          "L0_ffn_gc_w3", "L0_ffn_gc_b3", "L0_ffn_adaptive_range",
          "L1_xattn_W_src", "L1_xattn_b_src", "L1_xattn_W_tgt", "L1_xattn_b_tgt",
          "L1_xattn_W_out", "L1_xattn_b_out",
          "L1_ffn_U1", "L1_ffn_V1", "L1_ffn_b1", "L1_ffn_U2", "L1_ffn_V2", "L1_ffn_b2"]


def kernel(**inputs):
    import concourse.bacc as bacc
    from concourse.bass_utils import run_bass_kernel_spmd

    nc = bacc.Bacc("TRN2", target_bir_lowering=False, num_devices=1)
    arrays, args = {}, []
    for name in INPUTS:
        a = np.ascontiguousarray(inputs[name])
        arrays[f"in_{name}"] = a
        args.append(nc.dram_tensor(f"in_{name}", a.shape, mybir.dt.from_np(a.dtype), kind="ExternalInput").ap())
    args.append(nc.dram_tensor("out_x", (B, S, D), F32, kind="ExternalOutput").ap())
    build(nc, *args)
    r = run_bass_kernel_spmd(nc, [arrays], core_ids=[0])
    return r.results[0]["out_x"]
```

```python
import math
from contextlib import ExitStack

import numpy as np
import concourse.bass as bass
from concourse import mybir

F32 = mybir.dt.float32
F32R = mybir.dt.float32r
I32 = mybir.dt.int32
BF16 = mybir.dt.bfloat16
ALU = mybir.AluOpType
ACT = mybir.ActivationFunctionType

P = 128
B, S, D, DC = 16, 256, 256, 512
TILES = B * S // P
TS = S // P
DK = D // P
FK = DC // P
GROUP = 512
GT = GROUP // P
NG = B * S // GROUP
HEADS, HD = 8, 32
QH = 4
F = 1024
RANK = 64
CYCLES = 3
ITEMS = 4 * CYCLES
LN_EPS = 1e-5
RMS_EPS = 1e-5
LOGP = -0.001
DT = -math.log(-math.expm1(LOGP))
SCALE = 1.0 / math.sqrt(HD)
PARTS = 4
Q_LO, Q_HI, K_HI, K_LO = range(PARTS)
STACK_DMAS = 3 * QH
MASKED = -1e30


def need(eng, sem, count):
    if isinstance(count, int) and count <= 0:
        return
    eng.wait_ge(sem, count)


def need_alone(eng, sem, count, passed):
    if isinstance(count, int):
        return need(eng, sem, count)
    eng.wait_ge(sem, count)
    eng.sem_inc(passed, 1)


def over_pairs(eng, n, body):
    body(0, 0)
    body(1, 1)
    with eng.Fori(1, n // 2 - 1) as i:
        body(2 * i, 0)
        body(2 * i + 1, 1)
    body(n - 2, 0)
    body(n - 1, 1)


def beyond(b, n):
    return isinstance(b, int) and b >= n


def is_last(b, n):
    return isinstance(b, int) and b == n - 1


def is_first(b):
    return isinstance(b, int) and b == 0


def build(nc, x, ctx_in, lens, mask, g_xattn, g_ffn, w_in, b_in, g_res, g_init,
          cn_w1, cn_b1, cn_w2, cn_b2, cn_w3, cn_b3, cn_w4, cn_b4,
          gc_w1, gc_b1, gc_w2, gc_b2, gc_w3, gc_b3, adaptive_range,
          w_src, b_src, w_tgt, b_tgt, w_out, b_out, u1, v1, b1, u2, v2, b2, out):
    x_dram = x.rearrange("b (k p) d -> b p k d", p=P)
    ctx_dram = ctx_in.rearrange("b (k p) d -> b p k d", p=P)
    out_dram = out.rearrange("(n c) (k p) d -> n p c k d", c=GROUP // S, p=P)

    with ExitStack() as whole:
        def sb(name, shape, dt=F32, stack=whole):
            return stack.enter_context(nc.sbuf_tensor(name, shape, dt))

        def sem(name):
            return whole.enter_context(nc.semaphore(name))

        bank = [whole.enter_context(nc.psum_tensor(f"bank{i}", [P, 512], F32)) for i in range(8)]

        x_sb = sb("x_sb", [P, TILES, D])
        mu = sb("mu", [P, TILES])
        rstd = sb("rstd", [P, TILES])
        ident = sb("ident", [P, P])
        ones_bf = sb("ones_bf", [P, P], BF16)
        q1_col = sb("q1_col", [P, TS])
        lag_floor = sb("lag_floor", [P, TS])
        neg_half = sb("neg_half", [P, 2 * TS])
        sgn = sb("sgn", [P, 1])
        gates = sb("gates", [P, 4])
        gates_raw = sb("gates_raw", [P, 4])
        mask_b = sb("mask_b", [P, B, S])
        mask_col = sb("mask_col", [P, B, TS])
        gres_col = sb("gres_col", [P, DK])
        bout_b = sb("bout_b", [P, D])
        b2_b = sb("b2_b", [P, D])
        bv_b = sb("bv_b", [P, D])
        arange = sb("arange", [P, 1])
        k_tt = sb("k_tt", [P, 1])
        k_gt = sb("k_gt", [P, 1])
        k_one = sb("k_one", [P, 1])
        wsrcT = sb("wsrcT", [P, FK, 2 * D])
        wtgtT = sb("wtgtT", [P, DK, D])
        woutT = sb("woutT", [P, 2 * DK, D])
        bk_col = sb("bk_col", [P, DK])
        bq_col = sb("bq_col", [P, DK])
        u1_sb = sb("u1_sb", [P, DK, 2 * RANK])
        v1_sb = sb("v1_sb", [P, F // P, P])
        b1_col = sb("b1_col", [P, F // P])
        u2_sb = sb("u2_sb", [P, F // P, RANK])
        v2_sb = sb("v2_sb", [P, D])

        n_st = sb("n_st", [P, TS, 6])
        n_mv = [sb(f"n_mv{s}", [P, TS, 2]) for s in range(2)]
        n_tmp = [sb(f"n_tmp{s}", [P, TS]) for s in range(2)]

        with ExitStack() as st:
            lens_i = sb("lens_i", [B, S], I32, st)
            ones_row = sb("ones_row", [B, S], F32, st)
            iota_row = sb("iota_row", [P, S], F32, st)
            winT = sb("winT", [P, DK, D], F32, st)
            ginit_b = sb("ginit_b", [P, D], F32, st)
            bin_b = sb("bin_b", [P, D], F32, st)
            lens_f = sb("lens_f", [B, S], F32, st)
            bound = sb("bound", [B, S], F32, st)
            wrap = sb("wrap", [B, S], F32, st)
            boundT = sb("boundT", [P, TS, B], F32, st)
            hit = [[sb(f"hit{s}{j}", [P, S], BF16, st) for j in range(TS)] for s in range(2)]
            bmask = [sb(f"bmask{s}", [P, S], F32, st) for s in range(2)]
            ones_full = sb("ones_full", [P, S], F32, st)
            win_raw = sb("win_raw", [P, DK, D], F32, st)
            a_ctx = [sb(f"a_ctx{s}", [P, TS, DC], F32, st) for s in range(2)]
            a_junk = [[sb(f"a_junk{s}{k}", [P, DC], F32, st) for k in range(TS)] for s in range(2)]
            a_ssq = [sb(f"a_ssq{s}", [P, TS], F32, st) for s in range(2)]
            a_st = [sb(f"a_st{s}", [P, TS, 6], F32, st) for s in range(2)]
            a_mv = [sb(f"a_mv{s}", [P, TS, 2], F32, st) for s in range(2)]
            a_tmp = [sb(f"a_tmp{s}", [P, 2 * TS], F32, st) for s in range(2)]
            a_scl = [sb(f"a_scl{s}", [P, 2 * TS], F32, st) for s in range(2)]
            a_xs = [sb(f"a_xs{s}", [P, TS, D], F32, st) for s in range(2)]
            a_xsT = [sb(f"a_xsT{s}", [P, DK, S], F32, st) for s in range(2)]
            a_u = [sb(f"a_u{s}", [P, TS, D], F32, st) for s in range(2)]
            a_z = [sb(f"a_z{s}", [P, TS, S], F32, st) for s in range(2)]
            a_e = [sb(f"a_e{s}", [P, TS, S], F32, st) for s in range(2)]
            a_mT = [sb(f"a_mT{s}", [P, TS, S], F32, st) for s in range(2)]
            patches_b = sb("patches_b", [P, B, S], F32, st)
            wsrc_raw = sb("wsrc_raw", [P, FK, DC], F32, st)
            wtgt_raw = sb("wtgt_raw", [P, DK, D], F32, st)
            wout_raw = sb("wout_raw", [P, DK, 2 * D], F32, st)
        with ExitStack() as st:
            b_o = [sb(f"b_o{g}", [P, DK, GROUP], F32, st) for g in range(4)]
            b_h1 = [sb(f"b_h1{g}", [P, DK, GROUP], F32, st) for g in range(4)]
            b_h2 = [sb(f"b_h2{g}", [P, GROUP], F32, st) for g in range(4)]
            b_h3 = [sb(f"b_h3{g}", [D // 4, GROUP], F32, st) for g in range(4)]
            b_xn = [sb(f"b_xn{g}", [P, GT, D], F32, st) for g in range(4)]
            b_tt = [sb(f"b_tt{g}", [P, GROUP], F32, st) for g in range(4)]
            b_t0 = [sb(f"b_t0{s}", [P, GROUP], F32, st) for s in range(2)]
            b_t1 = [sb(f"b_t1{s}", [P, GROUP], F32, st) for s in range(2)]
            b_sum = sb("b_sum", [P, DK, 8], F32, st)
            b_g1 = sb("b_g1", [P, 8], F32, st)
            b_g2 = sb("b_g2", [D // 4, 8], F32, st)
            b_gt = sb("b_gt", [P, 8], F32, st)
            b_kb = sb("b_kb", [P, 8], F32, st)
            b_st = [sb(f"b_st{g}", [P, GT, 6], F32, st) for g in range(4)]
            b_mv = [sb(f"b_mv{g}", [P, GT, 2], F32, st) for g in range(4)]
            b_tmp = [sb(f"b_tmp{g}", [P, GT], F32, st) for g in range(4)]
            cw1 = sb("cw1", [P, DK, D], F32, st)
            cw2 = sb("cw2", [P, DK, D // 2], F32, st)
            cw3 = sb("cw3", [P, D // 4], F32, st)
            cw4_col = sb("cw4_col", [D // 4, 1], F32, st)
            cw4 = sb("cw4", [D // 4, P], F32, st)
            cb1 = sb("cb1", [P, DK], F32, st)
            cb2 = sb("cb2", [P, 1], F32, st)
            cb3 = sb("cb3", [D // 4, 1], F32, st)
            cb4 = sb("cb4", [P, 1], F32, st)
            gw1 = sb("gw1", [P, DK, D // 2], F32, st)
            gw2 = sb("gw2", [P, D // 4], F32, st)
            gw3_col = sb("gw3_col", [D // 4, 1], F32, st)
            gw3 = sb("gw3", [D // 4, P], F32, st)
            gb1 = sb("gb1", [P, 1], F32, st)
            gb2 = sb("gb2", [D // 4, 1], F32, st)
            gb3 = sb("gb3", [P, 1], F32, st)
        with ExitStack() as st:
            c_ctx = [sb(f"c_ctx{s}", [P, TS, DC], F32, st) for s in range(2)]
            c_ctxT = [sb(f"c_ctxT{s}", [P, FK, S], F32, st) for s in range(2)]
            c_xn = [sb(f"c_xn{s}", [P, TS, D], F32, st) for s in range(2)]
            c_xnT = [sb(f"c_xnT{s}", [P, DK, S], F32, st) for s in range(2)]
            c_xnTq = sb("c_xnTq", [P, DK, S], F32, st)
            c_kT = sb("c_kT", [P, DK, S], F32, st)
            c_qT = sb("c_qT", [P, DK, S], F32, st)
            c_parts = sb("c_parts", [P, PARTS, DK, S], F32R, st)
            c_stack = [sb(f"c_stack{s}", [3 * HD, 2, QH, DK, S], F32R, st) for s in range(2)]
            c_v = [sb(f"c_v{s}", [P, TS, D], F32, st) for s in range(2)]
            c_upT = [sb(f"c_upT{s}", [P, DK, S], F32, st) for s in range(2)]
            c_neg = [sb(f"c_neg{s}", [P, S], F32, st) for s in range(2)]
            c_s = [sb(f"c_s{h}", [P, TS, QH, S], F32, st) for h in range(2)]
            c_p = [sb(f"c_p{h}", [P, TS, QH, S], F32, st) for h in range(2)]
            c_pT = [sb(f"c_pT{h}", [P, QH, TS * S], F32, st) for h in range(2)]
            c_mx = [sb(f"c_mx{h}", [P, TS, QH], F32, st) for h in range(2)]
            c_nmx = [sb(f"c_nmx{h}", [P, TS, QH], F32, st) for h in range(2)]
            c_sum = [sb(f"c_sum{h}", [P, TS, QH], F32, st) for h in range(2)]
            c_inv = [sb(f"c_inv{h}", [P, TS, QH], F32, st) for h in range(2)]
        with ExitStack() as st:
            d_xn = [sb(f"d_xn{s}", [P, GT, D], F32, st) for s in range(2)]
            d_xnT = [sb(f"d_xnT{s}", [P, DK, GROUP], F32, st) for s in range(2)]
            d_pT = [sb(f"d_pT{s}", [P, GROUP], F32R, st) for s in range(2)]
            v1_hi = sb("v1_hi", [P, F // P, P], F32R, st)
            v1_lo = sb("v1_lo", [P, F // P, P], F32R, st)
            d_h = [sb(f"d_h{s}", [P, 2, GROUP], F32, st) for s in range(2)]
            d_qT = [sb(f"d_qT{s}", [P, GROUP], F32, st) for s in range(2)]

        s_lens, s_wa, s_wb, s_wc, s_wd = (sem(n) for n in ("lens_in", "weights_a_in", "weights_b_in",
                                                           "weights_c_in", "weights_d_in"))
        s_zero, s_const, s_vconst = sem("ident_zeroed"), sem("pool_consts"), sem("dve_consts")
        s_bchain, s_boundT_ps, s_boundT = sem("bound_chain"), sem("boundT_in_psum"), sem("boundT_copied")
        s_hit, s_cnt, s_end, s_patch = (sem("hits_ready"), sem("hit_counts_in_psum"), sem("ends_ready"),
                                        sem("patches_ready"))
        s_winT_ps, s_winT = sem("w_inT_in_psum"), sem("w_inT_ready")
        s_wT_ps, s_wT = sem("weightT_in_psum"), sem("weightT_copied")
        s_gate, s_scaled = sem("gates_ready"), sem("weights_scaled")

        s_passed = sem("waits_passed")

        s_x_in = sem("x_in")
        a_ctx_in = [sem(f"a_ctx_in{s}") for s in range(2)]
        a_bn, a_stat, a_ssqd, a_pre, a_scale = (sem("a_" + n) for n in (
            "bn_stats", "moments_ready", "square_sums_ready", "scale_chain", "scales_ready"))
        a_xs_ok, a_xsT_ps, a_xsT_ok, a_u_ok = (sem("a_" + n) for n in (
            "xs_ready", "xsT_in_psum", "xsT_copied", "u_ready"))
        a_z_ok, a_e_ok, a_mT_ok, a_out_ps, a_xb, a_x1 = (sem("a_" + n) for n in (
            "lag_ready", "decay_ready", "mix_ready", "out_in_psum", "bias_added", "x_updated"))
        a_nbn, a_nstat, a_npre, a_next = (sem("a_" + n) for n in (
            "next_bn", "next_moments", "next_chain", "next_stats_ready"))

        b_xn_ok, b_xT_ps, b_o_ok = sem("b_xn_ready"), sem("b_xnT_in_psum"), sem("b_state_ready")
        b_ps = [sem(f"b_layer{i}_in_psum") for i in range(1, 5)]
        b_ok = [sem(f"b_layer{i}_ready") for i in range(1, 5)]
        b_gps, b_gok, b_kbok = sem("b_global_in_psum"), sem("b_global_ready"), sem("b_offset_ready")
        b_mid, b_upd = sem("b_update_chain"), sem("b_cycle_done")
        b_back, b_x2 = sem("b_result_in_psum"), sem("b_x_updated")
        b_nbn, b_nstat, b_npre, b_next = (sem("b_" + n) for n in (
            "next_bn", "next_moments", "next_chain", "next_stats_ready"))

        c_ctx_in = [sem(f"c_ctx_in{s}") for s in range(2)]
        c_xn_ok, c_ctxT_ps, c_ctxT_ok, c_xnT_ps, c_xnTq_ok, c_xnT_ok = (sem("c_" + n) for n in (
            "xn_ready", "ctxT_in_psum", "ctxT_copied", "xnT_in_psum", "xnTq_copied", "xnT_copied"))
        c_k_ps, c_k_ok, c_q_ps, c_q_ok, c_v_ps, c_vraw, c_v_ok = (sem("c_" + n) for n in (
            "kT_in_psum", "kT_ready", "qT_in_psum", "qT_ready", "v_in_psum", "v_biased", "v_ready"))
        c_k_split, c_qhi_ok, c_qlo_ok, c_stack_in = (sem("c_" + n) for n in (
            "k_parts_ready", "q_high_ready", "q_low_ready", "stacks_in"))
        c_neg_ok, c_s_ps, c_mx_ok, c_s_ok, c_p_ok, c_inv_ok, c_pn_ok = (sem("c_" + n) for n in (
            "mask_bias_ready", "scores_in_psum", "max_ready", "scores_ready", "probs_ready",
            "inverse_sums_ready", "probs_normalised"))
        c_pT_ps, c_pT_act, c_pT_dve, c_up_ps, c_up_ok, c_out_ps, c_xb, c_x3 = (sem("c_" + n) for n in (
            "probsT_in_psum", "even_probsT_copied", "odd_probsT_copied", "update_in_psum",
            "update_copied", "out_in_psum", "bias_added", "x_updated"))
        c_nbn, c_nstat, c_npre, c_next = (sem("c_" + n) for n in (
            "next_bn", "next_moments", "next_chain", "next_stats_ready"))

        s_v1, d_phi = sem("v1_parts_ready"), sem("d_lowrank_high_ready")
        d_xn_ok, d_xT_ps, d_xT_ok, d_p_ps, d_p_ok, d_h_ps, d_h_ok = (sem("d_" + n) for n in (
            "xn_ready", "xnT_in_psum", "xnT_copied", "lowrank_in_psum", "lowrank_copied",
            "hidden_in_psum", "hidden_ready"))
        d_q_ps, d_q_ok, d_y_ps, d_y_ok, d_xb, d_stored = (sem("d_" + n) for n in (
            "second_lowrank_in_psum", "second_lowrank_copied", "out_in_psum", "x_updated",
            "bias_added", "stored"))

        def column(v):
            return v.rearrange("(c p) -> p c", p=P)

        def row_on_all(v):
            return v.partition_broadcast(P)

        loads_a = [
            (win_raw[:], w_in.rearrange("(c p) e -> p c e", p=P)),
            (gres_col[:], column(g_res)), (ginit_b[:], row_on_all(g_init[0:D])),
            (bin_b[:], row_on_all(b_in)), (gates_raw[:, 0:4:2], row_on_all(g_xattn)),
            (gates_raw[:, 1:4:2], row_on_all(g_ffn)), (bout_b[:], row_on_all(b_out)),
            (b2_b[:], row_on_all(b2)), (bv_b[:], row_on_all(b_src[D:2 * D])),
        ]
        loads_c = [
            (wsrc_raw[:], w_src.rearrange("(c p) f -> p c f", p=P)),
            (wtgt_raw[:], w_tgt.rearrange("(c p) f -> p c f", p=P)),
            (wout_raw[:], w_out.rearrange("(c p) f -> p c f", p=P)),
            (bk_col[:], column(b_src[0:D])), (bq_col[:], column(b_tgt)),
            (mask_b[:], mask.partition_broadcast(P)),
            (mask_col[:], mask.rearrange("b (k p) -> p b k", p=P)),
        ]
        loads_b = [
            (cw1[:], cn_w1.rearrange("(c p) e -> p c e", p=P)),
            (cw2[:], cn_w2.rearrange("(c p) e -> p c e", p=P)), (cw3[:], cn_w3),
            (cw4_col[:], cn_w4), (cb1[:], column(cn_b1)), (cb2[:], column(cn_b2)),
            (cb3[:], cn_b3.rearrange("(p c) -> p c", c=1)), (cb4[:], row_on_all(cn_b4)),
            (gw1[:], gc_w1.rearrange("(c p) e -> p c e", p=P)), (gw2[:], gc_w2),
            (gw3_col[:], gc_w3), (gb1[:], column(gc_b1)),
            (gb2[:], gc_b2.rearrange("(p c) -> p c", c=1)), (gb3[:], row_on_all(gc_b3)),
            (arange[:], row_on_all(adaptive_range)),
        ]
        loads_d = [
            (u1_sb[:, :, 0:RANK], u1.rearrange("(c p) r -> p c r", p=P)),
            (u1_sb[:, :, RANK:2 * RANK], u1.rearrange("(c p) r -> p c r", p=P)),
            (v1_sb[0:RANK], v1.rearrange("r (c f) -> r c f", f=P)),
            (v1_sb[RANK:2 * RANK], v1.rearrange("r (c f) -> r c f", f=P)),
            (b1_col[:], column(b1)), (u2_sb[:], u2.rearrange("(c p) r -> p c r", p=P)),
            (v2_sb[0:RANK, :], v2), (v2_sb[RANK:2 * RANK, :], v2),
        ]
        weight_turns = ([(wsrc_raw, o, f, wsrcT) for f in range(FK) for o in range(FK)]
                        + [(wtgt_raw, o, f, wtgtT) for f in range(DK) for o in range(DK)]
                        + [(wout_raw, o, f, woutT) for f in range(2 * DK) for o in range(DK)])
        WT_BANKS = len(weight_turns) // 4

        def scores_free(eng, b, hg):
            n = QH // 2 * (2 * b + hg)
            need(eng, c_pT_act, n)
            need(eng, c_pT_dve, n)

        block = whole.enter_context(nc.Block())

        @block.sync
        def _(sp):
            sp.dma_start(lens_i[:], lens).then_inc(s_lens, 16)
            for dst, src in loads_a:
                sp.dma_start(dst, src, allow_slow_non_contiguous=True).then_inc(s_wa, 16)
            sp.dma_start(a_ctx[0][:], ctx_dram[0]).then_inc(a_ctx_in[0], 16)
            sp.dma_start(a_ctx[1][:], ctx_dram[1]).then_inc(a_ctx_in[1], 16)
            for dst, src in loads_c:
                sp.dma_start(dst, src, allow_slow_non_contiguous=True).then_inc(s_wc, 16)
            for q in range(4):
                sp.dma_start(x_sb[:, q * TILES // 4:(q + 1) * TILES // 4, :].rearrange("p (b k) d -> p b k d", k=TS),
                             x_dram[q * B // 4:(q + 1) * B // 4].rearrange("b p k d -> p b k d")).then_inc(s_x_in, 16)

            for dst, src in loads_d:
                sp.dma_start(dst, src, allow_slow_non_contiguous=True).then_inc(s_wd, 16)
            sp.wait_ge(s_wT, WT_BANKS)
            for dst, src in loads_b:
                sp.dma_start(dst, src, allow_slow_non_contiguous=True).then_inc(s_wb, 16)

            def stream_a(b, s):
                if isinstance(b, int) and b < 2:
                    return
                need(sp, a_u_ok, b - 1)
                need(sp, a_ssqd, b - 1)
                sp.dma_start(a_ctx[s][:], ctx_dram[b]).then_inc(a_ctx_in[s], 16)

            over_pairs(sp, B, stream_a)

            need(sp, b_nstat, NG)

            def stream_c(b, s):
                need(sp, c_ctxT_ps, 2 * (b - 1))
                sp.dma_start(c_ctx[s][:], ctx_dram[b]).then_inc(c_ctx_in[s], 16)

            def stack_c(b, s):
                need_alone(sp, c_k_split, 2 * b + 2, s_passed)
                need_alone(sp, c_qlo_ok, b + 1, s_passed)
                need_alone(sp, c_s_ps, 2 * (b - 1), s_passed)
                for c, (first, step) in enumerate(((Q_HI, K_HI - Q_HI), (Q_LO, K_HI - Q_LO), (Q_HI, K_LO - Q_HI))):
                    for j in range(QH):
                        sp.dma_start(
                            c_stack[s][c * HD:(c + 1) * HD, :, j, :, :].rearrange("p a g t -> p a (g t)").bitcast(F32),
                            c_parts[j * HD:(j + 1) * HD, first:first + step + 1:step, :, :]
                            .rearrange("p a g t -> p a (g t)").bitcast(F32)).then_inc(c_stack_in, 16)

            def body_stack(b, s):
                stack_c(b, s)
                if not beyond(b + 2, B):
                    stream_c(b + 2, s)

            stream_c(0, 0)
            stream_c(1, 1)
            over_pairs(sp, B, body_stack)

            def store(n, s):
                need(sp, d_y_ok, 2 * (n + 1))
                sp.dma_start(out_dram[n], x_sb[:, bass.ds(GT * n, GT), :]
                             .rearrange("p (c k) d -> p c k d", k=TS)).then_inc(d_stored, 16)

            over_pairs(sp, NG, store)
            sp.wait_ge(d_stored, 16 * NG)

        @block.gpsimd
        def _(pool):
            nc.gpsimd.memset(ident[:], 0.0).then_inc(s_zero, 1)
            pool.wait_ge(s_zero, 1)
            nc.gpsimd.affine_select(out=ident[:], in_=ident[:], compare_op=ALU.not_equal, fill=1.0,
                                    base=0, pattern=[[-1, P]], channel_multiplier=1).then_inc(s_const, 1)
            nc.gpsimd.iota(iota_row[:], pattern=[[1, S]], base=0, channel_multiplier=0,
                           allow_small_or_imprecise_dtypes=True).then_inc(s_const, 1)
            nc.gpsimd.iota(q1_col[:], pattern=[[P, TS]], base=1, channel_multiplier=1,
                           allow_small_or_imprecise_dtypes=True).then_inc(s_const, 1)
            nc.gpsimd.memset(lag_floor[:], -1.0).then_inc(s_zero, 1)
            pool.wait_ge(s_zero, 2)
            nc.gpsimd.memset(lag_floor[0:1, 0:1], 0.0).then_inc(s_const, 1)
            nc.gpsimd.memset(neg_half[:], -0.5).then_inc(s_const, 1)
            pool.wait_ge(s_const, 5)

            def next_stats(b, s, tiles, mv, tmp, nstat, npre, nnext, count):
                need_alone(pool, nstat, count, s_passed)
                nc.gpsimd.tensor_scalar(tmp[:], mv[:, :, 1], LN_EPS, None, ALU.add).then_inc(npre, 1)
                nc.gpsimd.tensor_copy(mu[:, bass.ds(tiles * b, tiles)], mv[:, :, 0]).then_inc(nnext, 1)
                need(pool, npre, count)
                nc.gpsimd.tensor_tensor(rstd[:, bass.ds(tiles * b, tiles)], tmp[:],
                                        neg_half[:, 0:tiles], ALU.pow).then_inc(nnext, 1)

            def scales_a(b, s):
                need(pool, a_stat, b + 1)
                need(pool, a_xs_ok, b - 1)
                need_alone(pool, a_u_ok, b - 1, s_passed)
                nc.gpsimd.tensor_scalar(a_tmp[s][:, 0:TS], a_mv[s][:, :, 1], 1.0 + RMS_EPS,
                                        RMS_EPS * LN_EPS, ALU.mult, ALU.add).then_inc(a_pre, 1)
                need_alone(pool, a_ssqd, b + 1, s_passed)
                nc.gpsimd.tensor_scalar(a_tmp[s][:, TS:2 * TS], a_ssq[s][:], 1.0 / DC, RMS_EPS,
                                        ALU.mult, ALU.add).then_inc(a_pre, 1)
                need(pool, a_pre, 2 * b + 2)
                nc.gpsimd.tensor_tensor(a_scl[s][:], a_tmp[s][:], neg_half[:], ALU.pow).then_inc(a_scale, 1)

            def bias_a(b):
                need(pool, a_xs_ok, b + 1)
                xb = x_sb[:, bass.ds(TS * b, TS), :]
                nc.gpsimd.tensor_tensor(xb, xb, bin_b[:].unsqueeze(1).to_broadcast([P, TS, D]),
                                        ALU.add).then_inc(a_xb, 1)

            pool.wait_ge(s_scaled, 3)
            scales_a(0, 0)
            scales_a(1, 1)
            bias_a(0)

            def body_a(b, s):
                if not beyond(b + 2, B):
                    scales_a(b + 2, s)
                if not is_first(b):
                    next_stats(b - 1, 1 - s, TS, n_mv[1 - s], n_tmp[1 - s], a_nstat, a_npre, a_next, b)
                if not is_last(b, B):
                    bias_a(b + 1)

            over_pairs(pool, B, body_a)
            next_stats(B - 1, 1, TS, n_mv[1], n_tmp[1], a_nstat, a_npre, a_next, B)

            pool.sem_inc(b_next, 2 * 4)
            with pool.Fori(0, 2) as half:
                for g in range(4):
                    next_stats(4 * half + g, g, GT, b_mv[g], b_tmp[g], b_nstat, b_npre, b_next, 4 * half + g + 1)

            def bias_c(b):
                need(pool, c_xn_ok, b + 1)
                xb = x_sb[:, bass.ds(TS * b, TS), :]
                nc.gpsimd.tensor_tensor(xb, xb, bout_b[:].unsqueeze(1).to_broadcast([P, TS, D]),
                                        ALU.add).then_inc(c_xb, 1)

            def split_k(b):
                need_alone(pool, c_k_ok, b + 1, s_passed)
                need_alone(pool, c_stack_in, 16 * STACK_DMAS * b, s_passed)
                nc.gpsimd.tensor_copy(c_parts[:, K_HI, :, :], c_kT[:]).then_inc(c_k_split, 1)
                need(pool, c_k_split, 2 * b + 1)
                nc.gpsimd.tensor_tensor(c_parts[:, K_LO, :, :], c_kT[:], c_parts[:, K_HI, :, :].bitcast(F32),
                                        ALU.subtract).then_inc(c_k_split, 1)

            def split_q(b):
                need(pool, c_qhi_ok, b + 1)
                nc.gpsimd.tensor_tensor(c_parts[:, Q_LO, :, :], c_qT[:], c_parts[:, Q_HI, :, :].bitcast(F32),
                                        ALU.subtract).then_inc(c_qlo_ok, 1)

            def body_c(b, s):
                if not is_last(b, B):
                    split_k(b + 1)
                    split_q(b + 1)
                    bias_c(b + 1)
                if not is_first(b):
                    next_stats(b - 1, 1 - s, TS, n_mv[1 - s], n_tmp[1 - s], c_nstat, c_npre, c_next, b)

            split_k(0)
            bias_c(0)
            split_q(0)
            over_pairs(pool, B, body_c)
            next_stats(B - 1, 1, TS, n_mv[1], n_tmp[1], c_nstat, c_npre, c_next, B)

            def bias_d(n, s):
                need(pool, d_xn_ok, n + 1)
                xb = x_sb[:, bass.ds(GT * n, GT), :]
                nc.gpsimd.tensor_tensor(xb, xb, b2_b[:].unsqueeze(1).to_broadcast([P, GT, D]),
                                        ALU.add).then_inc(d_xb, 1)

            over_pairs(pool, NG, bias_d)

        @block.scalar
        def _(act):
            def ends(b, s):
                need(act, s_cnt, b + 1)
                need(act, s_patch, b - 1)
                nc.scalar.activation(bmask[s][:], bank[2 + s][:, 0:S], ACT.Sign).then_inc(s_end, 1)

            over_pairs(act, B, ends)

            for t in range(WT_BANKS):
                raw, _, f, turned = weight_turns[4 * t]
                act.wait_ge(s_wT_ps, t + 1)
                rows = 512 // turned.shape[2]
                nc.scalar.copy(turned[:, f:f + rows, :],
                               bank[4 + t % 2][:].rearrange("p (f o) -> p f o", f=rows)).then_inc(s_wT, 1)

            act.wait_ge(s_wa, 16 * len(loads_a))
            nc.scalar.activation(gates[:], gates_raw[:], ACT.Tanh).then_inc(s_gate, 1)
            act.wait_ge(s_winT_ps, 1)
            for c in range(DK):
                op = nc.scalar.activation(winT[:, c, :], bank[6][:, c * D:(c + 1) * D], ACT.Copy,
                                          scale=gres_col[:, c:c + 1])
            op.then_inc(s_winT, 1)

            def decays_a(b, s):
                need(act, a_ctx_in[s], 8 * (b - s) + 16)
                need(act, a_scale, b - 1)
                for k in range(TS):
                    op = nc.scalar.activation(a_junk[s][k][:], a_ctx[s][:, k, :], ACT.Square,
                                              accum_out=a_ssq[s][:, k:k + 1])
                op.then_inc(a_ssqd, 1)
                need(act, a_z_ok, b + 1)
                need(act, a_mT_ok, b - 1)
                nc.scalar.activation(a_e[s][:], a_z[s][:], ACT.Exp, scale=-DT).then_inc(a_e_ok, 1)

            def turned_a(b, s):
                need(act, a_xsT_ps, b + 1)
                need(act, a_out_ps, b - 1)
                nc.scalar.copy(a_xsT[s][:].rearrange("p c t -> p (c t)"), bank[s][:]).then_inc(a_xsT_ok, 1)

            def body_a(b, s):
                if not beyond(b + 2, B):
                    decays_a(b + 2, s)
                if not is_last(b, B):
                    turned_a(b + 1, 1 - s)

            decays_a(0, 0)
            decays_a(1, 1)
            turned_a(0, 0)
            over_pairs(act, B, body_a)

            act.wait_ge(a_out_ps, B)
            act.wait_ge(s_wb, 16 * len(loads_b))

            def layer_b(layer, half, m):
                if not 0 <= m < ITEMS:
                    return
                g = m % 4
                act.wait_ge(b_ps[layer - 1], ITEMS * half + m + 1)
                if layer == 1:
                    for c in range(DK):
                        op = nc.scalar.activation(b_h1[g][:, c, :], bank[2 * g + c][:], ACT.Gelu,
                                                  bias=cb1[:, c:c + 1])
                elif layer == 2:
                    op = nc.scalar.activation(b_h2[g][:], bank[2 * g][:], ACT.Gelu, bias=cb2[:])
                elif layer == 3:
                    op = nc.scalar.activation(b_h3[g][:], bank[2 * g + 1][0:D // 4, :], ACT.Gelu, bias=cb3[:])
                else:
                    op = nc.scalar.activation(b_tt[g][:], bank[2 * g][:], ACT.Tanh, bias=cb4[:], scale=0.5)
                op.then_inc(b_ok[layer - 1], 1)

            def global_b(step, half):
                act.wait_ge(b_gps, 3 * half + step + 1)
                if step == 0:
                    op = nc.scalar.activation(b_g1[:], bank[1][:, 0:8], ACT.Gelu, bias=gb1[:], scale=1.0 / S)
                elif step == 1:
                    op = nc.scalar.activation(b_g2[:], bank[3][0:D // 4, 0:8], ACT.Gelu, bias=gb2[:])
                else:
                    op = nc.scalar.activation(b_gt[:], bank[5][:, 0:8], ACT.Tanh, bias=gb3[:], scale=0.5)
                op.then_inc(b_gok, 1)

            act.wait_ge(s_vconst, 8)
            with act.Fori(0, 2) as half:
                for g in range(4):
                    act.wait_ge(b_xT_ps, 4 * half + g + 1)
                    for c in range(DK):
                        for q in range(2):
                            op = nc.scalar.activation(
                                b_o[g][:, c, q * S:(q + 1) * S], bank[2 * g + c][:, q * S:(q + 1) * S],
                                ACT.Copy, accum_out=b_sum[:, c, 2 * g + q:2 * g + q + 1])
                    op.then_inc(b_o_ok, 1)
                for m in range(ITEMS + 3):
                    layer_b(4, half, m - 3)
                    layer_b(3, half, m - 2)
                    if 1 <= m <= 3:
                        global_b(m - 1, half)
                    layer_b(2, half, m - 1)
                    layer_b(1, half, m)

            act.wait_ge(b_nstat, NG)
            act.wait_ge(s_wc, 16 * len(loads_c))

            def ctxT_c(b, s, h):
                need(act, c_ctxT_ps, 2 * b + 2 - h)
                need(act, c_v_ps, b - 1)
                nc.scalar.copy(c_ctxT[s][:, 2 * h:2 * h + 2, :].rearrange("p c t -> p (c t)"),
                               bank[4 + h][:]).then_inc(c_ctxT_ok, 1)

            def high_q(b):
                need(act, c_q_ok, b + 1)
                need(act, c_stack_in, 16 * STACK_DMAS * b)
                nc.scalar.copy(c_parts[:, Q_HI, :, :], c_qT[:]).then_inc(c_qhi_ok, 1)

            def xnTq_c(b):
                need(act, c_xnT_ps, b + 1)
                need(act, c_q_ps, b)
                need(act, c_xnT_ok, b)
                nc.scalar.copy(c_xnTq[:].rearrange("p c t -> p (c t)"), bank[5][:]).then_inc(c_xnTq_ok, 1)

            def xnT_c(b, s):
                need(act, c_xnTq_ok, b + 1)
                need(act, c_out_ps, b - 1)
                nc.scalar.copy(c_xnT[s][:], c_xnTq[:]).then_inc(c_xnT_ok, 1)

            def exps_c(b, hg, tc):
                n = 2 * b + hg
                need(act, c_s_ok, TS * n + tc + 1)
                need(act, c_pT_ps, QH * (n - 1))
                for j in range(QH):
                    op = nc.scalar.activation(c_p[hg][:, tc, j, :], c_s[hg][:, tc, j, :], ACT.Exp,
                                              bias=c_nmx[hg][:, tc, j:j + 1], scale=SCALE,
                                              accum_out=c_sum[hg][:, tc, j:j + 1])
                op.then_inc(c_p_ok, 1)

            def probsT_c(b, hg):
                n = 2 * b + hg
                for j in range(0, QH, 2):
                    need(act, c_pT_ps, QH * n + j + 1)
                    need(act, c_up_ps, n - 1)
                    nc.scalar.copy(c_pT[hg][:, j, :], bank[j][:]).then_inc(c_pT_act, 1)

            def update_c(b, s, hg):
                need(act, c_up_ps, 2 * b + hg + 1)
                need(act, c_out_ps, b - 1)
                nc.scalar.copy(c_upT[s][:, hg, :], bank[6][:, hg * S:(hg + 1) * S]).then_inc(c_up_ok, 1)

            def body_c(b, s):
                last, first = is_last(b, B), is_first(b)
                if not last:
                    xnTq_c(b + 1)
                exps_c(b, 0, 0)
                exps_c(b, 0, 1)
                if not first:
                    probsT_c(b - 1, 1)
                if not last:
                    high_q(b + 1)
                if not beyond(b + 2, B):
                    ctxT_c(b + 2, s, 1)
                if not first:
                    update_c(b - 1, 1 - s, 1)
                exps_c(b, 1, 0)
                probsT_c(b, 0)
                if not beyond(b + 2, B):
                    ctxT_c(b + 2, s, 0)
                update_c(b, s, 0)
                exps_c(b, 1, 1)
                if not last:
                    xnT_c(b + 1, 1 - s)

            ctxT_c(0, 0, 1)
            ctxT_c(0, 0, 0)
            xnTq_c(0)
            xnT_c(0, 0)
            high_q(0)
            ctxT_c(1, 1, 1)
            ctxT_c(1, 1, 0)
            over_pairs(act, B, body_c)
            probsT_c(B - 1, 1)
            update_c(B - 1, 1, 1)

            act.wait_ge(c_nstat, B)
            act.wait_ge(s_wd, 16 * len(loads_d))

            def xnT_d(n, s):
                need(act, d_xT_ps, n + 1)
                need(act, d_p_ps, n - 1)
                for c in range(DK):
                    op = nc.scalar.copy(d_xnT[s][:, c, :], bank[4 + c][:])
                op.then_inc(d_xT_ok, 1)

            def hidden_d(n, j):
                m = 4 * n + j
                need(act, d_h_ps, m + 1)
                need(act, d_q_ps, m - 1)
                for e in range(2):
                    op = nc.scalar.activation(d_h[j % 2][:, e, :], bank[2 * (j % 2) + e][:],
                                              ACT.Gelu_apprx_tanh, bias=b1_col[:, 2 * j + e:2 * j + e + 1])
                op.then_inc(d_h_ok, 1)

            def body_d(n, s):
                hidden_d(n, 0)
                hidden_d(n, 1)
                if not is_last(n, NG):
                    xnT_d(n + 1, 1 - s)
                hidden_d(n, 2)
                hidden_d(n, 3)

            xnT_d(0, 0)
            over_pairs(act, NG, body_d)

        @block.tensor
        def _(pe):
            mm = nc.tensor.matmul
            pe.wait_ge(s_const, 5)
            pe.wait_ge(s_bchain, 4)
            for k in range(TS):
                op = nc.tensor.transpose(bank[0][:, k * B:(k + 1) * B], bound[:, k * P:(k + 1) * P],
                                         ident[0:B, 0:B])
            op.then_inc(s_boundT_ps, 1)

            def count(b, s):
                need(pe, s_hit, b + 1)
                need(pe, s_end, b - 1)
                for k in range(TS):
                    op = mm(bank[2 + s][:, 0:S], ones_bf[:], hit[s][k][:], start=k == 0, stop=k == TS - 1)
                op.then_inc(s_cnt, 1)

            over_pairs(pe, B, count)

            pe.wait_ge(s_wc, 16 * len(loads_c))
            for t in range(WT_BANKS):
                need(pe, s_wT, t - 1)
                for q in range(4):
                    raw, o, f, _ = weight_turns[4 * t + q]
                    op = nc.tensor.transpose(bank[4 + t % 2][:, q * P:(q + 1) * P],
                                             raw[:, o, f * P:(f + 1) * P], ident[:])
                op.then_inc(s_wT_ps, 1)

            pe.wait_ge(s_wa, 16 * len(loads_a))
            for c in range(DK):
                for o in range(DK):
                    op = nc.tensor.transpose(bank[6][:, c * D + o * P:c * D + (o + 1) * P],
                                             win_raw[:, o, c * P:(c + 1) * P], ident[:])
            op.then_inc(s_winT_ps, 1)

            pe.wait_ge(s_boundT, 1)
            pe.wait_ge(s_winT, 1)

            def turn_a(b, s):
                need(pe, a_xs_ok, b + 1)
                need(pe, a_xsT_ok, b - 1)
                for c in range(DK):
                    for k in range(TS):
                        op = nc.tensor.transpose(bank[s][:, c * S + k * P:c * S + (k + 1) * P],
                                                 a_xs[s][:, k, c * P:(c + 1) * P], ident[:])
                op.then_inc(a_xsT_ps, 1)

            def mix_a(b, s):
                need(pe, a_xsT_ok, b + 1)
                need(pe, a_u_ok, b + 1)
                need(pe, a_mT_ok, b + 1)
                need(pe, a_x1, b - 1)
                for k in range(TS):
                    dst = bank[2 + s][:, k * D:(k + 1) * D]
                    for c in range(DK):
                        mm(dst, a_xsT[s][:, c, k * P:(k + 1) * P], winT[:, c, :], start=c == 0, stop=False)
                    for q in range(TS):
                        op = mm(dst, a_mT[s][:, q, k * P:(k + 1) * P], a_u[s][:, q, :],
                                start=False, stop=q == TS - 1)
                op.then_inc(a_out_ps, 1)

            def body_a(b, s):
                if not is_last(b, B):
                    turn_a(b + 1, 1 - s)
                mix_a(b, s)

            turn_a(0, 0)
            over_pairs(pe, B, body_a)

            pe.wait_ge(s_wb, 16 * len(loads_b))
            pe.wait_ge(s_vconst, 8)
            pe.wait_ge(s_wT, WT_BANKS)
            pe.wait_ge(a_x1, B)

            def layer_b(layer, half, m):
                if not 0 <= m < ITEMS:
                    return
                g, n = m % 4, ITEMS * half + m
                lo, hi = bank[2 * g], bank[2 * g + 1]
                if layer == 1:
                    if m < 4:
                        pe.wait_ge(b_o_ok, 4 * half + g + 1)
                    else:
                        pe.wait_ge(b_upd, n - 3)
                    for h in range(DK):
                        for c in range(DK):
                            op = mm((lo, hi)[h][:], cw1[:, c, h * P:(h + 1) * P], b_o[g][:, c, :],
                                    start=c == 0, stop=c == DK - 1)
                elif layer == 2:
                    pe.wait_ge(b_ok[0], n + 1)
                    for c in range(DK):
                        op = mm(lo[:], cw2[:, c, :], b_h1[g][:, c, :], start=c == 0, stop=c == DK - 1)
                elif layer == 3:
                    pe.wait_ge(b_ok[1], n + 1)
                    op = mm(hi[0:D // 4, :], cw3[:], b_h2[g][:], start=True, stop=True)
                else:
                    pe.wait_ge(b_ok[2], n + 1)
                    op = mm(lo[:], cw4[:], b_h3[g][:], start=True, stop=True)
                op.then_inc(b_ps[layer - 1], 1)

            def global_b(step, half):
                if step == 0:
                    pe.wait_ge(b_o_ok, 4 * half + 4)
                    pe.wait_ge(b_ok[0], ITEMS * half + 1)
                    for c in range(DK):
                        op = mm(bank[1][:, 0:8], gw1[:, c, :], b_sum[:, c, :], start=c == 0, stop=c == DK - 1)
                elif step == 1:
                    pe.wait_ge(b_ok[0], ITEMS * half + 2)
                    pe.wait_ge(b_gok, 3 * half + 1)
                    op = mm(bank[3][0:D // 4, 0:8], gw2[:], b_g1[:], start=True, stop=True)
                else:
                    pe.wait_ge(b_ok[0], ITEMS * half + 3)
                    pe.wait_ge(b_gok, 3 * half + 2)
                    op = mm(bank[5][:, 0:8], gw3[:], b_g2[:], start=True, stop=True)
                op.then_inc(b_gps, 1)

            def back_b(half, g):
                pe.wait_ge(b_upd, ITEMS * half + ITEMS - 4 + g + 1)
                for k in range(GT):
                    for c in range(DK):
                        op = nc.tensor.transpose(
                            bank[2 * g + k // 2][:, (k % 2) * D + c * P:(k % 2) * D + (c + 1) * P],
                            b_o[g][:, c, k * P:(k + 1) * P], ident[:])
                op.then_inc(b_back, 1)

            with pe.Fori(0, 2) as half:
                for g in range(4):
                    pe.wait_ge(b_xn_ok, 4 * half + g + 1)
                    pe.wait_ge(b_x2, 4 * half + g + 1)
                    for c in range(DK):
                        for k in range(GT):
                            op = nc.tensor.transpose(bank[2 * g + c][:, k * P:(k + 1) * P],
                                                     b_xn[g][:, k, c * P:(c + 1) * P], ident[:])
                    op.then_inc(b_xT_ps, 1)
                for m in range(ITEMS + 3):
                    layer_b(4, half, m - 3)
                    if 2 <= m <= 4:
                        pe.wait_ge(b_gok, 3 * half + m - 1)
                    layer_b(3, half, m - 2)
                    layer_b(2, half, m - 1)
                    if 1 <= m <= 3:
                        global_b(m - 1, half)
                    layer_b(1, half, m)
                    if m >= ITEMS:
                        back_b(half, m - ITEMS)
                back_b(half, 3)

            pe.wait_ge(b_x2, NG + 4)

            def ctxT_c(b, s, h):
                need(pe, c_ctx_in[s], 8 * (b - s) + 16)
                need(pe, (c_vraw, c_q_ok)[h], b)
                for c in range(2):
                    for k in range(TS):
                        f = 2 * h + c
                        op = nc.tensor.transpose(bank[4 + h][:, c * S + k * P:c * S + (k + 1) * P],
                                                 c_ctx[s][:, k, f * P:(f + 1) * P], ident[:])
                op.then_inc(c_ctxT_ps, 1)

            def k_c(b, s):
                need(pe, c_ctxT_ok, 2 * b + 2)
                for m in range(DK):
                    for f in range(FK):
                        op = mm(bank[4][:, m * S:(m + 1) * S], wsrcT[:, f, m * P:(m + 1) * P],
                                c_ctxT[s][:, f, :], start=f == 0, stop=f == FK - 1)
                op.then_inc(c_k_ps, 1)

            def xnT_c(b, s):
                need(pe, c_xn_ok, b + 1)
                need(pe, c_ctxT_ok, 2 * b + 2)
                for c in range(DK):
                    for k in range(TS):
                        op = nc.tensor.transpose(bank[5][:, c * S + k * P:c * S + (k + 1) * P],
                                                 c_xn[s][:, k, c * P:(c + 1) * P], ident[:])
                op.then_inc(c_xnT_ps, 1)

            def v_c(b, s):
                need(pe, c_k_ok, b + 1)
                for k in range(TS):
                    for f in range(FK):
                        op = mm(bank[4][:, k * D:(k + 1) * D], c_ctxT[s][:, f, k * P:(k + 1) * P],
                                wsrcT[:, f, D:2 * D], start=f == 0, stop=f == FK - 1)
                op.then_inc(c_v_ps, 1)

            def q_c(b, s):
                need(pe, c_xnTq_ok, b + 1)
                for m in range(DK):
                    for c in range(DK):
                        op = mm(bank[5][:, m * S:(m + 1) * S], wtgtT[:, c, m * P:(m + 1) * P],
                                c_xnTq[:, c, :], start=c == 0, stop=c == DK - 1)
                op.then_inc(c_q_ps, 1)

            def scores_c(b, s, hg):
                need(pe, c_stack_in, 16 * STACK_DMAS * (b + 1))
                scores_free(pe, b, hg - 1)
                need(pe, c_s_ok, TS * (2 * b + hg))
                for tc in range(TS):
                    for j in range(QH):
                        op = mm(bank[j][:, tc * S:(tc + 1) * S], c_stack[s][:, 0, j, hg, tc * P:(tc + 1) * P],
                                c_stack[s][:, 1, j, hg, :], start=True, stop=True)
                op.then_inc(c_s_ps, 1)

            def probsT_c(b, hg):
                need(pe, c_pn_ok, 2 * b + hg + 1)
                n = 2 * b + hg + 2
                need(pe, c_s_ok, TS * (min(n, 2 * B) if isinstance(n, int) else n))
                for j in range(QH):
                    for q in range(TS):
                        for tc in range(TS):
                            op = nc.tensor.transpose(
                                bank[j][:, q * S + tc * P:q * S + (tc + 1) * P],
                                c_p[hg][:, tc, j, q * P:(q + 1) * P], ident[:])
                    op.then_inc(c_pT_ps, 1)

            def update_c(b, s, hg):
                scores_free(pe, b, hg + 1)
                need(pe, c_v_ok, b + 1)
                need(pe, c_up_ok, 2 * b + hg)
                for q in range(TS):
                    for j in range(QH):
                        h = QH * hg + j
                        op = mm(bank[6][j * HD:(j + 1) * HD, hg * S:(hg + 1) * S],
                                c_v[s][:, q, h * HD:(h + 1) * HD], c_pT[hg][:, j, q * S:(q + 1) * S],
                                start=q == 0, stop=q == TS - 1)
                op.then_inc(c_up_ps, 1)

            def out_c(b, s):
                need(pe, c_up_ok, 2 * b + 2)
                need(pe, c_xnT_ok, b + 1)
                need(pe, c_x3, b)
                for k in range(TS):
                    for f in range(2 * DK):
                        src = c_xnT[s][:, f, :] if f < DK else c_upT[s][:, f - DK, :]
                        op = mm(bank[7][:, k * D:(k + 1) * D], src[:, k * P:(k + 1) * P], woutT[:, f, :],
                                start=f == 0, stop=f == 2 * DK - 1)
                op.then_inc(c_out_ps, 1)

            def body_c(b, s):
                last, first = is_last(b, B), is_first(b)
                if not last:
                    k_c(b + 1, 1 - s)
                scores_c(b, s, 0)
                if not last:
                    xnT_c(b + 1, 1 - s)
                    v_c(b + 1, 1 - s)
                    q_c(b + 1, 1 - s)
                if not first:
                    probsT_c(b - 1, 1)
                if not beyond(b + 2, B):
                    ctxT_c(b + 2, s, 1)
                if not first:
                    update_c(b - 1, 1 - s, 1)
                scores_c(b, s, 1)
                if not first:
                    out_c(b - 1, 1 - s)
                probsT_c(b, 0)
                if not beyond(b + 2, B):
                    ctxT_c(b + 2, s, 0)
                update_c(b, s, 0)

            ctxT_c(0, 0, 1)
            ctxT_c(0, 0, 0)
            k_c(0, 0)
            xnT_c(0, 0)
            v_c(0, 0)
            q_c(0, 0)
            ctxT_c(1, 1, 1)
            ctxT_c(1, 1, 0)
            over_pairs(pe, B, body_c)
            probsT_c(B - 1, 1)
            update_c(B - 1, 1, 1)
            out_c(B - 1, 1)

            pe.wait_ge(s_wd, 16 * len(loads_d))
            pe.wait_ge(c_x3, B)

            def xnT_d(n, s):
                need(pe, d_xn_ok, n + 1)
                need(pe, d_p_ok, n)
                for c in range(DK):
                    for k in range(GT):
                        op = nc.tensor.transpose(bank[4 + c][:, k * P:(k + 1) * P],
                                                 d_xn[s][:, k, c * P:(c + 1) * P], ident[:])
                op.then_inc(d_xT_ps, 1)

            def lowrank_d(n, s):
                need(pe, d_xT_ok, n + 1)
                for c in range(DK):
                    op = mm(bank[4][:], u1_sb[:, c, :], d_xnT[s][:, c, :], start=c == 0, stop=c == DK - 1)
                op.then_inc(d_p_ps, 1)

            def hidden_d(n, s, j):
                need(pe, d_p_ok, n + 1)
                need(pe, d_h_ok, 4 * n + j - 1)
                for e in range(2):
                    mm(bank[2 * (j % 2) + e][:], v1_hi[:, 2 * j + e, :], d_pT[s][:], start=True, stop=False)
                    op = mm(bank[2 * (j % 2) + e][:], v1_lo[:, 2 * j + e, :], d_pT[s][:], start=False, stop=True)
                op.then_inc(d_h_ps, 1)

            def second_d(n, s, j):
                need(pe, d_h_ok, 4 * n + j + 1)
                need(pe, d_q_ok, n)
                for e in range(2):
                    op = mm(bank[6][e * RANK:(e + 1) * RANK, :], u2_sb[:, 2 * j + e, :],
                            d_h[j % 2][:, e, :], start=j == 0, stop=j == 3)
                op.then_inc(d_q_ps, 1)

            def out_d(n, s, half):
                need(pe, d_q_ok, n + 1)
                need(pe, d_y_ok, 2 * n + half)
                for k in range(2):
                    t = 2 * half + k
                    op = mm(bank[7][:, k * D:(k + 1) * D], d_qT[s][:, t * P:(t + 1) * P], v2_sb[:],
                            start=True, stop=True)
                op.then_inc(d_y_ps, 1)

            def body_d(n, s):
                first, last = is_first(n), is_last(n, NG)
                hidden_d(n, s, 0)
                hidden_d(n, s, 1)
                if not last:
                    xnT_d(n + 1, 1 - s)
                if not first:
                    out_d(n - 1, 1 - s, 0)
                second_d(n, s, 0)
                hidden_d(n, s, 2)
                second_d(n, s, 1)
                hidden_d(n, s, 3)
                if not last:
                    lowrank_d(n + 1, 1 - s)
                if not first:
                    out_d(n - 1, 1 - s, 1)
                second_d(n, s, 2)
                second_d(n, s, 3)

            xnT_d(0, 0)
            lowrank_d(0, 0)
            pe.wait_ge(s_v1, 2)
            over_pairs(pe, NG, body_d)
            out_d(NG - 1, 1, 0)
            out_d(NG - 1, 1, 1)

        @block.vector
        def _(dve):
            v = nc.vector

            v.memset(ones_row[:], 1.0).then_inc(s_bchain, 1)
            v.memset(ones_full[:], 1.0)
            v.memset(ones_bf[:], 1.0)
            v.memset(sgn[0:P // 2, :], 1.0)
            v.memset(sgn[P // 2:P, :], -1.0).then_inc(s_vconst, 1)
            dve.wait_ge(s_lens, 16)
            v.tensor_copy(lens_f[:], lens_i[:]).then_inc(s_bchain, 1)
            dve.wait_ge(s_bchain, 2)
            v.tensor_tensor_scan(bound[:], ones_row[:], lens_f[:], -1.0, ALU.mult, ALU.add).then_inc(s_bchain, 1)
            dve.wait_ge(s_bchain, 3)
            v.tensor_scalar(wrap[:], bound[:], 0.0, float(S), ALU.is_lt, ALU.mult).then_inc(s_vconst, 1)
            dve.wait_ge(s_vconst, 2)
            v.tensor_tensor(bound[:], bound[:], wrap[:], ALU.add).then_inc(s_bchain, 1)
            dve.wait_ge(s_boundT_ps, 1)
            v.tensor_copy(boundT[:].rearrange("p k b -> p (k b)"), bank[0][:, 0:TS * B]).then_inc(s_boundT, 1)
            dve.wait_ge(s_boundT, 1)
            dve.wait_ge(s_const, 5)

            def hits(b, s):
                need(dve, s_cnt, b - 1)
                for k in range(TS):
                    op = v.tensor_scalar(hit[s][k][:], iota_row[:], boundT[:, k, bass.ds(b, 1)], None,
                                         ALU.is_equal)
                op.then_inc(s_hit, 1)

            def patches(b, s):
                need(dve, s_end, b + 1)
                v.tensor_tensor_scan(patches_b[:, b, :], ones_full[:], bmask[s][:], 0.0, ALU.mult, ALU.add)\
                    .then_inc(s_patch, 1)

            def body_patch(b, s):
                if not beyond(b + 2, B):
                    hits(b + 2, s)
                patches(b, s)

            hits(0, 0)
            hits(1, 1)
            over_pairs(dve, B, body_patch)
            dve.wait_ge(s_patch, B)

            dve.wait_ge(s_wa, 16 * len(loads_a))
            dve.wait_ge(s_gate, 1)
            v.tensor_scalar(ginit_b[:], ginit_b[:], math.exp(LOGP), None, ALU.mult).then_inc(s_scaled, 1)
            v.tensor_scalar(bin_b[:], bin_b[:], gates[:, 0:1], None, ALU.mult).then_inc(s_scaled, 1)
            v.tensor_scalar(bout_b[:], bout_b[:], gates[:, 2:3], None, ALU.mult)
            v.tensor_scalar(b2_b[:], b2_b[:], gates[:, 3:4], None, ALU.mult).then_inc(s_scaled, 1)
            dve.wait_ge(s_scaled, 3)

            def next_moments(b, s, nbn, nstat, nnext, x_ok):
                need_alone(dve, x_ok, b + 1, s_passed)
                for k in range(TS):
                    op = v.bn_stats(n_st[:, k, :], x_sb[:, bass.ds(TS * b + k, 1), :].rearrange("p o d -> p (o d)"))
                op.then_inc(nbn, 1)
                need(dve, nbn, b + 1)
                need_alone(dve, nnext, 2 * (b - 1), s_passed)
                for k in range(TS):
                    op = v.bn_aggr(n_mv[s][:, k, :], n_st[:, k, :])
                op.then_inc(nstat, 1)

            def moments_a(b, s):
                for k in range(TS):
                    op = v.bn_stats(a_st[s][:, k, :], x_sb[:, bass.ds(TS * b + k, 1), :].rearrange("p o d -> p (o d)"))
                op.then_inc(a_bn, 1)
                need(dve, a_e_ok, b - 1)
                for q in range(TS):
                    op = v.tensor_scalar(a_z[s][:, q, :], patches_b[:, bass.ds(b, 1), :].rearrange("p o t -> p (o t)"),
                                         q1_col[:, q:q + 1], lag_floor[:, q:q + 1], ALU.subtract, ALU.max)
                op.then_inc(a_z_ok, 1)
                need(dve, a_bn, b + 1)
                need_alone(dve, a_scale, b - 1, s_passed)
                for k in range(TS):
                    op = v.bn_aggr(a_mv[s][:, k, :], a_st[s][:, k, :])
                op.then_inc(a_stat, 1)

            def normalise_a(b, s):
                need(dve, a_stat, b + 1)
                need(dve, a_scale, b + 1)
                need(dve, a_xsT_ps, b - 1)
                for k in range(TS):
                    op = v.tensor_scalar(a_xs[s][:, k, :], x_sb[:, bass.ds(TS * b + k, 1), :].rearrange("p o d -> p (o d)"),
                                         a_mv[s][:, k, 0:1], a_scl[s][:, k:k + 1], ALU.subtract, ALU.mult)
                op.then_inc(a_xs_ok, 1)

            def operands_a(b, s):
                need(dve, a_ctx_in[s], 8 * (b - s) + 16)
                need(dve, a_out_ps, b - 1)
                for k in range(TS):
                    op = v.scalar_tensor_tensor(a_u[s][:, k, :], a_ctx[s][:, k, 0:D],
                                                a_scl[s][:, TS + k:TS + k + 1], ginit_b[:], ALU.mult, ALU.mult)
                op.then_inc(a_u_ok, 1)
                need(dve, a_e_ok, b + 1)
                v.scalar_tensor_tensor(a_mT[s][:].rearrange("p q t -> p (q t)"),
                                       a_e[s][:].rearrange("p q t -> p (q t)"), 1.5,
                                       a_e[s][:].rearrange("p q t -> p (q t)"), ALU.is_le, ALU.mult)\
                    .then_inc(a_mT_ok, 1)

            def finish_a(b, s):
                need(dve, a_out_ps, b + 1)
                need(dve, a_xb, b + 1)
                xb = x_sb[:, bass.ds(TS * b, TS), :].rearrange("p k d -> p (k d)")
                v.scalar_tensor_tensor(xb, bank[2 + s][:], gates[:, 0:1], xb, ALU.mult, ALU.add).then_inc(a_x1, 1)
                next_moments(b, s, a_nbn, a_nstat, a_next, a_x1)

            def body_a(b, s):
                if not is_last(b, B):
                    normalise_a(b + 1, 1 - s)
                if not beyond(b + 2, B):
                    moments_a(b + 2, s)
                if not is_first(b):
                    finish_a(b - 1, 1 - s)
                if not is_last(b, B):
                    operands_a(b + 1, 1 - s)

            dve.wait_ge(s_x_in, 16 * 4)
            moments_a(0, 0)
            moments_a(1, 1)
            normalise_a(0, 0)
            operands_a(0, 0)
            over_pairs(dve, B, body_a)
            finish_a(B - 1, 1)

            dve.wait_ge(s_wb, 16 * len(loads_b))
            v.tensor_copy(cw4[:], cw4_col[:].to_broadcast([D // 4, P])).then_inc(s_vconst, 1)
            v.tensor_copy(gw3[:], gw3_col[:].to_broadcast([D // 4, P])).then_inc(s_vconst, 1)
            v.tensor_scalar(cb4[:], cb4[:], 0.5, None, ALU.mult).then_inc(s_vconst, 1)
            v.tensor_scalar(gb3[:], gb3[:], 0.5, None, ALU.mult).then_inc(s_vconst, 1)
            v.tensor_scalar(k_tt[:], arange[:], sgn[:], 0.3, ALU.mult, ALU.mult).then_inc(s_vconst, 1)
            v.tensor_scalar(k_gt[:], arange[:], sgn[:], 0.7, ALU.mult, ALU.mult)
            v.tensor_scalar(k_one[:], sgn[:], 0.1, None, ALU.mult).then_inc(s_vconst, 1)
            dve.wait_ge(s_vconst, 8)
            dve.wait_ge(s_wT, WT_BANKS)
            dve.wait_ge(a_next, 2 * B)
            dve.sem_inc(b_x2, 4)

            def cycle_b(half, m):
                g, n = m % 4, ITEMS * half + m
                dve.wait_ge(b_ok[3], n + 1)
                for q in range(2):
                    tq = b_tt[g][:, q * S:(q + 1) * S]
                    op = v.tensor_scalar(tq, tq, k_tt[:], b_kb[:, 2 * g + q:2 * g + q + 1], ALU.mult, ALU.add)
                op.then_inc(b_mid, 1)
                dve.wait_ge(b_mid, 2 * n + 1)
                v.tensor_tensor(b_t0[m % 2][:], b_tt[g][:], b_o[g][:, 1, :], ALU.mult)
                v.tensor_tensor(b_t1[m % 2][:], b_tt[g][:], b_o[g][:, 0, :], ALU.mult).then_inc(b_mid, 1)
                dve.wait_ge(b_mid, 2 * n + 2)
                v.tensor_tensor(b_o[g][:, 0, :], b_o[g][:, 0, :], b_t0[m % 2][:], ALU.add)
                v.tensor_tensor(b_o[g][:, 1, :], b_o[g][:, 1, :], b_t1[m % 2][:], ALU.subtract).then_inc(b_upd, 1)

            def rows(t, count):
                return x_sb[:, bass.ds(t, count), :].rearrange("p k d -> p (k d)")

            def x_b(half, g):
                n = 4 * half + g
                dve.wait_ge(b_back, n + 1)
                for h in range(2):
                    xh = rows(GT * n + 2 * h, 2)
                    op = v.scalar_tensor_tensor(xh, bank[2 * g + h][:], gates[:, 1:2], xh, ALU.mult, ALU.add)
                op.then_inc(b_x2, 1)

            with dve.Fori(0, 2) as half:
                for g in range(4):
                    for k in range(GT):
                        t = GT * (4 * half + g) + k
                        op = v.tensor_scalar(b_xn[g][:, k, :], rows(t, 1), mu[:, bass.ds(t, 1)],
                                             rstd[:, bass.ds(t, 1)], ALU.subtract, ALU.mult)
                    op.then_inc(b_xn_ok, 1)
                dve.wait_ge(b_gok, 3 * half + 3)
                v.tensor_scalar(b_kb[:], b_gt[:], k_gt[:], k_one[:], ALU.mult, ALU.add).then_inc(b_kbok, 1)
                dve.wait_ge(b_kbok, half + 1)
                for m in range(ITEMS):
                    cycle_b(half, m)
                    if m >= ITEMS - 2:
                        x_b(half, m - ITEMS + 2)
                x_b(half, 2)
                x_b(half, 3)
                for g in range(4):
                    n = 4 * half + g
                    need_alone(dve, b_x2, 4 + n + 1, s_passed)
                    for k in range(GT):
                        op = v.bn_stats(b_st[g][:, k, :], rows(GT * n + k, 1))
                    op.then_inc(b_nbn, 1)
                for g in range(4):
                    n = 4 * half + g
                    need_alone(dve, b_nbn, n + 1, s_passed)
                    need_alone(dve, b_next, 2 * (n + 1), s_passed)
                    for k in range(GT):
                        op = v.bn_aggr(b_mv[g][:, k, :], b_st[g][:, k, :])
                    op.then_inc(b_nstat, 1)

            dve.wait_ge(b_next, 2 * NG + 2 * 4)
            dve.wait_ge(s_wc, 16 * len(loads_c))

            def xn_c(b, s):
                need(dve, c_xnT_ps, b - 1)
                for k in range(TS):
                    op = v.tensor_scalar(c_xn[s][:, k, :], x_sb[:, bass.ds(TS * b + k, 1), :].rearrange("p o d -> p (o d)"),
                                         mu[:, bass.ds(TS * b + k, 1)], rstd[:, bass.ds(TS * b + k, 1)],
                                         ALU.subtract, ALU.mult)
                op.then_inc(c_xn_ok, 1)

            def neg_c(b, s):
                v.tensor_scalar(c_neg[s][:], mask_b[:, bass.ds(b, 1), :].rearrange("p o t -> p (o t)"), 0.0, MASKED,
                                ALU.is_equal, ALU.mult).then_inc(c_neg_ok, 1)

            def biased(dst, src_bank, col, b, ps, ok, used, use_count):
                need(dve, ps, b + 1)
                need(dve, used, use_count)
                for m in range(DK):
                    op = v.scalar_tensor_tensor(dst[:, m, :], src_bank[:, m * S:(m + 1) * S], col[:, m:m + 1],
                                                mask_b[:, bass.ds(b, 1), :].rearrange("p o t -> p (o t)"),
                                                ALU.add, ALU.mult)
                op.then_inc(ok, 1)

            def v_c(b, s):
                need(dve, c_v_ps, b + 1)
                need(dve, c_up_ps, 2 * (b - 1))
                v.tensor_tensor(c_v[s][:], bank[4][:].rearrange("p (k d) -> p k d", k=TS),
                                bv_b[:].unsqueeze(1).to_broadcast([P, TS, D]), ALU.add).then_inc(c_vraw, 1)
                need(dve, c_vraw, b + 1)
                for k in range(TS):
                    op = v.tensor_scalar(c_v[s][:, k, :], c_v[s][:, k, :],
                                         mask_col[:, bass.ds(b, 1), k], None, ALU.mult)
                op.then_inc(c_v_ok, 1)

            def maxima_c(b, s, hg):
                n = 2 * b + hg
                need(dve, c_neg_ok, b + 1)
                need(dve, c_p_ok, TS * (n - 1))
                need_alone(dve, c_s_ps, n + 1, s_passed)
                for tc in range(TS):
                    for j in range(QH):
                        op = v.tensor_tensor_reduce(c_s[hg][:, tc, j, :], bank[j][:, tc * S:(tc + 1) * S],
                                                    c_neg[s][:], 1.0, -3.0e38, ALU.add, ALU.max,
                                                    c_mx[hg][:, tc, j:j + 1])
                    op.then_inc(c_mx_ok, 1)
                    need(dve, c_mx_ok, TS * n + tc + 1)
                    v.tensor_scalar(c_nmx[hg][:, tc, :], c_mx[hg][:, tc, :], -SCALE, None, ALU.mult)\
                        .then_inc(c_s_ok, 1)

            def normalise_c(b, hg):
                n = 2 * b + hg
                need(dve, c_p_ok, TS * n + TS)
                v.reciprocal(c_inv[hg][:], c_sum[hg][:]).then_inc(c_inv_ok, 1)
                need(dve, c_inv_ok, n + 1)
                for tc in range(TS):
                    for j in range(QH):
                        pr = c_p[hg][:, tc, j, :]
                        op = v.tensor_scalar(pr, pr, c_inv[hg][:, tc, j:j + 1], None, ALU.mult)
                op.then_inc(c_pn_ok, 1)

            def probsT_c(b, hg):
                n = 2 * b + hg
                for j in range(1, QH, 2):
                    need(dve, c_pT_ps, QH * n + j + 1)
                    need(dve, c_up_ps, n - 1)
                    v.tensor_copy(c_pT[hg][:, j, :], bank[j][:]).then_inc(c_pT_dve, 1)

            def finish_c(b, s):
                need(dve, c_out_ps, b + 1)
                need(dve, c_xb, b + 1)
                xb = x_sb[:, bass.ds(TS * b, TS), :].rearrange("p k d -> p (k d)")
                v.scalar_tensor_tensor(xb, bank[7][:], gates[:, 2:3], xb, ALU.mult, ALU.add).then_inc(c_x3, 1)
                next_moments(b, s, c_nbn, c_nstat, c_next, c_x3)

            def body_c(b, s):
                last, first = is_last(b, B), is_first(b)
                if not last:
                    biased(c_kT, bank[4], bk_col, b + 1, c_k_ps, c_k_ok, c_k_split, 2 * (b + 1))
                maxima_c(b, s, 0)
                if not last:
                    neg_c(b + 1, 1 - s)
                    biased(c_qT, bank[5], bq_col, b + 1, c_q_ps, c_q_ok, c_qlo_ok, b + 1)
                if not first:
                    probsT_c(b - 1, 1)
                normalise_c(b, 0)
                if not last:
                    v_c(b + 1, 1 - s)
                maxima_c(b, s, 1)
                probsT_c(b, 0)
                if not first:
                    finish_c(b - 1, 1 - s)
                if not beyond(b + 2, B):
                    xn_c(b + 2, s)
                normalise_c(b, 1)

            xn_c(0, 0)
            xn_c(1, 1)
            neg_c(0, 0)
            biased(c_kT, bank[4], bk_col, 0, c_k_ps, c_k_ok, c_k_split, 0)
            v_c(0, 0)
            biased(c_qT, bank[5], bq_col, 0, c_q_ps, c_q_ok, c_qlo_ok, 0)
            over_pairs(dve, B, body_c)
            probsT_c(B - 1, 1)
            finish_c(B - 1, 1)

            dve.wait_ge(c_next, 2 * B)
            dve.wait_ge(s_wd, 16 * len(loads_d))

            def xn_d(n, s):
                need(dve, d_xT_ps, n - 1)
                for k in range(GT):
                    t = bass.ds(GT * n + k, 1)
                    op = v.tensor_scalar(d_xn[s][:, k, :], x_sb[:, t, :].rearrange("p o d -> p (o d)"),
                                         mu[:, t], rstd[:, t], ALU.subtract, ALU.mult)
                op.then_inc(d_xn_ok, 1)

            def lowrank_d(n, s):
                need(dve, d_p_ps, n + 1)
                need(dve, d_h_ps, 4 * (n - 1))
                v.tensor_copy(d_pT[s][:], bank[4][:]).then_inc(d_phi, 1)
                need(dve, d_phi, n + 1)
                low = slice(RANK, 2 * RANK)
                v.tensor_tensor(d_pT[s][low, :], bank[4][low, :], d_pT[s][low, :].bitcast(F32),
                                ALU.subtract).then_inc(d_p_ok, 1)

            def second_d(n, s):
                need(dve, d_q_ps, 4 * n + 4)
                need(dve, d_y_ps, 2 * (n - 1))
                v.tensor_copy(d_qT[s][:], bank[6][:]).then_inc(d_q_ok, 1)

            def out_d(n, half):
                need(dve, d_y_ps, 2 * n + half + 1)
                need(dve, d_xb, n + 1)
                xh = x_sb[:, bass.ds(GT * n + 2 * half, 2), :].rearrange("p k d -> p (k d)")
                v.scalar_tensor_tensor(xh, bank[7][:], gates[:, 3:4], xh, ALU.mult, ALU.add).then_inc(d_y_ok, 1)

            def body_d(n, s):
                first, last = is_first(n), is_last(n, NG)
                if not last:
                    xn_d(n + 1, 1 - s)
                if not first:
                    out_d(n - 1, 0)
                if not last:
                    lowrank_d(n + 1, 1 - s)
                if not first:
                    out_d(n - 1, 1)
                second_d(n, s)

            xn_d(0, 0)
            v.tensor_copy(v1_hi[:], v1_sb[:]).then_inc(s_v1, 1)
            dve.wait_ge(s_v1, 1)
            v.tensor_tensor(v1_lo[:], v1_sb[:], v1_hi[:].bitcast(F32), ALU.subtract).then_inc(s_v1, 1)
            lowrank_d(0, 0)
            over_pairs(dve, NG, body_d)
            out_d(NG - 1, 0)
            out_d(NG - 1, 1)


INPUTS = ["x", "ctx_2048", "mask_BxS2_if0", "mask_BxS2_fk1", "g_xattn", "g_ffn",
          "L0_xattn_W_in", "L0_xattn_b_in", "L0_xattn_g_res", "L0_xattn_g_init",
          "L0_ffn_cn_w1", "L0_ffn_cn_b1", "L0_ffn_cn_w2", "L0_ffn_cn_b2", "L0_ffn_cn_w3", "L0_ffn_cn_b3",
          "L0_ffn_cn_w4", "L0_ffn_cn_b4", "L0_ffn_gc_w1", "L0_ffn_gc_b1", "L0_ffn_gc_w2", "L0_ffn_gc_b2",
          "L0_ffn_gc_w3", "L0_ffn_gc_b3", "L0_ffn_adaptive_range",
          "L1_xattn_W_src", "L1_xattn_b_src", "L1_xattn_W_tgt", "L1_xattn_b_tgt",
          "L1_xattn_W_out", "L1_xattn_b_out",
          "L1_ffn_U1", "L1_ffn_V1", "L1_ffn_b1", "L1_ffn_U2", "L1_ffn_V2", "L1_ffn_b2"]


def kernel(**inputs):
    import concourse.bacc as bacc
    from concourse.bass_utils import run_bass_kernel_spmd

    nc = bacc.Bacc("TRN2", target_bir_lowering=False, num_devices=1)
    arrays, args = {}, []
    for name in INPUTS:
        a = np.ascontiguousarray(inputs[name])
        arrays[f"in_{name}"] = a
        args.append(nc.dram_tensor(f"in_{name}", a.shape, mybir.dt.from_np(a.dtype), kind="ExternalInput").ap())
    args.append(nc.dram_tensor("out_x", (B, S, D), F32, kind="ExternalOutput").ap())
    build(nc, *args)
    r = run_bass_kernel_spmd(nc, [arrays], core_ids=[0])
    return r.results[0]["out_x"]
```

```python
import math
from contextlib import ExitStack

import numpy as np
import concourse.bass as bass
from concourse import mybir

F32 = mybir.dt.float32
F32R = mybir.dt.float32r
I32 = mybir.dt.int32
BF16 = mybir.dt.bfloat16
ALU = mybir.AluOpType
ACT = mybir.ActivationFunctionType

P = 128
B, S, D, DC = 16, 256, 256, 512
TILES = B * S // P
TS = S // P
DK = D // P
FK = DC // P
GROUP = 512
GT = GROUP // P
NG = B * S // GROUP
HEADS, HD = 8, 32
QH = 4
F = 1024
RANK = 64
CYCLES = 3
LANES = 4
ROUND = LANES * CYCLES
ITEMS = NG * CYCLES
LN_EPS = 1e-5
RMS_EPS = 1e-5
LOGP = -0.001
DT = -math.log(-math.expm1(LOGP))
SCALE = 1.0 / math.sqrt(HD)
PARTS = 4
Q_LO, Q_HI, K_HI, K_LO = range(PARTS)
GCOL = 8
V_EARLY = 6
STACK_DMAS = 3 * QH
STAGE_C_LAST = 3 * 2 * TS * QH * S + 2 * 2 * DK * S + 2 * S + 2 * QH * DK * S
MASKED = -1e30


def item_at(slot):
    r, m = divmod(slot, ROUND + 1)
    return r * ROUND + m if slot >= 0 and m < ROUND and r < NG // LANES else None


def group_of(m):
    return m // ROUND * LANES + m % LANES


def first_slot(n):
    return n // LANES * (ROUND + 1) + n % LANES


def globals_at(slot):
    return [(n, slot - first_slot(n) - 1) for n in range(NG) if 0 <= slot - first_slot(n) - 1 < 3]


def global_slots_before(slot):
    return sum(1 for t in range(slot) if globals_at(t))


SLOTS = first_slot(NG - 1) + ROUND + 1


def need(eng, sem, count):
    if isinstance(count, int) and count <= 0:
        return
    eng.wait_ge(sem, count)


def need_alone(eng, sem, count, passed):
    if isinstance(count, int):
        return need(eng, sem, count)
    eng.wait_ge(sem, count)
    eng.sem_inc(passed, 1)


def over_pairs(eng, n, body):
    body(0, 0)
    body(1, 1)
    with eng.Fori(1, n // 2 - 1) as i:
        body(2 * i, 0)
        body(2 * i + 1, 1)
    body(n - 2, 0)
    body(n - 1, 1)


def beyond(b, n):
    return isinstance(b, int) and b >= n


def is_last(b, n):
    return isinstance(b, int) and b == n - 1


def is_first(b):
    return isinstance(b, int) and b == 0


def build(nc, x, ctx_in, lens, mask, g_xattn, g_ffn, w_in, b_in, g_res, g_init,
          cn_w1, cn_b1, cn_w2, cn_b2, cn_w3, cn_b3, cn_w4, cn_b4,
          gc_w1, gc_b1, gc_w2, gc_b2, gc_w3, gc_b3, adaptive_range,
          w_src, b_src, w_tgt, b_tgt, w_out, b_out, u1, v1, b1, u2, v2, b2, out):
    x_dram = x.rearrange("b (k p) d -> b p k d", p=P)
    ctx_dram = ctx_in.rearrange("b (k p) d -> b p k d", p=P)
    out_dram = out.rearrange("(n c) (k p) d -> n p c k d", c=GROUP // S, p=P)

    with ExitStack() as whole:
        def sb(name, shape, dt=F32, stack=whole):
            return stack.enter_context(nc.sbuf_tensor(name, shape, dt))

        def sem(name):
            return whole.enter_context(nc.semaphore(name))

        bank = [whole.enter_context(nc.psum_tensor(f"bank{i}", [P, 512], F32)) for i in range(8)]

        x_sb = sb("x_sb", [P, TILES, D])
        mu = sb("mu", [P, TILES])
        rstd = sb("rstd", [P, TILES])
        ident = sb("ident", [P, P])
        ones_bf = sb("ones_bf", [P, P], BF16)
        q1_col = sb("q1_col", [P, TS])
        lag_floor = sb("lag_floor", [P, TS])
        neg_half = sb("neg_half", [P, 2 * TS])
        sgn = sb("sgn", [P, 1])
        gates = sb("gates", [P, 4])
        gates_raw = sb("gates_raw", [P, 4])
        mask_b = sb("mask_b", [P, B, S])
        mask_col = sb("mask_col", [P, B, TS])
        gres_col = sb("gres_col", [P, DK])
        bout_b = sb("bout_b", [P, D])
        b2_b = sb("b2_b", [P, D])
        bv_b = sb("bv_b", [P, D])
        arange = sb("arange", [P, 1])
        k_tt = sb("k_tt", [P, 1])
        k_gt = sb("k_gt", [P, 1])
        k_one = sb("k_one", [P, 1])
        wsrcT = sb("wsrcT", [P, FK, 2 * D])
        wtgtT = sb("wtgtT", [P, DK, D])
        woutT = sb("woutT", [P, 2 * DK, D])
        bk_col = sb("bk_col", [P, DK])
        bq_col = sb("bq_col", [P, DK])
        u1_sb = sb("u1_sb", [P, DK, 2 * RANK])
        v1_sb = sb("v1_sb", [P, F // P, P])
        b1_col = sb("b1_col", [P, F // P])
        u2_sb = sb("u2_sb", [P, F // P, RANK])
        v2_sb = sb("v2_sb", [P, D])

        a_ssq = [sb(f"a_ssq{s}", [P, TS]) for s in range(2)]
        a_st = [sb(f"a_st{s}", [P, TS, 6]) for s in range(2)]
        a_mv = [sb(f"a_mv{s}", [P, TS, 2]) for s in range(2)]
        a_tmp = [sb(f"a_tmp{s}", [P, 2 * TS]) for s in range(2)]
        a_scl = [sb(f"a_scl{s}", [P, 2 * TS]) for s in range(2)]
        b_st = [sb(f"b_st{g}", [P, GT, 6]) for g in range(LANES)]
        b_mv = [sb(f"b_mv{g}", [P, GT, 2]) for g in range(LANES)]
        b_tmp = [sb(f"b_tmp{g}", [P, GT]) for g in range(LANES)]
        n_st = sb("n_st", [P, TS, 6])
        n_mv = [sb(f"n_mv{s}", [P, TS, 2]) for s in range(2)]
        n_tmp = [sb(f"n_tmp{s}", [P, TS]) for s in range(2)]

        with ExitStack() as st:
            a_ctx = [sb(f"a_ctx{s}", [P, TS, DC], F32, st) for s in range(2)]
            a_junk = [[sb(f"a_junk{s}{k}", [P, DC], F32, st) for k in range(TS)] for s in range(2)]
            a_xs = [sb(f"a_xs{s}", [P, TS, D], F32, st) for s in range(2)]
            a_xsT = [sb(f"a_xsT{s}", [P, DK, S], F32, st) for s in range(2)]
            a_u = [sb(f"a_u{s}", [P, TS, D], F32, st) for s in range(2)]
            a_z = [sb(f"a_z{s}", [P, TS, S], F32, st) for s in range(2)]
            a_e = [sb(f"a_e{s}", [P, TS, S], F32, st) for s in range(2)]
            a_mT = [sb(f"a_mT{s}", [P, TS, S], F32, st) for s in range(2)]
            winT = sb("winT", [P, DK, D], F32, st)
            ginit_b = sb("ginit_b", [P, D], F32, st)
            bin_b = sb("bin_b", [P, D], F32, st)
            patches_b = sb("patches_b", [P, B, S], F32, st)
            ones_row = sb("ones_row", [B, S], F32, st)
            iota_row = sb("iota_row", [P, S], F32, st)
            lens_i = sb("lens_i", [B, S], I32, st)
            lens_f = sb("lens_f", [B, S], F32, st)
            bound = sb("bound", [B, S], F32, st)
            wrap = sb("wrap", [B, S], F32, st)
            boundT = sb("boundT", [P, TS, B], F32, st)
            hit = [[sb(f"hit{s}{j}", [P, S], BF16, st) for j in range(TS)] for s in range(2)]
            bmask = [sb(f"bmask{s}", [P, S], F32, st) for s in range(2)]
            ones_full = sb("ones_full", [P, S], F32, st)
            win_raw = sb("win_raw", [P, DK, D], F32, st)
            wsrc_raw = sb("wsrc_raw", [P, FK, DC], F32, st)
            wtgt_raw = sb("wtgt_raw", [P, DK, D], F32, st)
            wout_raw = sb("wout_raw", [P, DK, 2 * D], F32, st)
        with ExitStack() as st:
            b_o = [sb(f"b_o{g}", [P, DK, GROUP], F32, st) for g in range(LANES)]
            b_h1 = [sb(f"b_h1{g}", [P, DK, GROUP], F32, st) for g in range(LANES)]
            b_h2 = [sb(f"b_h2{s}", [P, GROUP], F32, st) for s in range(2)]
            b_h3 = [sb(f"b_h3{s}", [D // 4, GROUP], F32, st) for s in range(2)]
            b_tt = [sb(f"b_tt{s}", [P, GROUP], F32, st) for s in range(2)]
            b_t0 = [sb(f"b_t0{s}", [P, GROUP], F32, st) for s in range(2)]
            b_t1 = [sb(f"b_t1{s}", [P, GROUP], F32, st) for s in range(2)]
            b_xn = [sb(f"b_xn{g}", [P, GT, D], F32, st) for g in range(2)]
            cw1 = sb("cw1", [P, DK, D], F32, st)
            cw2 = sb("cw2", [P, DK, D // 2], F32, st)
            cw3 = sb("cw3", [P, D // 4], F32, st)
            cw4_col = sb("cw4_col", [D // 4, 1], F32, st)
            cw4 = sb("cw4", [D // 4, P], F32, st)
            cb1 = sb("cb1", [P, DK], F32, st)
            cb2 = sb("cb2", [P, 1], F32, st)
            cb3 = sb("cb3", [D // 4, 1], F32, st)
            cb4 = sb("cb4", [P, 1], F32, st)
            gw1 = sb("gw1", [P, DK, D // 2], F32, st)
            gw2 = sb("gw2", [P, D // 4], F32, st)
            gw3_col = sb("gw3_col", [D // 4, 1], F32, st)
            gw3 = sb("gw3", [D // 4, P], F32, st)
            gb1 = sb("gb1", [P, 1], F32, st)
            gb2 = sb("gb2", [D // 4, 1], F32, st)
            gb3 = sb("gb3", [P, 1], F32, st)
            b_xn += [sb(f"b_xn{g}", [P, GT, D], F32, st) for g in range(2, LANES)]
            b_sum = sb("b_sum", [P, DK, 2 * LANES], F32, st)
            b_g1 = sb("b_g1", [P, 2 * LANES], F32, st)
            b_g2 = sb("b_g2", [D // 4, 2 * LANES], F32, st)
            b_gt = sb("b_gt", [P, 2 * LANES], F32, st)
            b_kb = sb("b_kb", [P, 2 * LANES], F32, st)
        with ExitStack() as st:
            c_s = [sb(f"c_s{h}", [P, TS, QH, S], F32, st) for h in range(2)]
            c_p = [sb(f"c_p{h}", [P, TS, QH, S], F32, st) for h in range(2)]
            c_pT = [sb(f"c_pT{h}", [P, QH, TS * S], F32, st) for h in range(2)]
            c_xnT = [sb(f"c_xnT{s}", [P, DK, S], F32, st) for s in range(2)]
            c_upT = [sb(f"c_upT{s}", [P, DK, S], F32, st) for s in range(2)]
            c_neg = [sb(f"c_neg{s}", [P, S], F32, st) for s in range(2)]
            c_stack = [None, sb("c_stack1", [3 * HD, 2, QH, DK, S], F32R, st)]
            c_stack[0] = sb("c_stack0", [3 * HD, 2, QH, DK, S], F32R, st)
            c_ctx = [sb(f"c_ctx{s}", [P, TS, DC], F32, st) for s in range(2)]
            c_ctxT = [sb(f"c_ctxT{s}", [P, FK, S], F32, st) for s in range(2)]
            c_xn = [sb(f"c_xn{s}", [P, TS, D], F32, st) for s in range(2)]
            c_xnTq = sb("c_xnTq", [P, DK, S], F32, st)
            c_kT = sb("c_kT", [P, DK, S], F32, st)
            c_qT = sb("c_qT", [P, DK, S], F32, st)
            c_parts = sb("c_parts", [P, PARTS, DK, S], F32R, st)
            c_v = [sb(f"c_v{s}", [P, TS, D], F32, st) for s in range(2)]
            c_mx = [sb(f"c_mx{h}", [P, TS, QH], F32, st) for h in range(2)]
            c_nmx = [sb(f"c_nmx{h}", [P, TS, QH], F32, st) for h in range(2)]
            c_sum = [sb(f"c_sum{h}", [P, TS, QH], F32, st) for h in range(2)]
            c_inv = [sb(f"c_inv{h}", [P, TS, QH], F32, st) for h in range(2)]
        with ExitStack() as st:
            sb("c_last", [P, STAGE_C_LAST], F32, st)
            d_xn = [sb(f"d_xn{s}", [P, GT, D], F32, st) for s in range(2)]
            d_xnT = [sb(f"d_xnT{s}", [P, DK, GROUP], F32, st) for s in range(2)]
            d_pT = [sb(f"d_pT{s}", [P, GROUP], F32R, st) for s in range(2)]
            v1_hi = sb("v1_hi", [P, F // P, P], F32R, st)
            v1_lo = sb("v1_lo", [P, F // P, P], F32R, st)
            d_h = [sb(f"d_h{s}", [P, 2, GROUP], F32, st) for s in range(2)]
            d_qT = [sb(f"d_qT{s}", [P, GROUP], F32, st) for s in range(2)]

        s_lens, s_wa, s_wb, s_wc, s_wd = (sem(n) for n in ("lens_in", "weights_a_in", "weights_b_in",
                                                           "weights_c_in", "weights_d_in"))
        s_zero, s_const, s_vconst = sem("ident_zeroed"), sem("pool_consts"), sem("dve_consts")
        s_bchain, s_boundT_ps, s_boundT = sem("bound_chain"), sem("boundT_in_psum"), sem("boundT_copied")
        s_hit, s_cnt, s_end, s_patch = (sem("hits_ready"), sem("hit_counts_in_psum"), sem("ends_ready"),
                                        sem("patches_ready"))
        s_winT_ps, s_winT = sem("w_inT_in_psum"), sem("w_inT_ready")
        s_wT_ps, s_wT = sem("weightT_in_psum"), sem("weightT_copied")
        s_gate, s_scaled = sem("gates_ready"), sem("weights_scaled")

        s_passed = sem("waits_passed")

        s_x0_in, s_x_in = sem("first_x_in"), sem("rest_of_x_in")
        a_ctx_in = [sem(f"a_ctx_in{s}") for s in range(2)]
        a_bn, a_stat, a_ssqd, a_pre, a_scale = (sem("a_" + n) for n in (
            "bn_stats", "moments_ready", "square_sums_ready", "scale_chain", "scales_ready"))
        a_xs_ok, a_xsT_ps, a_xsT_ok, a_u_ok = (sem("a_" + n) for n in (
            "xs_ready", "xsT_in_psum", "xsT_copied", "u_ready"))
        a_z_ok, a_e_ok, a_mT_ok, a_out_ps, a_xb, a_x1 = (sem("a_" + n) for n in (
            "lag_ready", "decay_ready", "mix_ready", "out_in_psum", "bias_added", "x_updated"))
        a_nbn, a_nstat, a_npre, a_next = (sem("a_" + n) for n in (
            "next_bn", "next_moments", "next_chain", "next_stats_ready"))

        b_xn_ok, b_xT_ps, b_o_ok = sem("b_xn_ready"), sem("b_xnT_in_psum"), sem("b_state_ready")
        b_ps = [sem(f"b_layer{i}_in_psum") for i in range(1, 5)]
        b_ok = [sem(f"b_layer{i}_ready") for i in range(1, 5)]
        b_gps, b_gok, b_kbok = sem("b_global_in_psum"), sem("b_global_ready"), sem("b_offset_ready")
        b_mid, b_upd = sem("b_update_chain"), sem("b_cycle_done")
        b_back, b_x2 = sem("b_result_in_psum"), sem("b_x_updated")
        b_nbn, b_nstat, b_npre, b_next = (sem("b_" + n) for n in (
            "next_bn", "next_moments", "next_chain", "next_stats_ready"))

        c_ctx_in = [sem(f"c_ctx_in{s}") for s in range(2)]
        c_xn_ok, c_ctxT_ps, c_ctxT_ok, c_xnT_ps, c_xnTq_ok, c_xnT_ok = (sem("c_" + n) for n in (
            "xn_ready", "ctxT_in_psum", "ctxT_copied", "xnT_in_psum", "xnTq_copied", "xnT_copied"))
        c_k_ps, c_k_ok, c_q_ps, c_q_ok, c_v_ps, c_vraw, c_v_ok = (sem("c_" + n) for n in (
            "kT_in_psum", "kT_ready", "qT_in_psum", "qT_ready", "v_in_psum", "v_biased", "v_ready"))
        c_k_split, c_qhi_ok, c_qlo_ok, c_stack_in = (sem("c_" + n) for n in (
            "k_parts_ready", "q_high_ready", "q_low_ready", "stacks_in"))
        c_neg_ok, c_s_ps, c_mx_ok, c_s_ok, c_p_ok, c_inv_ok, c_pn_ok = (sem("c_" + n) for n in (
            "mask_bias_ready", "scores_in_psum", "max_ready", "scores_ready", "probs_ready",
            "inverse_sums_ready", "probs_normalised"))
        c_pT_ps, c_pT_act, c_pT_dve, c_up_ps, c_up_ok, c_out_ps, c_xb, c_x3 = (sem("c_" + n) for n in (
            "probsT_in_psum", "even_probsT_copied", "odd_probsT_copied", "update_in_psum",
            "update_copied", "out_in_psum", "bias_added", "x_updated"))
        c_nbn, c_nstat, c_npre, c_next = (sem("c_" + n) for n in (
            "next_bn", "next_moments", "next_chain", "next_stats_ready"))

        s_v1, d_phi = sem("v1_parts_ready"), sem("d_lowrank_high_ready")
        d_xn_ok, d_xT_ps, d_xT_ok, d_p_ps, d_p_ok, d_h_ps, d_h_ok = (sem("d_" + n) for n in (
            "xn_ready", "xnT_in_psum", "xnT_copied", "lowrank_in_psum", "lowrank_copied",
            "hidden_in_psum", "hidden_ready"))
        d_q_ps, d_q_ok, d_y_ps, d_y_ok, d_xb, d_stored = (sem("d_" + n) for n in (
            "second_lowrank_in_psum", "second_lowrank_copied", "out_in_psum", "x_updated",
            "bias_added", "stored"))

        def column(v):
            return v.rearrange("(c p) -> p c", p=P)

        def row_on_all(v):
            return v.partition_broadcast(P)

        loads_a = [
            (win_raw[:], w_in.rearrange("(c p) e -> p c e", p=P)),
            (gres_col[:], column(g_res)), (ginit_b[:], row_on_all(g_init[0:D])),
            (bin_b[:], row_on_all(b_in)), (gates_raw[:, 0:4:2], row_on_all(g_xattn)),
            (gates_raw[:, 1:4:2], row_on_all(g_ffn)), (bout_b[:], row_on_all(b_out)),
            (b2_b[:], row_on_all(b2)), (bv_b[:], row_on_all(b_src[D:2 * D])),
        ]
        loads_c = [
            (wsrc_raw[:], w_src.rearrange("(c p) f -> p c f", p=P)),
            (wtgt_raw[:], w_tgt.rearrange("(c p) f -> p c f", p=P)),
            (wout_raw[:], w_out.rearrange("(c p) f -> p c f", p=P)),
            (bk_col[:], column(b_src[0:D])), (bq_col[:], column(b_tgt)),
            (mask_b[:], mask.partition_broadcast(P)),
            (mask_col[:], mask.rearrange("b (k p) -> p b k", p=P)),
        ]
        loads_b = [
            (cw1[:], cn_w1.rearrange("(c p) e -> p c e", p=P)),
            (cw2[:], cn_w2.rearrange("(c p) e -> p c e", p=P)), (cw3[:], cn_w3),
            (cw4_col[:], cn_w4), (cb1[:], column(cn_b1)), (cb2[:], column(cn_b2)),
            (cb3[:], cn_b3.rearrange("(p c) -> p c", c=1)), (cb4[:], row_on_all(cn_b4)),
            (gw1[:], gc_w1.rearrange("(c p) e -> p c e", p=P)), (gw2[:], gc_w2),
            (gw3_col[:], gc_w3), (gb1[:], column(gc_b1)),
            (gb2[:], gc_b2.rearrange("(p c) -> p c", c=1)), (gb3[:], row_on_all(gc_b3)),
            (arange[:], row_on_all(adaptive_range)),
        ]
        loads_d = [
            (u1_sb[:, :, 0:RANK], u1.rearrange("(c p) r -> p c r", p=P)),
            (u1_sb[:, :, RANK:2 * RANK], u1.rearrange("(c p) r -> p c r", p=P)),
            (v1_sb[0:RANK], v1.rearrange("r (c f) -> r c f", f=P)),
            (v1_sb[RANK:2 * RANK], v1.rearrange("r (c f) -> r c f", f=P)),
            (b1_col[:], column(b1)), (u2_sb[:], u2.rearrange("(c p) r -> p c r", p=P)),
            (v2_sb[0:RANK, :], v2), (v2_sb[RANK:2 * RANK, :], v2),
        ]
        weight_turns = ([(wsrc_raw, o, f, wsrcT) for f in range(FK) for o in range(FK)]
                        + [(wtgt_raw, o, f, wtgtT) for f in range(DK) for o in range(DK)]
                        + [(wout_raw, o, f, woutT) for f in range(2 * DK) for o in range(DK)])
        WT_BANKS = len(weight_turns) // 4
        WT_HALVES = (range(WT_BANKS // 2), range(WT_BANKS // 2, WT_BANKS))

        def scores_free(eng, b, hg):
            n = QH // 2 * (2 * b + hg)
            need(eng, c_pT_act, n)
            need(eng, c_pT_dve, n)

        block = whole.enter_context(nc.Block())

        @block.sync
        def _(sp):
            sp.dma_start(lens_i[:], lens).then_inc(s_lens, 16)
            for dst, src in loads_a:
                sp.dma_start(dst, src, allow_slow_non_contiguous=True).then_inc(s_wa, 16)
            sp.dma_start(a_ctx[0][:], ctx_dram[0]).then_inc(a_ctx_in[0], 16)
            sp.dma_start(a_ctx[1][:], ctx_dram[1]).then_inc(a_ctx_in[1], 16)

            def load_x(q):
                return sp.dma_start(
                    x_sb[:, q * TILES // 4:(q + 1) * TILES // 4, :].rearrange("p (b k) d -> p b k d", k=TS),
                    x_dram[q * B // 4:(q + 1) * B // 4].rearrange("b p k d -> p b k d"))

            load_x(0).then_inc(s_x0_in, 16)
            for q in range(1, 4):
                load_x(q).then_inc(s_x_in, 16)

            def stream_a(b, s):
                need(sp, a_u_ok, b - 1)
                need(sp, a_ssqd, b - 1)
                sp.dma_start(a_ctx[s][:], ctx_dram[b]).then_inc(a_ctx_in[s], 16)

            sp.wait_ge(s_winT_ps, 1)
            sp.wait_ge(s_patch, B)
            parts = ([(s_wb, loads_b[i:i + 3]) for i in range(0, len(loads_b), 3)]
                     + [(s_wc, loads_c[0:1]), (s_wc, loads_c[1:3]), (s_wc, loads_c[3:6]), (s_wc, loads_c[6:])])
            for b in range(2, B):
                stream_a(b, b % 2)
                done, part = parts[b - 4] if 4 <= b < 4 + len(parts) else (s_wb, ())
                for dst, src in part:
                    sp.dma_start(dst, src, allow_slow_non_contiguous=True).then_inc(done, 16)
            for dst, src in loads_d:
                sp.dma_start(dst, src, allow_slow_non_contiguous=True).then_inc(s_wd, 16)

            sp.wait_ge(b_o_ok, 1)

            def stream_c(b, s):
                need(sp, c_ctxT_ps, 2 * (b - 1))
                sp.dma_start(c_ctx[s][:], ctx_dram[b]).then_inc(c_ctx_in[s], 16)

            def stack_c(b, s):
                if isinstance(b, int) and b == 1:
                    sp.wait_ge(b_nstat, NG)
                need_alone(sp, c_k_split, 2 * b + 2, s_passed)
                need_alone(sp, c_qlo_ok, b + 1, s_passed)
                need_alone(sp, c_s_ps, 2 * (b - 1), s_passed)
                for c, (first, step) in enumerate(((Q_HI, K_HI - Q_HI), (Q_LO, K_HI - Q_LO), (Q_HI, K_LO - Q_HI))):
                    for j in range(QH):
                        sp.dma_start(
                            c_stack[s][c * HD:(c + 1) * HD, :, j, :, :].rearrange("p a g t -> p a (g t)").bitcast(F32),
                            c_parts[j * HD:(j + 1) * HD, first:first + step + 1:step, :, :]
                            .rearrange("p a g t -> p a (g t)").bitcast(F32)).then_inc(c_stack_in, 16)

            def body_stack(b, s):
                stack_c(b, s)
                if not beyond(b + 2, B):
                    stream_c(b + 2, s)

            stream_c(0, 0)
            stream_c(1, 1)
            over_pairs(sp, B, body_stack)

            def store(n, s):
                need(sp, d_y_ok, 2 * (n + 1))
                sp.dma_start(out_dram[n], x_sb[:, bass.ds(GT * n, GT), :]
                             .rearrange("p (c k) d -> p c k d", k=TS)).then_inc(d_stored, 16)

            over_pairs(sp, NG, store)
            sp.wait_ge(d_stored, 16 * NG)

        @block.gpsimd
        def _(pool):
            nc.gpsimd.memset(ident[:], 0.0).then_inc(s_zero, 1)
            pool.wait_ge(s_zero, 1)
            nc.gpsimd.affine_select(out=ident[:], in_=ident[:], compare_op=ALU.not_equal, fill=1.0,
                                    base=0, pattern=[[-1, P]], channel_multiplier=1).then_inc(s_const, 1)
            nc.gpsimd.iota(iota_row[:], pattern=[[1, S]], base=0, channel_multiplier=0,
                           allow_small_or_imprecise_dtypes=True).then_inc(s_const, 1)
            nc.gpsimd.iota(q1_col[:], pattern=[[P, TS]], base=1, channel_multiplier=1,
                           allow_small_or_imprecise_dtypes=True).then_inc(s_const, 1)
            nc.gpsimd.memset(lag_floor[:], -1.0).then_inc(s_zero, 1)
            pool.wait_ge(s_zero, 2)
            nc.gpsimd.memset(lag_floor[0:1, 0:1], 0.0).then_inc(s_const, 1)
            nc.gpsimd.memset(neg_half[:], -0.5).then_inc(s_const, 1)
            pool.wait_ge(s_const, 5)

            def next_stats(b, s, tiles, mv, tmp, nstat, npre, nnext, count):
                need_alone(pool, nstat, count, s_passed)
                nc.gpsimd.tensor_scalar(tmp[:], mv[:, :, 1], LN_EPS, None, ALU.add).then_inc(npre, 1)
                nc.gpsimd.tensor_copy(mu[:, bass.ds(tiles * b, tiles)], mv[:, :, 0]).then_inc(nnext, 1)
                need(pool, npre, count)
                nc.gpsimd.tensor_tensor(rstd[:, bass.ds(tiles * b, tiles)], tmp[:],
                                        neg_half[:, 0:tiles], ALU.pow).then_inc(nnext, 1)

            def scales_a(b, s):
                need(pool, a_stat, b + 1)
                need(pool, a_xs_ok, b - 1)
                need_alone(pool, a_u_ok, b - 1, s_passed)
                nc.gpsimd.tensor_scalar(a_tmp[s][:, 0:TS], a_mv[s][:, :, 1], 1.0 + RMS_EPS,
                                        RMS_EPS * LN_EPS, ALU.mult, ALU.add).then_inc(a_pre, 1)
                need_alone(pool, a_ssqd, b + 1, s_passed)
                nc.gpsimd.tensor_scalar(a_tmp[s][:, TS:2 * TS], a_ssq[s][:], 1.0 / DC, RMS_EPS,
                                        ALU.mult, ALU.add).then_inc(a_pre, 1)
                need(pool, a_pre, 2 * b + 2)
                nc.gpsimd.tensor_tensor(a_scl[s][:], a_tmp[s][:], neg_half[:], ALU.pow).then_inc(a_scale, 1)

            def bias_a(b):
                need(pool, a_xs_ok, b + 1)
                xb = x_sb[:, bass.ds(TS * b, TS), :]
                nc.gpsimd.tensor_tensor(xb, xb, bin_b[:].unsqueeze(1).to_broadcast([P, TS, D]),
                                        ALU.add).then_inc(a_xb, 1)

            pool.wait_ge(s_scaled, 3)
            scales_a(0, 0)
            scales_a(1, 1)
            bias_a(0)

            def body_a(b, s):
                if not beyond(b + 2, B):
                    scales_a(b + 2, s)
                if not is_first(b):
                    next_stats(b - 1, 1 - s, TS, n_mv[1 - s], n_tmp[1 - s], a_nstat, a_npre, a_next, b)
                if not is_last(b, B):
                    bias_a(b + 1)

            over_pairs(pool, B, body_a)
            next_stats(B - 1, 1, TS, n_mv[1], n_tmp[1], a_nstat, a_npre, a_next, B)

            def stats_b(n):
                next_stats(n, n % LANES, GT, b_mv[n % LANES], b_tmp[n % LANES], b_nstat, b_npre, b_next, n + 1)

            for n in range(NG - 2):
                stats_b(n)

            def bias_c(b):
                need(pool, c_xn_ok, b + 1)
                xb = x_sb[:, bass.ds(TS * b, TS), :]
                nc.gpsimd.tensor_tensor(xb, xb, bout_b[:].unsqueeze(1).to_broadcast([P, TS, D]),
                                        ALU.add).then_inc(c_xb, 1)

            def split_k(b):
                need_alone(pool, c_k_ok, b + 1, s_passed)
                need_alone(pool, c_stack_in, 16 * STACK_DMAS * b, s_passed)
                nc.gpsimd.tensor_copy(c_parts[:, K_HI, :, :], c_kT[:]).then_inc(c_k_split, 1)
                need(pool, c_k_split, 2 * b + 1)
                nc.gpsimd.tensor_tensor(c_parts[:, K_LO, :, :], c_kT[:], c_parts[:, K_HI, :, :].bitcast(F32),
                                        ALU.subtract).then_inc(c_k_split, 1)

            def split_q(b):
                need(pool, c_qhi_ok, b + 1)
                nc.gpsimd.tensor_tensor(c_parts[:, Q_LO, :, :], c_qT[:], c_parts[:, Q_HI, :, :].bitcast(F32),
                                        ALU.subtract).then_inc(c_qlo_ok, 1)

            def body_c(b, s):
                if not is_last(b, B):
                    split_k(b + 1)
                    split_q(b + 1)
                    bias_c(b + 1)
                if not is_first(b):
                    next_stats(b - 1, 1 - s, TS, n_mv[1 - s], n_tmp[1 - s], c_nstat, c_npre, c_next, b)

            split_q(0)
            split_k(0)
            bias_c(0)
            stats_b(NG - 2)
            stats_b(NG - 1)
            over_pairs(pool, B, body_c)
            next_stats(B - 1, 1, TS, n_mv[1], n_tmp[1], c_nstat, c_npre, c_next, B)

            def bias_d(n, s):
                need(pool, d_xn_ok, n + 1)
                xb = x_sb[:, bass.ds(GT * n, GT), :]
                nc.gpsimd.tensor_tensor(xb, xb, b2_b[:].unsqueeze(1).to_broadcast([P, GT, D]),
                                        ALU.add).then_inc(d_xb, 1)

            over_pairs(pool, NG, bias_d)

        @block.scalar
        def _(act):
            def ends(b, s):
                need(act, s_cnt, b + 1)
                need(act, s_patch, b - 1)
                nc.scalar.activation(bmask[s][:], bank[2 + s][:, 0:S], ACT.Sign).then_inc(s_end, 1)

            over_pairs(act, B, ends)

            act.wait_ge(s_wa, 16 * len(loads_a))
            nc.scalar.activation(gates[:], gates_raw[:], ACT.Tanh).then_inc(s_gate, 1)
            act.wait_ge(s_winT_ps, 1)
            for c in range(DK):
                op = nc.scalar.activation(winT[:, c, :], bank[6][:, c * D:(c + 1) * D], ACT.Copy,
                                          scale=gres_col[:, c:c + 1])
            op.then_inc(s_winT, 1)

            def weights_turned(half):
                for t in WT_HALVES[half]:
                    raw, _, f, turned = weight_turns[4 * t]
                    act.wait_ge(s_wT_ps, t + 1)
                    rows = 512 // turned.shape[2]
                    nc.scalar.copy(turned[:, f:f + rows, :],
                                   bank[4 + t % 2][:].rearrange("p (f o) -> p f o", f=rows)).then_inc(s_wT, 1)

            def decays_a(b, s):
                need(act, a_ctx_in[s], 8 * (b - s) + 16)
                need(act, a_scale, b - 1)
                for k in range(TS):
                    op = nc.scalar.activation(a_junk[s][k][:], a_ctx[s][:, k, :], ACT.Square,
                                              accum_out=a_ssq[s][:, k:k + 1])
                op.then_inc(a_ssqd, 1)
                need(act, a_z_ok, b + 1)
                need(act, a_mT_ok, b - 1)
                nc.scalar.activation(a_e[s][:], a_z[s][:], ACT.Exp, scale=-DT).then_inc(a_e_ok, 1)

            def turned_a(b, s):
                need(act, a_xsT_ps, b + 1)
                need(act, a_out_ps, b - 1)
                nc.scalar.copy(a_xsT[s][:].rearrange("p c t -> p (c t)"), bank[s][:]).then_inc(a_xsT_ok, 1)

            def body_a(b, s):
                if not beyond(b + 2, B):
                    decays_a(b + 2, s)
                if not is_last(b, B):
                    turned_a(b + 1, 1 - s)
                if isinstance(b, int) and b >= B - 2:
                    weights_turned(b - (B - 2))

            decays_a(0, 0)
            decays_a(1, 1)
            turned_a(0, 0)
            over_pairs(act, B, body_a)

            act.wait_ge(a_out_ps, B)
            act.wait_ge(s_wb, 16 * len(loads_b))

            def layer_b(layer, slot):
                m = item_at(slot)
                if m is None:
                    return
                g, u = m % LANES, m % 2
                act.wait_ge(b_ps[layer - 1], m + 1)
                if layer == 1:
                    for c in range(DK):
                        op = nc.scalar.activation(b_h1[g][:, c, :], bank[2 * g + c][:], ACT.Gelu,
                                                  bias=cb1[:, c:c + 1])
                elif layer == 2:
                    op = nc.scalar.activation(b_h2[u][:], bank[2 * g][:], ACT.Gelu, bias=cb2[:])
                elif layer == 3:
                    op = nc.scalar.activation(b_h3[u][:], bank[2 * g + 1][0:D // 4, :], ACT.Gelu, bias=cb3[:])
                else:
                    need(act, b_upd, m - 1)
                    op = nc.scalar.activation(b_tt[u][:], bank[2 * g][:], ACT.Tanh, bias=cb4[:], scale=0.5)
                op.then_inc(b_ok[layer - 1], 1)

            def turned_b(n):
                g = n % LANES
                act.wait_ge(b_xT_ps, n + 1)
                for c in range(DK):
                    for q in range(2):
                        op = nc.scalar.activation(
                            b_o[g][:, c, q * S:(q + 1) * S], bank[2 * g + c][:, q * S:(q + 1) * S],
                            ACT.Copy, accum_out=b_sum[:, c, 2 * g + q:2 * g + q + 1])
                op.then_inc(b_o_ok, 1)

            def globals_b(slot):
                work = globals_at(slot)
                if not work:
                    return
                src = bank[2 * (item_at(slot - 1) % LANES) + 1]
                act.wait_ge(b_gps, global_slots_before(slot) + 1)
                for n, layer in work:
                    two = slice(2 * (n % LANES), 2 * (n % LANES) + 2)
                    ps = slice(GCOL * layer, GCOL * layer + 2)
                    if layer == 0:
                        op = nc.scalar.activation(b_g1[:, two], src[:, ps], ACT.Gelu, bias=gb1[:], scale=1.0 / S)
                    elif layer == 1:
                        op = nc.scalar.activation(b_g2[:, two], src[0:D // 4, ps], ACT.Gelu, bias=gb2[:])
                    else:
                        op = nc.scalar.activation(b_gt[:, two], src[:, ps], ACT.Tanh, bias=gb3[:], scale=0.5)
                op.then_inc(b_gok, 1)

            act.wait_ge(s_vconst, 8)
            for n in range(LANES):
                turned_b(n)

            def slot_b(slot):
                layer_b(4, slot - 3)
                layer_b(3, slot - 2)
                for n in range(LANES, NG):
                    if slot == first_slot(n):
                        turned_b(n)
                layer_b(2, slot - 1)
                globals_b(slot)
                layer_b(1, slot)

            for slot in range(SLOTS - 2):
                slot_b(slot)

            act.wait_ge(s_wc, 16 * len(loads_c))

            def ctxT_c(b, s, h, src=4):
                need(act, c_ctxT_ps, 2 * b + 2 - h)
                need(act, c_v_ps, b - 1)
                nc.scalar.copy(c_ctxT[s][:, 2 * h:2 * h + 2, :].rearrange("p c t -> p (c t)"),
                               bank[src + h][:]).then_inc(c_ctxT_ok, 1)

            def high_q(b):
                need(act, c_q_ok, b + 1)
                need(act, c_stack_in, 16 * STACK_DMAS * b)
                nc.scalar.copy(c_parts[:, Q_HI, :, :], c_qT[:]).then_inc(c_qhi_ok, 1)

            def xnTq_c(b, src=5):
                need(act, c_xnT_ps, b + 1)
                need(act, c_q_ps, b)
                need(act, c_xnT_ok, b)
                nc.scalar.copy(c_xnTq[:].rearrange("p c t -> p (c t)"), bank[src][:]).then_inc(c_xnTq_ok, 1)

            def xnT_c(b, s):
                need(act, c_xnTq_ok, b + 1)
                need(act, c_out_ps, b - 1)
                nc.scalar.copy(c_xnT[s][:], c_xnTq[:]).then_inc(c_xnT_ok, 1)

            def exps_c(b, hg, tc):
                n = 2 * b + hg
                need(act, c_s_ok, TS * n + tc + 1)
                need(act, c_pT_ps, QH * (n - 1))
                for j in range(QH):
                    op = nc.scalar.activation(c_p[hg][:, tc, j, :], c_s[hg][:, tc, j, :], ACT.Exp,
                                              bias=c_nmx[hg][:, tc, j:j + 1], scale=SCALE,
                                              accum_out=c_sum[hg][:, tc, j:j + 1])
                op.then_inc(c_p_ok, 1)

            def probsT_c(b, hg):
                n = 2 * b + hg
                for j in range(0, QH, 2):
                    need(act, c_pT_ps, QH * n + j + 1)
                    need(act, c_up_ps, n - 1)
                    nc.scalar.copy(c_pT[hg][:, j, :], bank[j][:]).then_inc(c_pT_act, 1)

            def update_c(b, s, hg):
                need(act, c_up_ps, 2 * b + hg + 1)
                need(act, c_out_ps, b - 1)
                nc.scalar.copy(c_upT[s][:, hg, :], bank[6][:, hg * S:(hg + 1) * S]).then_inc(c_up_ok, 1)

            def xnT_d(n, s):
                need(act, d_xT_ps, n + 1)
                need(act, d_p_ps, n - 1)
                for c in range(DK):
                    op = nc.scalar.copy(d_xnT[s][:, c, :], bank[4 + c][:])
                op.then_inc(d_xT_ok, 1)

            def body_c(b, s):
                last, first, ahead = is_last(b, B), is_first(b), not beyond(b + 2, B)
                exps_c(b, 0, 0)
                exps_c(b, 0, 1)
                if not first:
                    probsT_c(b - 1, 1)
                if not last:
                    high_q(b + 1)
                if ahead:
                    ctxT_c(b + 2, s, 1)
                if not first:
                    update_c(b - 1, 1 - s, 1)
                if last:
                    xnT_d(0, 0)
                exps_c(b, 1, 0)
                if not last:
                    xnT_c(b + 1, 1 - s)
                probsT_c(b, 0)
                if ahead:
                    xnTq_c(b + 2)
                    ctxT_c(b + 2, s, 0)
                update_c(b, s, 0)
                exps_c(b, 1, 1)

            ctxT_c(0, 0, 1, 0)
            ctxT_c(0, 0, 0, 0)
            xnTq_c(0, 2)
            high_q(0)
            slot_b(SLOTS - 2)
            ctxT_c(1, 1, 1, 2)
            act.wait_ge(b_nstat, NG)
            xnT_c(0, 0)
            ctxT_c(1, 1, 0, 2)
            xnTq_c(1, 0)
            over_pairs(act, B, body_c)
            probsT_c(B - 1, 1)
            update_c(B - 1, 1, 1)

            act.wait_ge(s_wd, 16 * len(loads_d))
            def hidden_d(n, j):
                m = 4 * n + j
                need(act, d_h_ps, m + 1)
                need(act, d_q_ps, m - 1)
                for e in range(2):
                    op = nc.scalar.activation(d_h[j % 2][:, e, :], bank[2 * (j % 2) + e][:],
                                              ACT.Gelu_apprx_tanh, bias=b1_col[:, 2 * j + e:2 * j + e + 1])
                op.then_inc(d_h_ok, 1)

            def body_d(n, s):
                hidden_d(n, 0)
                hidden_d(n, 1)
                if not is_last(n, NG):
                    xnT_d(n + 1, 1 - s)
                hidden_d(n, 2)
                hidden_d(n, 3)

            over_pairs(act, NG, body_d)

        @block.tensor
        def _(pe):
            mm = nc.tensor.matmul
            pe.wait_ge(s_const, 5)
            pe.wait_ge(s_bchain, 4)
            for k in range(TS):
                op = nc.tensor.transpose(bank[0][:, k * B:(k + 1) * B], bound[:, k * P:(k + 1) * P],
                                         ident[0:B, 0:B])
            op.then_inc(s_boundT_ps, 1)

            def count(b, s):
                need(pe, s_hit, b + 1)
                need(pe, s_end, b - 1)
                for k in range(TS):
                    op = mm(bank[2 + s][:, 0:S], ones_bf[:], hit[s][k][:], start=k == 0, stop=k == TS - 1)
                op.then_inc(s_cnt, 1)

            over_pairs(pe, B, count)

            pe.wait_ge(s_wa, 16 * len(loads_a))
            for c in range(DK):
                for o in range(DK):
                    op = nc.tensor.transpose(bank[6][:, c * D + o * P:c * D + (o + 1) * P],
                                             win_raw[:, o, c * P:(c + 1) * P], ident[:])
            op.then_inc(s_winT_ps, 1)

            def turn_weights(half):
                pe.wait_ge(s_wc, 16 * len(loads_c))
                for t in WT_HALVES[half]:
                    need(pe, s_wT, t - 1)
                    for q in range(4):
                        raw, o, f, _ = weight_turns[4 * t + q]
                        op = nc.tensor.transpose(bank[4 + t % 2][:, q * P:(q + 1) * P],
                                                 raw[:, o, f * P:(f + 1) * P], ident[:])
                    op.then_inc(s_wT_ps, 1)

            pe.wait_ge(s_boundT, 1)
            pe.wait_ge(s_winT, 1)

            def turn_a(b, s):
                need(pe, a_xs_ok, b + 1)
                need(pe, a_xsT_ok, b - 1)
                for c in range(DK):
                    for k in range(TS):
                        op = nc.tensor.transpose(bank[s][:, c * S + k * P:c * S + (k + 1) * P],
                                                 a_xs[s][:, k, c * P:(c + 1) * P], ident[:])
                op.then_inc(a_xsT_ps, 1)

            def mix_a(b, s):
                need(pe, a_xsT_ok, b + 1)
                need(pe, a_u_ok, b + 1)
                need(pe, a_mT_ok, b + 1)
                need(pe, a_x1, b - 1)
                for k in range(TS):
                    dst = bank[2 + s][:, k * D:(k + 1) * D]
                    for c in range(DK):
                        mm(dst, a_xsT[s][:, c, k * P:(k + 1) * P], winT[:, c, :], start=c == 0, stop=False)
                    for q in range(TS):
                        op = mm(dst, a_mT[s][:, q, k * P:(k + 1) * P], a_u[s][:, q, :],
                                start=False, stop=q == TS - 1)
                op.then_inc(a_out_ps, 1)

            def body_a(b, s):
                if not is_last(b, B):
                    turn_a(b + 1, 1 - s)
                mix_a(b, s)
                if isinstance(b, int) and b >= B - 2:
                    turn_weights(b - (B - 2))

            turn_a(0, 0)
            over_pairs(pe, B, body_a)

            pe.wait_ge(a_xsT_ok, B)

            def layer_b(layer, slot):
                m = item_at(slot)
                if m is None:
                    return
                g, u = m % LANES, m % 2
                lo, hi = bank[2 * g], bank[2 * g + 1]
                if layer == 1:
                    if m % ROUND < LANES:
                        pe.wait_ge(b_o_ok, group_of(m) + 1)
                    else:
                        pe.wait_ge(b_upd, m - LANES + 1)
                    for h in range(DK):
                        for c in range(DK):
                            op = mm((lo, hi)[h][:], cw1[:, c, h * P:(h + 1) * P], b_o[g][:, c, :],
                                    start=c == 0, stop=c == DK - 1)
                elif layer == 2:
                    pe.wait_ge(b_ok[0], m + 1)
                    for c in range(DK):
                        op = mm(lo[:], cw2[:, c, :], b_h1[g][:, c, :], start=c == 0, stop=c == DK - 1)
                elif layer == 3:
                    pe.wait_ge(b_ok[1], m + 1)
                    need(pe, b_gok, global_slots_before(slot + 2))
                    op = mm(hi[0:D // 4, :], cw3[:], b_h2[u][:], start=True, stop=True)
                else:
                    pe.wait_ge(b_ok[2], m + 1)
                    op = mm(lo[:], cw4[:], b_h3[u][:], start=True, stop=True)
                op.then_inc(b_ps[layer - 1], 1)

            def globals_b(slot):
                work = globals_at(slot)
                if not work:
                    return
                dst = bank[2 * (item_at(slot - 1) % LANES) + 1]
                need(pe, b_gok, global_slots_before(slot))
                for n, layer in work:
                    two = slice(2 * (n % LANES), 2 * (n % LANES) + 2)
                    ps = slice(GCOL * layer, GCOL * layer + 2)
                    if layer == 0:
                        for c in range(DK):
                            op = mm(dst[:, ps], gw1[:, c, :], b_sum[:, c, two], start=c == 0, stop=c == DK - 1)
                    elif layer == 1:
                        op = mm(dst[0:D // 4, ps], gw2[:], b_g1[:, two], start=True, stop=True)
                    else:
                        op = mm(dst[:, ps], gw3[:], b_g2[:, two], start=True, stop=True)
                op.then_inc(b_gps, 1)

            def turn_b(n):
                g = n % LANES
                pe.wait_ge(b_xn_ok, n + 1)
                need(pe, b_x2, n - LANES + 1)
                for c in range(DK):
                    for k in range(GT):
                        op = nc.tensor.transpose(bank[2 * g + c][:, k * P:(k + 1) * P],
                                                 b_xn[g][:, k, c * P:(c + 1) * P], ident[:])
                op.then_inc(b_xT_ps, 1)

            def back_b(n):
                g = n % LANES
                pe.wait_ge(b_upd, n // LANES * ROUND + ROUND - LANES + g + 1)
                for k in range(GT):
                    for c in range(DK):
                        op = nc.tensor.transpose(
                            bank[2 * g + k // 2][:, (k % 2) * D + c * P:(k % 2) * D + (c + 1) * P],
                            b_o[g][:, c, k * P:(k + 1) * P], ident[:])
                op.then_inc(b_back, 1)

            def slot_b(slot):
                layer_b(4, slot - 3)
                for n in range(LANES, NG):
                    if slot == first_slot(n):
                        turn_b(n)
                layer_b(3, slot - 2)
                for n in range(NG):
                    if slot == first_slot(n) + ROUND:
                        back_b(n)
                layer_b(2, slot - 1)
                globals_b(slot)
                layer_b(1, slot)

            turn_b(0)
            pe.wait_ge(s_wT, WT_BANKS)
            pe.wait_ge(s_wb, 16 * len(loads_b))
            pe.wait_ge(s_vconst, 8)
            pe.wait_ge(a_x1, B)
            for n in range(1, LANES):
                turn_b(n)
            for slot in range(SLOTS - 2):
                slot_b(slot)


            def ctxT_c(b, s, h, dst=4):
                need(pe, c_ctx_in[s], 8 * (b - s) + 16)
                need(pe, (c_vraw, c_q_ok)[h], b)
                for c in range(2):
                    for k in range(TS):
                        f = 2 * h + c
                        op = nc.tensor.transpose(bank[dst + h][:, c * S + k * P:c * S + (k + 1) * P],
                                                 c_ctx[s][:, k, f * P:(f + 1) * P], ident[:])
                op.then_inc(c_ctxT_ps, 1)

            def k_c(b, s, dst=4):
                need(pe, c_ctxT_ok, 2 * b + 2)
                for m in range(DK):
                    for f in range(FK):
                        op = mm(bank[dst][:, m * S:(m + 1) * S], wsrcT[:, f, m * P:(m + 1) * P],
                                c_ctxT[s][:, f, :], start=f == 0, stop=f == FK - 1)
                op.then_inc(c_k_ps, 1)

            def xnT_c(b, s, dst=5):
                need(pe, c_xn_ok, b + 1)
                need(pe, c_ctxT_ok, 2 * b + 1)
                for c in range(DK):
                    for k in range(TS):
                        op = nc.tensor.transpose(bank[dst][:, c * S + k * P:c * S + (k + 1) * P],
                                                 c_xn[s][:, k, c * P:(c + 1) * P], ident[:])
                op.then_inc(c_xnT_ps, 1)

            def v_c(b, s, first_part, last_part, dst=4):
                if first_part == 0:
                    need(pe, c_k_ok, b + 1)
                for part in range(first_part, last_part):
                    k, f = divmod(part, FK)
                    op = mm(bank[dst][:, k * D:(k + 1) * D], c_ctxT[s][:, f, k * P:(k + 1) * P],
                            wsrcT[:, f, D:2 * D], start=f == 0, stop=f == FK - 1)
                if last_part == TS * FK:
                    op.then_inc(c_v_ps, 1)

            def q_c(b, s, dst=5):
                need(pe, c_xnTq_ok, b + 1)
                for m in range(DK):
                    for c in range(DK):
                        op = mm(bank[dst][:, m * S:(m + 1) * S], wtgtT[:, c, m * P:(m + 1) * P],
                                c_xnTq[:, c, :], start=c == 0, stop=c == DK - 1)
                op.then_inc(c_q_ps, 1)

            def scores_c(b, s, hg):
                need(pe, c_stack_in, 16 * STACK_DMAS * (b + 1))
                scores_free(pe, b, hg - 1)
                need(pe, c_s_ok, TS * (2 * b + hg))
                for tc in range(TS):
                    for j in range(QH):
                        op = mm(bank[j][:, tc * S:(tc + 1) * S], c_stack[s][:, 0, j, hg, tc * P:(tc + 1) * P],
                                c_stack[s][:, 1, j, hg, :], start=True, stop=True)
                op.then_inc(c_s_ps, 1)

            def probsT_c(b, hg):
                need(pe, c_pn_ok, 2 * b + hg + 1)
                n = 2 * b + hg + 2
                need(pe, c_s_ok, TS * (min(n, 2 * B) if isinstance(n, int) else n))
                for j in range(QH):
                    for q in range(TS):
                        for tc in range(TS):
                            op = nc.tensor.transpose(
                                bank[j][:, q * S + tc * P:q * S + (tc + 1) * P],
                                c_p[hg][:, tc, j, q * P:(q + 1) * P], ident[:])
                    op.then_inc(c_pT_ps, 1)

            def update_c(b, s, hg):
                scores_free(pe, b, hg + 1)
                need(pe, c_v_ok, b + 1)
                need(pe, c_up_ok, 2 * b + hg)
                for q in range(TS):
                    for j in range(QH):
                        h = QH * hg + j
                        op = mm(bank[6][j * HD:(j + 1) * HD, hg * S:(hg + 1) * S],
                                c_v[s][:, q, h * HD:(h + 1) * HD], c_pT[hg][:, j, q * S:(q + 1) * S],
                                start=q == 0, stop=q == TS - 1)
                op.then_inc(c_up_ps, 1)

            def out_part(s, k, f):
                src = c_xnT[s][:, f, :] if f < DK else c_upT[s][:, f - DK, :]
                return mm(bank[7][:, k * D:(k + 1) * D], src[:, k * P:(k + 1) * P], woutT[:, f, :],
                          start=f == 0, stop=f == 2 * DK - 1)

            def out_begin(b, s):
                need(pe, c_xnT_ok, b + 1)
                need(pe, c_x3, b)
                for f in range(DK):
                    out_part(s, 0, f)

            def out_c(b, s):
                need(pe, c_up_ok, 2 * b + 2)
                for k in range(TS):
                    for f in range(DK if k == 0 else 0, 2 * DK):
                        op = out_part(s, k, f)
                op.then_inc(c_out_ps, 1)

            def xnT_d(n, s):
                need(pe, d_xn_ok, n + 1)
                need(pe, d_p_ok, n)
                for c in range(DK):
                    for k in range(GT):
                        op = nc.tensor.transpose(bank[4 + c][:, k * P:(k + 1) * P],
                                                 d_xn[s][:, k, c * P:(c + 1) * P], ident[:])
                op.then_inc(d_xT_ps, 1)

            def lowrank_d(n, s):
                if is_first(n):
                    pe.wait_ge(s_wd, 16 * len(loads_d))
                need(pe, d_xT_ok, n + 1)
                for c in range(DK):
                    op = mm(bank[4][:], u1_sb[:, c, :], d_xnT[s][:, c, :], start=c == 0, stop=c == DK - 1)
                op.then_inc(d_p_ps, 1)

            def body_c(b, s):
                last, first, ahead = is_last(b, B), is_first(b), not beyond(b + 2, B)
                if not last:
                    k_c(b + 1, 1 - s)
                scores_c(b, s, 0)
                if last:
                    pe.wait_ge(c_q_ok, B)
                    pe.wait_ge(c_vraw, B)
                    xnT_d(0, 0)
                if not last:
                    q_c(b + 1, 1 - s)
                    v_c(b + 1, 1 - s, 0, V_EARLY)
                if not first:
                    probsT_c(b - 1, 1)
                if ahead:
                    ctxT_c(b + 2, s, 1)
                if not first:
                    out_begin(b - 1, 1 - s)
                    update_c(b - 1, 1 - s, 1)
                scores_c(b, s, 1)
                if not first:
                    out_c(b - 1, 1 - s)
                if not last:
                    v_c(b + 1, 1 - s, V_EARLY, TS * FK)
                if last:
                    lowrank_d(0, 0)
                probsT_c(b, 0)
                if ahead:
                    xnT_c(b + 2, s)
                    ctxT_c(b + 2, s, 0)
                update_c(b, s, 0)

            pe.wait_ge(b_x2, LANES + 1)
            ctxT_c(0, 0, 1, 0)
            ctxT_c(0, 0, 0, 0)
            pe.wait_ge(b_x2, LANES + 2)
            xnT_c(0, 0, 2)
            q_c(0, 0, 3)
            slot_b(SLOTS - 2)
            k_c(0, 0, 0)
            slot_b(SLOTS - 1)
            pe.wait_ge(c_ctxT_ok, 2)
            for part in range(TS * FK):
                k, f = divmod(part, FK)
                op = mm(bank[1][:, k * D:(k + 1) * D], c_ctxT[0][:, f, k * P:(k + 1) * P],
                        wsrcT[:, f, D:2 * D], start=f == 0, stop=f == FK - 1)
            op.then_inc(c_v_ps, 1)
            ctxT_c(1, 1, 1, 2)
            ctxT_c(1, 1, 0, 2)
            xnT_c(1, 1, 0)
            pe.wait_ge(b_x2, NG)
            pe.wait_ge(c_xnTq_ok, 2)
            over_pairs(pe, B, body_c)
            probsT_c(B - 1, 1)
            out_begin(B - 1, 1)
            update_c(B - 1, 1, 1)
            out_c(B - 1, 1)

            scores_free(pe, B, 0)
            pe.wait_ge(c_x3, B)

            def hidden_d(n, s, j):
                need(pe, d_p_ok, n + 1)
                need(pe, d_h_ok, 4 * n + j - 1)
                for e in range(2):
                    mm(bank[2 * (j % 2) + e][:], v1_hi[:, 2 * j + e, :], d_pT[s][:], start=True, stop=False)
                    op = mm(bank[2 * (j % 2) + e][:], v1_lo[:, 2 * j + e, :], d_pT[s][:], start=False, stop=True)
                op.then_inc(d_h_ps, 1)

            def second_d(n, s, j):
                need(pe, d_h_ok, 4 * n + j + 1)
                need(pe, d_q_ok, n)
                for e in range(2):
                    op = mm(bank[6][e * RANK:(e + 1) * RANK, :], u2_sb[:, 2 * j + e, :],
                            d_h[j % 2][:, e, :], start=j == 0, stop=j == 3)
                op.then_inc(d_q_ps, 1)

            def out_d(n, s, half):
                need(pe, d_q_ok, n + 1)
                need(pe, d_y_ok, 2 * n + half)
                for k in range(2):
                    t = 2 * half + k
                    op = mm(bank[7][:, k * D:(k + 1) * D], d_qT[s][:, t * P:(t + 1) * P], v2_sb[:],
                            start=True, stop=True)
                op.then_inc(d_y_ps, 1)

            def body_d(n, s):
                first, last = is_first(n), is_last(n, NG)
                hidden_d(n, s, 0)
                hidden_d(n, s, 1)
                if not last:
                    xnT_d(n + 1, 1 - s)
                if not first:
                    out_d(n - 1, 1 - s, 0)
                second_d(n, s, 0)
                hidden_d(n, s, 2)
                second_d(n, s, 1)
                hidden_d(n, s, 3)
                if not last:
                    lowrank_d(n + 1, 1 - s)
                if not first:
                    out_d(n - 1, 1 - s, 1)
                second_d(n, s, 2)
                second_d(n, s, 3)

            pe.wait_ge(s_v1, 2)
            over_pairs(pe, NG, body_d)
            out_d(NG - 1, 1, 0)
            out_d(NG - 1, 1, 1)

        @block.vector
        def _(dve):
            v = nc.vector

            v.memset(ones_row[:], 1.0).then_inc(s_bchain, 1)
            v.memset(ones_full[:], 1.0)
            v.memset(ones_bf[:], 1.0)
            v.memset(sgn[0:P // 2, :], 1.0)
            v.memset(sgn[P // 2:P, :], -1.0).then_inc(s_vconst, 1)
            dve.wait_ge(s_lens, 16)
            v.tensor_copy(lens_f[:], lens_i[:]).then_inc(s_bchain, 1)
            dve.wait_ge(s_bchain, 2)
            v.tensor_tensor_scan(bound[:], ones_row[:], lens_f[:], -1.0, ALU.mult, ALU.add).then_inc(s_bchain, 1)
            dve.wait_ge(s_bchain, 3)
            v.tensor_scalar(wrap[:], bound[:], 0.0, float(S), ALU.is_lt, ALU.mult).then_inc(s_vconst, 1)
            dve.wait_ge(s_vconst, 2)
            v.tensor_tensor(bound[:], bound[:], wrap[:], ALU.add).then_inc(s_bchain, 1)
            dve.wait_ge(s_boundT_ps, 1)
            v.tensor_copy(boundT[:].rearrange("p k b -> p (k b)"), bank[0][:, 0:TS * B]).then_inc(s_boundT, 1)
            dve.wait_ge(s_boundT, 1)
            dve.wait_ge(s_const, 5)

            def hits(b, s):
                need(dve, s_cnt, b - 1)
                for k in range(TS):
                    op = v.tensor_scalar(hit[s][k][:], iota_row[:], boundT[:, k, bass.ds(b, 1)], None,
                                         ALU.is_equal)
                op.then_inc(s_hit, 1)

            def patches(b, s):
                need(dve, s_end, b + 1)
                v.tensor_tensor_scan(patches_b[:, b, :], ones_full[:], bmask[s][:], 0.0, ALU.mult, ALU.add)\
                    .then_inc(s_patch, 1)

            def body_patch(b, s):
                if not beyond(b + 2, B):
                    hits(b + 2, s)
                patches(b, s)

            hits(0, 0)
            hits(1, 1)
            over_pairs(dve, B, body_patch)
            dve.wait_ge(s_patch, B)

            dve.wait_ge(s_wa, 16 * len(loads_a))
            dve.wait_ge(s_gate, 1)
            v.tensor_scalar(ginit_b[:], ginit_b[:], math.exp(LOGP), None, ALU.mult).then_inc(s_scaled, 1)
            v.tensor_scalar(bin_b[:], bin_b[:], gates[:, 0:1], None, ALU.mult).then_inc(s_scaled, 1)
            v.tensor_scalar(bout_b[:], bout_b[:], gates[:, 2:3], None, ALU.mult)
            v.tensor_scalar(b2_b[:], b2_b[:], gates[:, 3:4], None, ALU.mult).then_inc(s_scaled, 1)
            dve.wait_ge(s_scaled, 3)

            def next_moments(b, s, nbn, nstat, nnext, x_ok):
                need_alone(dve, x_ok, b + 1, s_passed)
                for k in range(TS):
                    op = v.bn_stats(n_st[:, k, :], x_sb[:, bass.ds(TS * b + k, 1), :].rearrange("p o d -> p (o d)"))
                op.then_inc(nbn, 1)
                need(dve, nbn, b + 1)
                need_alone(dve, nnext, 2 * (b - 1), s_passed)
                for k in range(TS):
                    op = v.bn_aggr(n_mv[s][:, k, :], n_st[:, k, :])
                op.then_inc(nstat, 1)

            def moments_a(b, s):
                for k in range(TS):
                    op = v.bn_stats(a_st[s][:, k, :], x_sb[:, bass.ds(TS * b + k, 1), :].rearrange("p o d -> p (o d)"))
                op.then_inc(a_bn, 1)
                need(dve, a_e_ok, b - 1)
                for q in range(TS):
                    op = v.tensor_scalar(a_z[s][:, q, :], patches_b[:, bass.ds(b, 1), :].rearrange("p o t -> p (o t)"),
                                         q1_col[:, q:q + 1], lag_floor[:, q:q + 1], ALU.subtract, ALU.max)
                op.then_inc(a_z_ok, 1)
                need(dve, a_bn, b + 1)
                need_alone(dve, a_scale, b - 1, s_passed)
                for k in range(TS):
                    op = v.bn_aggr(a_mv[s][:, k, :], a_st[s][:, k, :])
                op.then_inc(a_stat, 1)

            def normalise_a(b, s):
                need(dve, a_stat, b + 1)
                need(dve, a_scale, b + 1)
                need(dve, a_xsT_ps, b - 1)
                for k in range(TS):
                    op = v.tensor_scalar(a_xs[s][:, k, :], x_sb[:, bass.ds(TS * b + k, 1), :].rearrange("p o d -> p (o d)"),
                                         a_mv[s][:, k, 0:1], a_scl[s][:, k:k + 1], ALU.subtract, ALU.mult)
                op.then_inc(a_xs_ok, 1)

            def operands_a(b, s):
                need(dve, a_ctx_in[s], 8 * (b - s) + 16)
                need(dve, a_out_ps, b - 1)
                for k in range(TS):
                    op = v.scalar_tensor_tensor(a_u[s][:, k, :], a_ctx[s][:, k, 0:D],
                                                a_scl[s][:, TS + k:TS + k + 1], ginit_b[:], ALU.mult, ALU.mult)
                op.then_inc(a_u_ok, 1)
                need(dve, a_e_ok, b + 1)
                v.scalar_tensor_tensor(a_mT[s][:].rearrange("p q t -> p (q t)"),
                                       a_e[s][:].rearrange("p q t -> p (q t)"), 1.5,
                                       a_e[s][:].rearrange("p q t -> p (q t)"), ALU.is_le, ALU.mult)\
                    .then_inc(a_mT_ok, 1)

            def finish_a(b, s):
                need(dve, a_out_ps, b + 1)
                need(dve, a_xb, b + 1)
                xb = x_sb[:, bass.ds(TS * b, TS), :].rearrange("p k d -> p (k d)")
                v.scalar_tensor_tensor(xb, bank[2 + s][:], gates[:, 0:1], xb, ALU.mult, ALU.add).then_inc(a_x1, 1)
                next_moments(b, s, a_nbn, a_nstat, a_next, a_x1)

            def body_a(b, s):
                if not is_last(b, B):
                    normalise_a(b + 1, 1 - s)
                if not beyond(b + 2, B):
                    moments_a(b + 2, s)
                if not is_first(b):
                    finish_a(b - 1, 1 - s)
                if not is_last(b, B):
                    operands_a(b + 1, 1 - s)
                if isinstance(b, int) and b == 1:
                    dve.wait_ge(s_x_in, 16 * 3)

            def rows(t, count):
                return x_sb[:, bass.ds(t, count), :].rearrange("p k d -> p (k d)")

            def xn_b(n):
                need(dve, b_xT_ps, n - LANES + 1)
                for k in range(GT):
                    t = GT * n + k
                    op = v.tensor_scalar(b_xn[n % LANES][:, k, :], rows(t, 1), mu[:, t:t + 1], rstd[:, t:t + 1],
                                         ALU.subtract, ALU.mult)
                op.then_inc(b_xn_ok, 1)

            dve.wait_ge(s_x0_in, 16)
            moments_a(0, 0)
            moments_a(1, 1)
            normalise_a(0, 0)
            operands_a(0, 0)
            over_pairs(dve, B, body_a)
            dve.wait_ge(a_next, 2 * LANES * GT // TS)
            xn_b(0)
            xn_b(1)
            dve.wait_ge(s_wb, 16 * len(loads_b))
            v.tensor_copy(cw4[:], cw4_col[:].to_broadcast([D // 4, P])).then_inc(s_vconst, 1)
            v.tensor_copy(gw3[:], gw3_col[:].to_broadcast([D // 4, P])).then_inc(s_vconst, 1)
            v.tensor_scalar(cb4[:], cb4[:], 0.5, None, ALU.mult).then_inc(s_vconst, 1)
            v.tensor_scalar(gb3[:], gb3[:], 0.5, None, ALU.mult).then_inc(s_vconst, 1)
            v.tensor_scalar(k_tt[:], arange[:], sgn[:], 0.3, ALU.mult, ALU.mult).then_inc(s_vconst, 1)
            v.tensor_scalar(k_gt[:], arange[:], sgn[:], 0.7, ALU.mult, ALU.mult)
            v.tensor_scalar(k_one[:], sgn[:], 0.1, None, ALU.mult).then_inc(s_vconst, 1)
            dve.wait_ge(s_vconst, 8)
            finish_a(B - 1, 1)
            dve.wait_ge(s_wT, WT_BANKS)
            xn_b(2)
            xn_b(3)

            dve.wait_ge(a_next, 2 * B)

            def cycle_b(slot):
                m = item_at(slot)
                if m is None:
                    return
                g, u, n = m % LANES, m % 2, group_of(m)
                if m % ROUND < LANES:
                    two = slice(2 * g, 2 * g + 2)
                    dve.wait_ge(b_gok, global_slots_before(first_slot(n) + 3) + 1)
                    v.tensor_scalar(b_kb[:, two], b_gt[:, two], k_gt[:], k_one[:], ALU.mult, ALU.add)\
                        .then_inc(b_kbok, 1)
                    dve.wait_ge(b_kbok, n + 1)
                dve.wait_ge(b_ok[3], m + 1)
                for q in range(2):
                    tq = b_tt[u][:, q * S:(q + 1) * S]
                    op = v.tensor_scalar(tq, tq, k_tt[:], b_kb[:, 2 * g + q:2 * g + q + 1], ALU.mult, ALU.add)
                op.then_inc(b_mid, 1)
                dve.wait_ge(b_mid, 2 * m + 1)
                v.tensor_tensor(b_t0[u][:], b_tt[u][:], b_o[g][:, 1, :], ALU.mult)
                v.tensor_tensor(b_t1[u][:], b_tt[u][:], b_o[g][:, 0, :], ALU.mult).then_inc(b_mid, 1)
                dve.wait_ge(b_mid, 2 * m + 2)
                v.tensor_tensor(b_o[g][:, 0, :], b_o[g][:, 0, :], b_t0[u][:], ALU.add)
                v.tensor_tensor(b_o[g][:, 1, :], b_o[g][:, 1, :], b_t1[u][:], ALU.subtract).then_inc(b_upd, 1)

            def x_b(n):
                dve.wait_ge(b_back, n + 1)
                for h in range(2):
                    xh = rows(GT * n + 2 * h, 2)
                    op = v.scalar_tensor_tensor(xh, bank[2 * (n % LANES) + h][:], gates[:, 1:2], xh,
                                                ALU.mult, ALU.add)
                op.then_inc(b_x2, 1)

            def stats_b(n):
                g = n % LANES
                dve.wait_ge(b_x2, n + 1)
                need(dve, b_nstat, n - LANES + 1)
                for k in range(GT):
                    op = v.bn_stats(b_st[g][:, k, :], rows(GT * n + k, 1))
                op.then_inc(b_nbn, 1)
                dve.wait_ge(b_nbn, n + 1)
                need(dve, b_next, 2 * (n - LANES + 1))
                for k in range(GT):
                    op = v.bn_aggr(b_mv[g][:, k, :], b_st[g][:, k, :])
                op.then_inc(b_nstat, 1)

            def slot_b(slot):
                for n in range(NG):
                    if slot == first_slot(n) + ROUND:
                        x_b(n)
                cycle_b(slot - 3)
                for n in range(NG):
                    if slot == first_slot(n) + ROUND:
                        stats_b(n)
                    if n >= LANES and slot == n + 1:
                        xn_b(n)

            def xn_c(b, s):
                need(dve, c_xnT_ps, b - 1)
                for k in range(TS):
                    op = v.tensor_scalar(c_xn[s][:, k, :], x_sb[:, bass.ds(TS * b + k, 1), :].rearrange("p o d -> p (o d)"),
                                         mu[:, bass.ds(TS * b + k, 1)], rstd[:, bass.ds(TS * b + k, 1)],
                                         ALU.subtract, ALU.mult)
                op.then_inc(c_xn_ok, 1)

            dve.wait_ge(s_wc, 16 * len(loads_c))
            for slot in range(3, SLOTS - 2):
                if slot == SLOTS - 4:
                    dve.wait_ge(b_next, 2)
                    xn_c(0, 0)
                    xn_c(1, 1)
                slot_b(slot)


            def neg_c(b, s):
                v.tensor_scalar(c_neg[s][:], mask_b[:, bass.ds(b, 1), :].rearrange("p o t -> p (o t)"), 0.0, MASKED,
                                ALU.is_equal, ALU.mult).then_inc(c_neg_ok, 1)

            def biased(dst, src_bank, col, b, ps, ok, used, use_count):
                need(dve, ps, b + 1)
                need(dve, used, use_count)
                for m in range(DK):
                    op = v.scalar_tensor_tensor(dst[:, m, :], src_bank[:, m * S:(m + 1) * S], col[:, m:m + 1],
                                                mask_b[:, bass.ds(b, 1), :].rearrange("p o t -> p (o t)"),
                                                ALU.add, ALU.mult)
                op.then_inc(ok, 1)

            def v_c(b, s, src=4):
                need(dve, c_v_ps, b + 1)
                need(dve, c_up_ps, 2 * (b - 1))
                v.tensor_tensor(c_v[s][:], bank[src][:].rearrange("p (k d) -> p k d", k=TS),
                                bv_b[:].unsqueeze(1).to_broadcast([P, TS, D]), ALU.add).then_inc(c_vraw, 1)
                need(dve, c_vraw, b + 1)
                for k in range(TS):
                    op = v.tensor_scalar(c_v[s][:, k, :], c_v[s][:, k, :],
                                         mask_col[:, bass.ds(b, 1), k], None, ALU.mult)
                op.then_inc(c_v_ok, 1)

            def maxima_c(b, s, hg):
                n = 2 * b + hg
                need(dve, c_neg_ok, b + 1)
                need(dve, c_p_ok, TS * (n - 1))
                need_alone(dve, c_s_ps, n + 1, s_passed)
                for tc in range(TS):
                    for j in range(QH):
                        op = v.tensor_tensor_reduce(c_s[hg][:, tc, j, :], bank[j][:, tc * S:(tc + 1) * S],
                                                    c_neg[s][:], 1.0, -3.0e38, ALU.add, ALU.max,
                                                    c_mx[hg][:, tc, j:j + 1])
                    op.then_inc(c_mx_ok, 1)
                    need(dve, c_mx_ok, TS * n + tc + 1)
                    v.tensor_scalar(c_nmx[hg][:, tc, :], c_mx[hg][:, tc, :], -SCALE, None, ALU.mult)\
                        .then_inc(c_s_ok, 1)

            def normalise_c(b, hg):
                n = 2 * b + hg
                need(dve, c_p_ok, TS * n + TS)
                v.reciprocal(c_inv[hg][:], c_sum[hg][:]).then_inc(c_inv_ok, 1)
                need(dve, c_inv_ok, n + 1)
                for tc in range(TS):
                    for j in range(QH):
                        pr = c_p[hg][:, tc, j, :]
                        op = v.tensor_scalar(pr, pr, c_inv[hg][:, tc, j:j + 1], None, ALU.mult)
                op.then_inc(c_pn_ok, 1)

            def probsT_c(b, hg):
                n = 2 * b + hg
                for j in range(1, QH, 2):
                    need(dve, c_pT_ps, QH * n + j + 1)
                    need(dve, c_up_ps, n - 1)
                    v.tensor_copy(c_pT[hg][:, j, :], bank[j][:]).then_inc(c_pT_dve, 1)

            def finish_c(b, s):
                need(dve, c_out_ps, b + 1)
                need(dve, c_xb, b + 1)
                xb = x_sb[:, bass.ds(TS * b, TS), :].rearrange("p k d -> p (k d)")
                v.scalar_tensor_tensor(xb, bank[7][:], gates[:, 2:3], xb, ALU.mult, ALU.add).then_inc(c_x3, 1)
                next_moments(b, s, c_nbn, c_nstat, c_next, c_x3)

            def xn_d(n, s):
                need(dve, d_xT_ps, n - 1)
                for k in range(GT):
                    t = bass.ds(GT * n + k, 1)
                    op = v.tensor_scalar(d_xn[s][:, k, :], x_sb[:, t, :].rearrange("p o d -> p (o d)"),
                                         mu[:, t], rstd[:, t], ALU.subtract, ALU.mult)
                op.then_inc(d_xn_ok, 1)

            def lowrank_d(n, s):
                need(dve, d_p_ps, n + 1)
                need(dve, d_h_ps, 4 * (n - 1))
                v.tensor_copy(d_pT[s][:], bank[4][:]).then_inc(d_phi, 1)
                need(dve, d_phi, n + 1)
                low = slice(RANK, 2 * RANK)
                v.tensor_tensor(d_pT[s][low, :], bank[4][low, :], d_pT[s][low, :].bitcast(F32),
                                ALU.subtract).then_inc(d_p_ok, 1)

            def begin_d():
                dve.wait_ge(c_stack_in, 16 * STACK_DMAS * B)
                dve.wait_ge(c_xnT_ps, B)
                dve.wait_ge(c_v_ps, B)
                dve.wait_ge(s_wd, 16 * len(loads_d))
                xn_d(0, 0)
                v.tensor_copy(v1_hi[:], v1_sb[:]).then_inc(s_v1, 1)
                dve.wait_ge(s_v1, 1)
                v.tensor_tensor(v1_lo[:], v1_sb[:], v1_hi[:].bitcast(F32), ALU.subtract).then_inc(s_v1, 1)

            def body_c(b, s):
                last, first = is_last(b, B), is_first(b)
                if not last:
                    biased(c_kT, bank[4], bk_col, b + 1, c_k_ps, c_k_ok, c_k_split, 2 * (b + 1))
                maxima_c(b, s, 0)
                if last:
                    begin_d()
                if not last:
                    biased(c_qT, bank[5], bq_col, b + 1, c_q_ps, c_q_ok, c_qlo_ok, b + 1)
                    neg_c(b + 1, 1 - s)
                if not beyond(b + 2, B):
                    xn_c(b + 2, s)
                if not first:
                    probsT_c(b - 1, 1)
                normalise_c(b, 0)
                maxima_c(b, s, 1)
                if not last:
                    v_c(b + 1, 1 - s)
                probsT_c(b, 0)
                if last:
                    lowrank_d(0, 0)
                if not first:
                    finish_c(b - 1, 1 - s)
                normalise_c(b, 1)

            biased(c_qT, bank[3], bq_col, 0, c_q_ps, c_q_ok, c_qlo_ok, 0)
            slot_b(SLOTS - 2)
            biased(c_kT, bank[0], bk_col, 0, c_k_ps, c_k_ok, c_k_split, 0)
            slot_b(SLOTS - 1)
            v_c(0, 0, 1)
            neg_c(0, 0)
            over_pairs(dve, B, body_c)
            probsT_c(B - 1, 1)
            finish_c(B - 1, 1)

            dve.wait_ge(c_next, 2 * B)

            def second_d(n, s):
                need(dve, d_q_ps, 4 * n + 4)
                need(dve, d_y_ps, 2 * (n - 1))
                v.tensor_copy(d_qT[s][:], bank[6][:]).then_inc(d_q_ok, 1)

            def out_d(n, half):
                need(dve, d_y_ps, 2 * n + half + 1)
                need(dve, d_xb, n + 1)
                xh = x_sb[:, bass.ds(GT * n + 2 * half, 2), :].rearrange("p k d -> p (k d)")
                v.scalar_tensor_tensor(xh, bank[7][:], gates[:, 3:4], xh, ALU.mult, ALU.add).then_inc(d_y_ok, 1)

            def body_d(n, s):
                first, last = is_first(n), is_last(n, NG)
                if not last:
                    xn_d(n + 1, 1 - s)
                if not first:
                    out_d(n - 1, 0)
                if not last:
                    lowrank_d(n + 1, 1 - s)
                if not first:
                    out_d(n - 1, 1)
                second_d(n, s)

            over_pairs(dve, NG, body_d)
            out_d(NG - 1, 0)
            out_d(NG - 1, 1)


INPUTS = ["x", "ctx_2048", "mask_BxS2_if0", "mask_BxS2_fk1", "g_xattn", "g_ffn",
          "L0_xattn_W_in", "L0_xattn_b_in", "L0_xattn_g_res", "L0_xattn_g_init",
          "L0_ffn_cn_w1", "L0_ffn_cn_b1", "L0_ffn_cn_w2", "L0_ffn_cn_b2", "L0_ffn_cn_w3", "L0_ffn_cn_b3",
          "L0_ffn_cn_w4", "L0_ffn_cn_b4", "L0_ffn_gc_w1", "L0_ffn_gc_b1", "L0_ffn_gc_w2", "L0_ffn_gc_b2",
          "L0_ffn_gc_w3", "L0_ffn_gc_b3", "L0_ffn_adaptive_range",
          "L1_xattn_W_src", "L1_xattn_b_src", "L1_xattn_W_tgt", "L1_xattn_b_tgt",
          "L1_xattn_W_out", "L1_xattn_b_out",
          "L1_ffn_U1", "L1_ffn_V1", "L1_ffn_b1", "L1_ffn_U2", "L1_ffn_V2", "L1_ffn_b2"]


def kernel(**inputs):
    import concourse.bacc as bacc
    from concourse.bass_utils import run_bass_kernel_spmd

    nc = bacc.Bacc("TRN2", target_bir_lowering=False, num_devices=1)
    arrays, args = {}, []
    for name in INPUTS:
        a = np.ascontiguousarray(inputs[name])
        arrays[f"in_{name}"] = a
        args.append(nc.dram_tensor(f"in_{name}", a.shape, mybir.dt.from_np(a.dtype), kind="ExternalInput").ap())
    args.append(nc.dram_tensor("out_x", (B, S, D), F32, kind="ExternalOutput").ap())
    build(nc, *args)
    r = run_bass_kernel_spmd(nc, [arrays], core_ids=[0])
    return r.results[0]["out_x"]
```
